# Optimizing a Trainium2 kernel written in Bass

```python
import numpy as np
import jax
import jax.numpy as jnp

def _softmax(x, axis=-1):
    return jax.nn.softmax(x, axis=axis)

def _gelu(x):
    return jax.nn.gelu(x, approximate=True)

def _silu(x):
    return jax.nn.silu(x)

def _sigmoid(x):
    return jax.nn.sigmoid(x)

def _layernorm(x, axis=-1, eps=1e-05):
    m = jnp.mean(x, axis=axis, keepdims=True)
    v = jnp.var(x, axis=axis, keepdims=True)
    return (x - m) / jnp.sqrt(v + eps)

def _scatter_add(tgt, idx, src, axis=0):
    return tgt.at[idx].add(src)

def _segment_sum(src, seg, n):
    return jax.ops.segment_sum(src, seg, n)
kernel_name = 'mk_gnn_preln_d2_gnn_r8_4770c7'

def setup_inputs(seed: int=0):
    np.random.seed(seed)
    _w = jnp.asarray

    def _rec_inputs():
        import jax
        import jax.numpy as jnp
        _gk = jax.random.key(seed)
        x = -0.0005121 + 1.001 * jax.random.normal(jax.random.fold_in(_gk, 1), (12500, 32), jnp.float32)
        src = jax.random.randint(jax.random.fold_in(_gk, 2), (200000,), 0, 12500, jnp.int32)
        dst = jax.random.randint(jax.random.fold_in(_gk, 3), (200000,), 0, 12500, jnp.int32)
        _o = jnp.argsort(dst, stable=True)
        src = src[_o]
        dst = dst[_o]
        edge_attr_32 = -9.77346e-05 + 0.999888 * jax.random.normal(jax.random.fold_in(_gk, 12), (200000, 32), jnp.float32)
        edge_attr_4 = 0.00109026 + 0.999989 * jax.random.normal(jax.random.fold_in(_gk, 13), (200000, 4), jnp.float32)
        edge_attr_8 = jax.random.uniform(jax.random.fold_in(_gk, 14), (200000, 8), jnp.float32, 0.0, 1)
        return (x, src, dst, edge_attr_32, edge_attr_4, edge_attr_8)
    x, src, dst, edge_attr_32, edge_attr_4, edge_attr_8 = _rec_inputs()

    def _L0_gnn_setup():
        import jax, jax.numpy as jnp
        import numpy as np
        EPS_DENOM = 1e-07
        EPS_NORM = 1e-05

        def _fcnn(x, W1, b1, W2, b2):
            return jax.nn.relu(x @ W1 + b1) @ W2 + b2
        key = jax.random.key(seed)
        N, E, D, H = (12500, 200000, 32, 128)
        ks = jax.random.split(key, 11)
        node_features = jax.random.normal(ks[0], (N, D), jnp.float32)
        edge_features = jax.random.normal(ks[1], (E, D), jnp.float32)
        edge_index = jax.random.randint(ks[2], (2, E), 0, N, dtype=jnp.int64)
        sD = 1.0 / np.sqrt(D)
        sH = 1.0 / np.sqrt(H)
        W1a = jax.random.normal(ks[3], (D, H), jnp.float32) * sD
        b1a = jax.random.normal(ks[4], (H,), jnp.float32) * sD
        W2a = jax.random.normal(ks[5], (H, D), jnp.float32) * sH
        b2a = jax.random.normal(ks[6], (D,), jnp.float32) * sH
        W1b = jax.random.normal(ks[7], (D, H), jnp.float32) * sD
        b1b = jax.random.normal(ks[8], (H,), jnp.float32) * sD
        W2b = jax.random.normal(ks[9], (H, D), jnp.float32) * sH
        b2b = jax.random.normal(ks[10], (D,), jnp.float32) * sH
        return dict(node_features=node_features, edge_features=edge_features, W1a=W1a, b1a=b1a, W2a=W2a, b2a=b2a, W1b=W1b, b1b=b1b, W2b=W2b, b2b=b2b, edge_index=edge_index)
    _L0_gnn_all = _L0_gnn_setup()
    _L0_gnn_in = {k: v for k, v in _L0_gnn_all.items() if k in ('W1a', 'b1a', 'W2a', 'b2a', 'W1b', 'b1b', 'W2b', 'b2b')}
    del _L0_gnn_all

    def _L1_gnn_setup():
        import jax, jax.numpy as jnp
        import numpy as np
        MUL = 8
        INV_SQRT3 = float(1.0 / np.sqrt(3.0))
        A_SCALAR = float(np.sqrt(1.0 / 128.0))
        A_VECTOR = float(np.sqrt(3.0 / 128.0))
        SQRT2 = float(np.sqrt(2.0))
        N_NODES, N_EDGES, NUM_BASIS, HIDDEN = (6250, 100000, 8, 256)
        WEIGHT_NUMEL = 4 * MUL * MUL
        k = jax.random.split(jax.random.key(seed), 7)
        node_features = jax.random.normal(k[0], (N_NODES, 4 * MUL), jnp.float32)
        edge_src = jax.random.randint(k[1], (N_EDGES,), 0, N_NODES)
        edge_dst = jax.random.randint(k[2], (N_EDGES,), 0, N_NODES)
        edge_sh = jax.random.normal(k[3], (N_EDGES, 4), jnp.float32)
        edge_scalars = jax.random.uniform(k[4], (N_EDGES, NUM_BASIS), jnp.float32)
        fc_w1 = jax.random.normal(k[5], (NUM_BASIS, HIDDEN), jnp.float32)
        fc_w2 = jax.random.normal(k[6], (HIDDEN, WEIGHT_NUMEL), jnp.float32)
        return dict(node_features=node_features, edge_src=edge_src, edge_dst=edge_dst, edge_sh=edge_sh, edge_scalars=edge_scalars, fc_w1=fc_w1, fc_w2=fc_w2)
    _L1_gnn_all = _L1_gnn_setup()
    _L1_gnn_in = {k: v for k, v in _L1_gnn_all.items() if k in ('fc_w1', 'fc_w2')}
    del _L1_gnn_all
    return {'x': x, 'src': src, 'dst': dst, 'edge_attr_32': edge_attr_32, 'edge_attr_4': edge_attr_4, 'edge_attr_8': edge_attr_8, 'L0_gnn_W1a': _L0_gnn_in['W1a'], 'L0_gnn_b1a': _L0_gnn_in['b1a'], 'L0_gnn_W2a': _L0_gnn_in['W2a'], 'L0_gnn_b2a': _L0_gnn_in['b2a'], 'L0_gnn_W1b': _L0_gnn_in['W1b'], 'L0_gnn_b1b': _L0_gnn_in['b1b'], 'L0_gnn_W2b': _L0_gnn_in['W2b'], 'L0_gnn_b2b': _L0_gnn_in['b2b'], 'L1_gnn_fc_w1': _L1_gnn_in['fc_w1'], 'L1_gnn_fc_w2': _L1_gnn_in['fc_w2']}

def reference(x, src, dst, edge_attr_32, edge_attr_4, edge_attr_8, L0_gnn_W1a, L0_gnn_b1a, L0_gnn_W2a, L0_gnn_b2a, L0_gnn_W1b, L0_gnn_b1b, L0_gnn_W2b, L0_gnn_b2b, L1_gnn_fc_w1, L1_gnn_fc_w2):
    import jax
    import jax.numpy as jnp

    def _L0_gnn_ref(node_features, edge_features, W1a, b1a, W2a, b2a, W1b, b1b, W2b, b2b, edge_index):
        import jax, jax.numpy as jnp
        import numpy as np
        EPS_DENOM = 1e-07
        EPS_NORM = 1e-05

        def _fcnn(x, W1, b1, W2, b2):
            return jax.nn.relu(x @ W1 + b1) @ W2 + b2
        x = node_features
        N = x.shape[0]
        h1 = _fcnn(x, W1a, b1a, W2a, b2a)
        h2 = _fcnn(x, W1b, b1b, W2b, b2b)
        s = jax.nn.sigmoid(edge_features)
        seg = jnp.concatenate([edge_index[0], edge_index[1]])
        nbr = jnp.concatenate([edge_index[1], edge_index[0]])
        s2 = jnp.concatenate([s, s], axis=0)
        denom = EPS_DENOM + jax.ops.segment_sum(s2, seg, num_segments=N)
        msg = s2 / denom[seg] * h2[nbr]
        agg = jax.ops.segment_sum(msg, seg, num_segments=N)
        h = h1 + agg
        mu = jnp.mean(h, axis=-1, keepdims=True)
        var = jnp.var(h, axis=-1, keepdims=True)
        hn = (h - mu) * jax.lax.rsqrt(var + EPS_NORM)
        return x + jax.nn.relu(hn)

    def _L1_gnn_ref(node_features, edge_src, edge_dst, edge_sh, edge_scalars, fc_w1, fc_w2):
        import jax, jax.numpy as jnp
        import numpy as np
        MUL = 8
        INV_SQRT3 = float(1.0 / np.sqrt(3.0))
        A_SCALAR = float(np.sqrt(1.0 / 128.0))
        A_VECTOR = float(np.sqrt(3.0 / 128.0))
        SQRT2 = float(np.sqrt(2.0))
        N_NODES, N_EDGES, NUM_BASIS, HIDDEN = (6250, 100000, 8, 256)
        WEIGHT_NUMEL = 4 * MUL * MUL
        N = node_features.shape[0]
        E = edge_src.shape[0]
        h = jax.nn.relu(edge_scalars @ (fc_w1 * (1.0 / np.sqrt(NUM_BASIS)))) * SQRT2
        w = (h @ (fc_w2 * (1.0 / np.sqrt(HIDDEN)))).reshape(E, 4, MUL, MUL)
        x = node_features[edge_src]
        s1 = x[:, :MUL]
        v1 = x[:, MUL:].reshape(E, MUL, 3)
        s2 = edge_sh[:, 0]
        v2 = edge_sh[:, 1:4]
        out_s = A_SCALAR * (jnp.einsum('eu,euw->ew', s1 * s2[:, None], w[:, 0]) + INV_SQRT3 * jnp.einsum('eui,ei,euw->ew', v1, v2, w[:, 1]))
        out_v = A_VECTOR * INV_SQRT3 * (jnp.einsum('eu,euw,ei->ewi', s1, w[:, 2], v2) + jnp.einsum('eui,euw->ewi', v1 * s2[:, None, None], w[:, 3]))
        edge_features = jnp.concatenate([out_s, out_v.reshape(E, 3 * MUL)], axis=1)
        node_out = jax.ops.segment_sum(edge_features, edge_dst, num_segments=N)
        return node_out * (1.0 / np.sqrt(E / N))
    edge_index = jnp.stack([src, dst])
    h = jnp.maximum(_layernorm(x, axis=-1), 0.0)
    x = x + _L0_gnn_ref(h, edge_attr_32, L0_gnn_W1a, L0_gnn_b1a, L0_gnn_W2a, L0_gnn_b2a, L0_gnn_W1b, L0_gnn_b1b, L0_gnn_W2b, L0_gnn_b2b, edge_index)
    h = jnp.maximum(_layernorm(x, axis=-1), 0.0)
    x = x + _L1_gnn_ref(h, src, dst, edge_attr_4, edge_attr_8, L1_gnn_fc_w1, L1_gnn_fc_w2)
    return x

_drawn_inputs = setup_inputs


def setup_inputs(seed=0):
    import zlib

    import numpy as np

    out = dict(_drawn_inputs(seed))
    spreads = {}
    factors = {'edge_attr_32': 3.721}
    for name, (base, spread) in spreads.items():
        noise = np.random.default_rng([zlib.crc32(name.encode()), seed]).standard_normal(out[name].shape)
        drawn = base * np.exp(spread * noise) if base else spread * noise
        out[name] = jnp.asarray(drawn.astype(out[name].dtype))
    for name, factor in factors.items():
        out[name] = (out[name] * factor).astype(out[name].dtype)
    return out
```

```python
from contextlib import ExitStack

import numpy as np

import concourse.bass as bass
from concourse import mybir

F32 = mybir.dt.float32
BF16 = mybir.dt.bfloat16
I32 = mybir.dt.int32
ALU = mybir.AluOpType
ACT = mybir.ActivationFunctionType
AX = mybir.AxisListType.X

P = 128
T = 4
GROUP = P * T
WINDOW = 64
TABLES = T
SLOTS = 6
SHIFT = 1000.0


def gnn_kernel(nc, x, src, dst, edge32, edge4, edge8, w1a, b1a, w2a, b2a, w1b, b1b, w2b, b2b,
               fc1, fc2, out):
    N, D = x.shape
    E = src.shape[0]
    H = w1a.shape[1]
    NB = edge8.shape[1]
    HID = fc1.shape[1]
    WN = fc2.shape[1]
    U = 8
    VEC = 3
    D2 = 2 * D
    G = -(-E // GROUP)
    SEEN = (G * GROUP - E) // T
    assert G % 2 == 1 and (G * GROUP - E) % T == 0 and SEEN <= P
    NP = 125
    NC = N // NP
    NBLK, BLK = 25, 4
    MBLK, MB = 20, 5
    assert NP * NC == N and NBLK * BLK == NC and MBLK * MB == NC and BLK * D == P and D == 4 * U
    ROWS = N + P
    NPAD = N + WINDOW
    EPS = 1e-5
    EPS_DENOM = 1e-7
    KS = SLOTS * NB
    A_SCALAR = float(np.sqrt(1.0 / 128.0))
    A_VECTOR = float(np.sqrt(3.0 / 128.0))
    INV3 = float(1.0 / np.sqrt(3.0))
    COMMON = float(np.sqrt(2.0) / np.sqrt(HID) / np.sqrt(E / N))
    BLOCK_SCALE = [A_SCALAR * COMMON, A_SCALAR * INV3 * COMMON, A_VECTOR * INV3 * COMMON, A_VECTOR * INV3 * COMMON]
    W_LOADS = 2 * 4 + 2
    ROWQ = [min(P, G - q * P) for q in range(-(-G // P))]

    acc_tab = [nc.dram_tensor(f"acc_tab{j}", (ROWS, D2), F32).ap() for j in range(TABLES)]
    acc1_tab = nc.dram_tensor("acc1_tab", (ROWS, D), F32).ap()
    h2_tab = nc.dram_tensor("h2_tab", (NPAD, D), F32).ap()
    h1_tab = nc.dram_tensor("h1_tab", (N, D), F32).ap()
    est_tab = nc.dram_tensor("est_tab", (G, KS, GROUP), BF16).ap()

    def nodes(a):
        return a[0:N, :].rearrange("(p c) d -> p c d", c=NC)

    def edges(a, g):
        start = E - GROUP if isinstance(g, int) and g == G - 1 else g * GROUP
        if len(a.shape) == 1:
            return a[bass.ds(start, GROUP)].rearrange("(p j) -> p j", j=T)
        return a[bass.ds(start, GROUP), :].rearrange("(p j) d -> p j d", j=T)

    ctx = ExitStack()
    with ctx:
        def sb(name, shape, dt=F32):
            return ctx.enter_context(nc.sbuf_tensor(name, shape, dt))

        def sem(name):
            return ctx.enter_context(nc.semaphore(name))

        ident = sb("ident", [P, P])
        identb = sb("identb", [P, P], BF16)
        later = sb("later", [P, P])
        iota_w = sb("iota_w", [P, WINDOW])
        trash = sb("trash", [P, 1])
        ones = sb("ones", [P, 1])
        w1s = [sb(f"w1s{k}", [D, H]) for k in range(2)]
        b1s = [sb(f"b1s{k}", [P, 1]) for k in range(2)]
        w2s = [sb(f"w2s{k}", [P, D]) for k in range(2)]
        b2s = [sb(f"b2s{k}", [P, D]) for k in range(2)]
        fc1f = sb("fc1f", [NB, HID])
        fc1r = sb("fc1r", [NB, 2, HID])
        fc1p = sb("fc1p", [NB, 3, HID], BF16)
        fc1s = sb("fc1s", [KS, HID], BF16)
        fc2s = sb("fc2s", [P, 2, WN])
        local = sb("local", [P, G, T])
        key_all = [sb(f"key_all{s}", [P, G, T]) for s in range(2)]
        rows_l = sb("rows_l", [P, GROUP])
        base_i = sb("base_i", [1, G], I32)
        bound = sb("bound", [P, 2 * len(ROWQ)])
        outside = sb("outside", [P, 2 * len(ROWQ)])
        outside_sum = sb("outside_sum", [P, 1])
        flag_i = sb("flag_i", [1, 1], I32)
        sum_t = sb("sum_t", [P, NPAD])
        x_sb = sb("x_sb", [P, NC, D])
        h_sb = sb("h_sb", [P, NC, D])
        h1_sb = sb("h1_sb", [P, NC, D])
        work = sb("work", [P, NC, D2])
        flat = work[:, :, :].rearrange("p c d -> p (c d)")
        tmp_a = flat[:, 0:NC * D].rearrange("p (c d) -> p c d", d=D)
        tmp_b = flat[:, NC * D:].rearrange("p (c d) -> p c d", d=D)
        small = [sb(f"small{k}", [P, NC]) for k in range(3)]
        stage = [sb(f"stage{b}", [P, P]) for b in range(2)]
        mst = [sb(f"mst{b}", [D2, MB, NP]) for b in range(2)]
        hid = [[sb(f"hid{b}{c}", [P, GROUP]) for c in range(2)] for b in range(2)]
        hid_n = [[hid[b][k][:, 0:BLK * NP].rearrange("p (c n) -> p c n", c=BLK) for k in range(2)] for b in range(2)]
        tab_in = [sb(f"tab_in{b}", [P, TABLES, MB, D2]) for b in range(2)]
        tab_flat_in = [tab_in[b][:, :, :, :].rearrange("p j c d -> p (j c d)") for b in range(2)]
        rows_i = tab_flat_in[0][:, 0:2 * GROUP].bitcast(I32).rearrange("p (s e) -> p s e", s=2)
        rows_f = tab_flat_in[1][:, 0:2 * GROUP].rearrange("p (s e) -> p s e", s=2)
        node_t = [tab_flat_in[b][0:D, 0:BLK * NP] for b in range(2)]
        gidx = [[sb(f"gidx{b}{s}", [P, T], I32) for s in range(2)] for b in range(2)]
        key = [[sb(f"key{b}{s}", [P, T]) for s in range(2)] for b in range(2)]
        keym = [[sb(f"keym{b}{s}", [P, T]) for s in range(2)] for b in range(2)]
        same = [[sb(f"same{b}{s}", [P, T, P]) for s in range(2)] for b in range(2)]
        count = [[sb(f"count{b}{s}", [P, T]) for s in range(2)] for b in range(2)]
        sidx_f = [[sb(f"sidx_f{b}{s}", [P, T]) for s in range(2)] for b in range(2)]
        sidx = [[sb(f"sidx{b}{s}", [P, T], I32) for s in range(2)] for b in range(2)]
        merged = [[sb(f"merged{b}{s}", [P, T, D2]) for s in range(2)] for b in range(2)]
        onehot = [sb(f"onehot{b}", [P, T, WINDOW]) for b in range(2)]
        got = [[sb(f"got{b}{s}", [P, T, D]) for s in range(2)] for b in range(2)]
        ea32 = [sb(f"ea32{b}", [P, T, D]) for b in range(2)]
        ea8 = [sb(f"ea8{b}", [P, T, NB]) for b in range(2)]
        rest8 = [sb(f"rest8{b}", [P, T, NB]) for b in range(2)]
        parts8 = [sb(f"parts8{b}", [P, T, SLOTS, NB], BF16) for b in range(2)]
        onehot_t = [mst[b][0:WINDOW, :, :].rearrange("w c n -> w (c n)")[:, 0:T * P]
                    .rearrange("w (t e) -> w t e", t=T) for b in range(2)]
        win = [sb(f"win{b}", [WINDOW, D]) for b in range(2)]
        pay = [[sb(f"pay{b}{s}", [P, T, D2]) for s in range(2)] for b in range(2)]
        est = [sb(f"est{b}", [KS, GROUP], BF16) for b in range(2)]
        ea4 = [sb(f"ea4{b}", [P, T, 4]) for b in range(2)]
        v2 = [sb(f"v2{b}", [P, T, VEC]) for b in range(2)]
        zc = [sb(f"zc{b}", [P, T, 6 * U]) for b in range(2)]
        vv = [sb(f"vv{b}", [P, T, U, VEC]) for b in range(2)]
        prod = sb("prod", [P, T, 6, U, U])
        apart = sb("apart", [P, T, WINDOW])
        red = [sb(f"red{b}", [P, T, 6, U]) for b in range(2)]
        outer = [sb(f"outer{b}", [P, T, U, VEC]) for b in range(2)]
        mess = [sb(f"mess{b}", [P, T, D]) for b in range(2)]

        BANK = 512
        pair = [ctx.enter_context(nc.psum_tensor(f"pair{i}", [P, 2 * BANK], F32)) for i in range(4)]
        bank = [pair[i // 2][:, (i % 2) * BANK:(i % 2 + 1) * BANK] for i in range(8)]

        in_loads = sem("in_loads")
        w_loads = sem("w_loads")
        c_pool = sem("c_pool")
        zeroed = sem("zeroed")
        tab_zero = sem("tab_zero")
        fc_parts = sem("fc_parts")
        fc_scaled = sem("fc_scaled")
        rows_ready = sem("rows_ready")
        rows_turned = sem("rows_turned")
        rows_kept = sem("rows_kept")
        base_turned = sem("base_turned")
        base_kept = sem("base_kept")
        outside_ready = sem("outside_ready")
        outside_counted = sem("outside_counted")
        chained = sem("chained")
        passed = {e.engine: sem(f"passed_{k}") for k, e in enumerate([nc.sync, nc.gpsimd, nc.tensor])}
        row_loads = sem("row_loads")
        fc_moved = sem("fc_moved")
        flag_ready = sem("flag_ready")
        variance_ready = sem("variance_ready")
        root_ready = sem("root_ready")
        h_ready = sem("h_ready")
        staged = sem("staged")
        turned = sem("turned")
        turned_kept = sem("turned_kept")
        hid_mm = sem("hid_mm")
        hid_kept = sem("hid_kept")
        out_mm = sem("out_mm")
        out_kept = sem("out_kept")
        h2_stored = sem("h2_stored")
        m_staged = sem("m_staged")
        m_turned = sem("m_turned")
        m_summed = sem("m_summed")
        m_added = sem("m_added")
        m_tabs = [sem(f"m_tabs{b}") for b in range(2)]
        m1_staged = sem("m1_staged")
        m1_turned = sem("m1_turned")
        m1_added = sem("m1_added")
        sum_zeroed = sem("sum_zeroed")
        h1_stored = sem("h1_stored")
        tab1_read = sem("tab1_read")
        stored = sem("stored")
        ea32_in = [sem(f"ea32_in{b}") for b in range(2)]
        ea8_in = [sem(f"ea8_in{b}") for b in range(2)]
        gidx_in = [sem(f"gidx_in{b}") for b in range(2)]
        win_in = [sem(f"win_in{b}") for b in range(2)]
        est_out = [sem(f"est_out{b}") for b in range(2)]
        gathered = [sem(f"gathered{b}") for b in range(2)]
        scattered = [sem(f"scattered{j}") for j in range(TABLES)]
        sig_done = sem("sig_done")
        part1_done = sem("part1_done")
        rest_done = sem("rest_done")
        part2_done = sem("part2_done")
        parts_ready = sem("parts_ready")
        parts_turned = sem("parts_turned")
        est_ready = sem("est_ready")
        key_ready = sem("key_ready")
        key_spread = sem("key_spread")
        same_ready = sem("same_ready")
        sidxf_done = sem("sidxf_done")
        sidx_ready = sem("sidx_ready")
        oh_ready = sem("oh_ready")
        oh_turned = sem("oh_turned")
        oht_ready = sem("oht_ready")
        dst_rows = sem("dst_rows")
        pay0_ready = sem("pay0_ready")
        pay1_ready = sem("pay1_ready")
        merge_done = sem("merge_done")
        merged_ready = sem("merged_ready")
        win_summed = sem("win_summed")
        sum_added = sem("sum_added")
        edges0_pool = sem("edges0_pool")
        edges0_dve = sem("edges0_dve")
        edges0_sp = sem("edges0_sp")
        l1_ea4_in = [sem(f"l1_ea4_in{b}") for b in range(2)]
        l1_est_in = [sem(f"l1_est_in{b}") for b in range(2)]
        l1_gidx_in = [sem(f"l1_gidx_in{b}") for b in range(2)]
        l1_gathered = [sem(f"l1_gathered{b}") for b in range(2)]
        l1_scattered = sem("l1_scattered")
        l1_mlp1 = sem("l1_mlp1")
        l1_relu = sem("l1_relu")
        l1_mlp2 = sem("l1_mlp2")
        l1_sz = sem("l1_sz")
        l1_far = sem("l1_far")
        l1_vv = sem("l1_vv")
        l1_vz = sem("l1_vz")
        l1_prod = sem("l1_prod")
        l1_red = sem("l1_red")
        l1_outer = sem("l1_outer")
        l1_mess = sem("l1_mess")
        l1_oh = sem("l1_oh")
        l1_win = sem("l1_win")
        l1_added = sem("l1_added")
        l1_key = sem("l1_key")
        l1_spread = sem("l1_spread")
        l1_same = sem("l1_same")
        l1_sidxf = sem("l1_sidxf")
        l1_sidx = sem("l1_sidx")
        l1_merge = sem("l1_merge")
        l1_merged = sem("l1_merged")
        edges1_pool = sem("edges1_pool")
        edges1_dve = sem("edges1_dve")

        def wait(eng, s, n):
            if not isinstance(n, int) or n > 0:
                eng.wait_ge(s, n)

        def stand(eng):
            eng.sem_inc(passed[eng.engine], 1)

        def for_all(eng, n, step):
            step(0, 0, 0)
            step(1, 0, 1)
            with eng.Fori(1, n // 2) as i:
                step(i * 2, i, 0)
                step(i * 2 + 1, i, 1)
            step(n - 1, (n - 1) // 2, 0)

        def by_kind(eng, fast, general):
            eng.wait_ge(flag_ready, 1)
            n_outside = eng.value_load(flag_i[0:1, 0:1], min_val=0, max_val=4 * P * len(ROWQ))
            with eng.If(n_outside > 0):
                general()
            with eng.Else():
                fast()

        block = ctx.enter_context(nc.Block())

        @block.sync
        def _(sp):
            sp.dma_start(x_sb[0:NP, :, :], nodes(x)).then_inc(in_loads, 16)
            for k, (w1, b1, w2, b2) in enumerate([(w1a, b1a, w2a, b2a), (w1b, b1b, w2b, b2b)]):
                sp.dma_start(w1s[k][:, :], w1).then_inc(w_loads, 16)
                sp.dma_start(b1s[k][:, :], b1.rearrange("(h a) -> h a", a=1)).then_inc(w_loads, 16)
                sp.dma_start(w2s[k][:, :], w2).then_inc(w_loads, 16)
                sp.dma_start(b2s[k][:, :], b2.rearrange("(a d) -> a d", a=1).to_broadcast([P, D])).then_inc(w_loads, 16)
            sp.dma_start(fc1f[:, :], fc1).then_inc(w_loads, 16)
            sp.dma_start(fc2s[:, :, :], fc2.rearrange("(c k) n -> k c n", c=2)).then_inc(w_loads, 16)
            sp.wait_ge(fc_parts, 1)
            for k, part in enumerate([0, 1, 2, 0, 1, 0]):
                sp.dma_start(fc1s[k * NB:(k + 1) * NB, :], fc1p[:, part, :]).then_inc(fc_moved, 16)
            sp.wait_ge(out_kept, 2 * NBLK)
            sp.dma_start(nodes(h2_tab), tmp_b[0:NP, :, :]).then_inc(h2_stored, 16)
            sp.wait_ge(zeroed, 1)
            sp.dma_start(h2_tab[N:NPAD, :], sum_t[0:WINDOW, 0:D]).then_inc(h2_stored, 16)
            sp.wait_ge(h2_stored, 32)

            def layer0(general):
                ns = 2 if general else 1

                def step(g, n, b):
                    wait(sp, sig_done, g - 1)
                    stand(sp)
                    sp.dma_start(ea32[b][:, :, :], edges(edge32, g)).then_inc(ea32_in[b], 16)
                    wait(sp, gathered[b], n * (16 * T * ns))
                    stand(sp)
                    sp.dma_start(gidx[b][0][:, :], edges(src, g)).then_inc(gidx_in[b], 16)
                    if general:
                        sp.dma_start(gidx[b][1][:, :], edges(dst, g)).then_inc(gidx_in[b], 16)
                    wait(sp, parts_ready, g - 1)
                    stand(sp)
                    sp.dma_start(ea8[b][:, :, :], edges(edge8, g)).then_inc(ea8_in[b], 16)
                    if not general:
                        wait(sp, dst_rows, g - 1)
                        stand(sp)
                        base = sp.value_load(base_i[0:1, bass.ds(g, 1)], min_val=0, max_val=N - 1)
                        sp.dma_start(win[b][:, :], h2_tab[bass.ds(base, WINDOW), :]).then_inc(win_in[b], 16)
                    if not (isinstance(g, int) and g == 0):
                        store(g - 1, 1 - b)

                def store(g, b):
                    wait(sp, est_ready, g + 1)
                    stand(sp)
                    sp.dma_start(est_tab[bass.ds(g, 1), :, :].rearrange("a k e -> (a k) e"), est[b][:, :])\
                      .then_inc(est_out[b], 16)

                for_all(sp, G, step)
                store(G - 1, (G - 1) % 2)
                sp.wait_ge(est_out[0], 16 * (G // 2 + 1))
                sp.wait_ge(est_out[1], 16 * (G // 2))

            by_kind(sp, lambda: layer0(False), lambda: layer0(True))

            sp.wait_ge(edges0_pool, 1)

            def tables(m, b):
                for j in range(TABLES):
                    sp.dma_start(tab_in[b][0:NP, j, :, :], nodes(acc_tab[j])[:, bass.ds(m * MB, MB), :])\
                      .then_inc(m_tabs[b], 16)

            tables(0, 0)
            tables(1, 1)
            with sp.Fori(1, MBLK // 2) as i:
                for b in range(2):
                    sp.wait_ge(m_added, i * 2 + (b - 1))
                    stand(sp)
                    tables(i * 2 + b, b)
            sp.wait_ge(h_ready, 2)
            sp.dma_start(nodes(h1_tab), h_sb[0:NP, :, :]).then_inc(h1_stored, 16)
            sp.wait_ge(h1_stored, 16)

            def layer1(g, n, b):
                wait(sp, l1_gathered[b], n * (16 * T))
                stand(sp)
                sp.dma_start(gidx[b][0][:, :], edges(src, g)).then_inc(l1_gidx_in[b], 16)
                wait(sp, l1_mlp1, (g - 1) * 2)
                stand(sp)
                sp.dma_start(est[b][:, :], est_tab[bass.ds(g, 1), :, :].rearrange("a k e -> (a k) e"))\
                  .then_inc(l1_est_in[b], 16)
                wait(sp, l1_vz, g - 1)
                wait(sp, l1_sz, g - 1)
                stand(sp)
                sp.dma_start(ea4[b][:, :, :], edges(edge4, g)).then_inc(l1_ea4_in[b], 16)

            for_all(sp, G, layer1)
            sp.wait_ge(edges1_pool, 1)
            sp.dma_start(h1_sb[0:NP, :, :], nodes(acc1_tab)).then_inc(tab1_read, 16)
            sp.wait_ge(m1_added, MBLK + 1)
            sp.dma_start(nodes(out), x_sb[0:NP, :, :]).then_inc(stored, 16)
            sp.wait_ge(stored, 16)

        @block.gpsimd
        def _(pool):
            nc.gpsimd.memset(sum_t[:, :], 0.0).then_inc(zeroed, 1)
            nc.gpsimd.memset(ones[:, :], 1.0).then_inc(c_pool, 1)
            nc.gpsimd.memset(ident[:, :], 0.0).then_inc(c_pool, 1)
            nc.gpsimd.memset(later[:, :], 1.0).then_inc(c_pool, 1)
            pool.wait_ge(c_pool, 3)
            nc.gpsimd.affine_select(out=ident[:, :], in_=ident[:, :], compare_op=ALU.not_equal, fill=1.0, base=0,
                                    pattern=[[-1, P]], channel_multiplier=1).then_inc(c_pool, 1)
            nc.gpsimd.affine_select(out=later[:, :], in_=later[:, :], compare_op=ALU.is_ge, fill=0.0, base=0,
                                    pattern=[[1, P]], channel_multiplier=-1).then_inc(c_pool, 1)
            nc.gpsimd.iota(iota_w[:, :], pattern=[[1, WINDOW]], base=0, channel_multiplier=0,
                           allow_small_or_imprecise_dtypes=True).then_inc(c_pool, 1)
            nc.gpsimd.iota(trash[:, :], pattern=[[0, 1]], base=N, channel_multiplier=1,
                           allow_small_or_imprecise_dtypes=True).then_inc(c_pool, 1)
            pool.wait_ge(c_pool, 7)
            nc.gpsimd.tensor_copy(identb[:, :], ident[:, :]).then_inc(c_pool, 1)
            for q, rows in enumerate(ROWQ):
                wait(pool, rows_ready, q)
                for s, a in enumerate([src, dst]):
                    whole = rows if (q + 1) * P < G else rows - 1
                    pool.dma_start(rows_i[0:whole, s, :],
                                   a[q * P * GROUP:(q * P + whole) * GROUP].rearrange("(g e) -> g e", e=GROUP))\
                        .then_inc(row_loads, 16)
                    if whole < rows:
                        pool.dma_start(rows_i[whole:rows, s, :], a[E - GROUP:E].rearrange("(g e) -> g e", g=1))\
                            .then_inc(row_loads, 16)
            pool.wait_ge(zeroed, 1)
            for tab in acc_tab + [acc1_tab]:
                tab_flat = tab.rearrange("n d -> (n d)").rearrange("(p n) -> p n", p=P)
                pool.dma_start(tab_flat, sum_t[:, 0:ROWS * tab.shape[1] // P]).then_inc(tab_zero, 16)
            pool.wait_ge(tab_zero, 16 * (TABLES + 1))
            pool.wait_ge(h2_stored, 32)

            def layer0(general):
                ns = 2 if general else 1

                def gather(g, n, b):
                    pool.wait_ge(gidx_in[b], n * (16 * ns) + 16 * ns)
                    wait(pool, pay1_ready, g - 1)
                    if general:
                        wait(pool, pay0_ready, g - 1)
                    stand(pool)
                    for s in range(ns):
                        for j in range(T):
                            pool.indirect_dma_start(got[b][s][:, j, :], None, h2_tab,
                                                    bass.IndirectOffsetOnAxis(ap=gidx[b][s][:, j:j + 1], axis=0))\
                                .then_inc(gathered[b], 16)

                def step(g, n, b):
                    if not (isinstance(g, int) and g == G - 1):
                        gather(g + 1, n + b, 1 - b)
                    pool.wait_ge(merged_ready, g + 1)
                    pool.wait_ge(sidx_ready, (g + 1) * ns)
                    for s in range(ns):
                        for j in range(T):
                            wait(pool, scattered[j], (g * ns + s) * 16)
                            stand(pool)
                            pool.indirect_dma_start(acc_tab[j],
                                                    bass.IndirectOffsetOnAxis(ap=sidx[b][s][:, j:j + 1], axis=0),
                                                    merged[b][s][:, j, :], None, compute_op=ALU.add)\
                                .then_inc(scattered[j], 16)

                gather(0, 0, 0)
                for_all(pool, G, step)
                for j in range(TABLES):
                    pool.wait_ge(scattered[j], 16 * G * ns)

            by_kind(pool, lambda: layer0(False), lambda: layer0(True))
            nc.gpsimd.memset(count[0][0][0:1, 0:1], 0.0).then_inc(edges0_pool, 1)

            pool.wait_ge(m_staged, MBLK)
            nc.gpsimd.memset(sum_t[0:D, :], 0.0).then_inc(sum_zeroed, 1)
            pool.wait_ge(h1_stored, 16)

            def layer1(general):
                def gather(g, n, b):
                    pool.wait_ge(l1_gidx_in[b], n * 16 + 16)
                    wait(pool, l1_vz, g - 1)
                    wait(pool, l1_sz, g - 1)
                    stand(pool)
                    for j in range(T):
                        pool.indirect_dma_start(got[b][0][:, j, :], None, h1_tab,
                                                bass.IndirectOffsetOnAxis(ap=gidx[b][0][:, j:j + 1], axis=0))\
                            .then_inc(l1_gathered[b], 16)

                def step(g, n, b):
                    if not (isinstance(g, int) and g == G - 1):
                        gather(g + 1, n + b, 1 - b)
                    pool.wait_ge(l1_merged, g + 1)
                    pool.wait_ge(l1_sidx, g + 1)
                    for j in range(T):
                        wait(pool, l1_scattered, (g * T + j) * 16)
                        stand(pool)
                        pool.indirect_dma_start(acc1_tab,
                                                bass.IndirectOffsetOnAxis(ap=sidx[b][1][:, j:j + 1], axis=0),
                                                merged[b][1][:, j, 0:D], None, compute_op=ALU.add)\
                            .then_inc(l1_scattered, 16)

                if general:
                    gather(0, 0, 0)
                    for_all(pool, G, step)
                    pool.wait_ge(l1_scattered, 16 * T * G)
                else:
                    for_all(pool, G, gather)

            by_kind(pool, lambda: layer1(False), lambda: layer1(True))
            nc.gpsimd.memset(count[0][0][0:1, 0:1], 0.0).then_inc(edges1_pool, 1)

        @block.scalar
        def _(act):
            def root(k):
                act.wait_ge(variance_ready, k + 1)
                nc.scalar.activation(small[2][0:NP, :], small[1][0:NP, :], ACT.Sqrt).then_inc(root_ready, 1)

            root(0)

            act.wait_ge(w_loads, 16 * W_LOADS)
            act.wait_ge(h_ready, 1)

            def perceptron(m, n, b):
                wait(act, turned, m - 1)
                nc.scalar.copy(stage[b][0:NP, 0:P],
                               h_sb[0:NP, bass.ds(m * BLK, BLK), :].rearrange("p c d -> p (c d)")).then_inc(staged, 1)
                wait(act, out_mm, (m - 1) * 2)
                for k in range(2):
                    act.wait_ge(hid_mm, m * 2 + (k + 1))
                    nc.scalar.activation(hid_n[b][k][:, :, :],
                                         bank[1 + k][:, 0:BLK * NP].rearrange("p (c n) -> p c n", c=BLK), ACT.Relu,
                                         bias=b1s[k][:, 0:1]).then_inc(hid_kept, 1)

            for_all(act, NBLK, perceptron)

            def layer0(general):
                ns = 2 if general else 1

                def step(g, n, b):
                    act.wait_ge(ea32_in[b], n * 16 + 16)
                    wait(act, merge_done, g - 1)
                    if not general:
                        wait(act, win_summed, g - 1)
                    for s in range(2):
                        gate = nc.scalar.activation(pay[b][s][:, :, 0:D], ea32[b][:, :, :], ACT.Sigmoid)
                    gate.then_inc(sig_done, 1)
                    act.wait_ge(ea8_in[b], n * 16 + 16)
                    wait(act, parts_turned, g - 1)
                    nc.scalar.copy(parts8[b][:, :, 0:3, :],
                                   ea8[b][:, :, :].rearrange("p t (a k) -> p t a k", a=1).to_broadcast([P, T, 3, NB]))\
                      .then_inc(part1_done, 1)
                    act.wait_ge(rest_done, g + 1)
                    nc.scalar.copy(parts8[b][:, :, 3:5, :],
                                   rest8[b][:, :, :].rearrange("p t (a k) -> p t a k", a=1).to_broadcast([P, T, 2, NB]))\
                      .then_inc(part2_done, 1)
                    if not general:
                        act.wait_ge(oh_turned, g + 1)
                        wait(act, dst_rows, g - 1)
                        nc.scalar.copy(onehot_t[b][:, :, :].rearrange("w t e -> w (t e)"), bank[1][0:WINDOW, :])\
                          .then_inc(oht_ready, 1)
                    act.wait_ge(parts_turned, g + 1)
                    wait(act, est_out[b], n * 16)
                    nc.scalar.copy(est[b][:, :], bank[5][0:KS, 0:GROUP // 2].bitcast(BF16)).then_inc(est_ready, 1)
                    act.wait_ge(merge_done, g + 1)
                    for j in range(T):
                        wait(act, scattered[j], (g - 1) * (16 * ns))
                    for s in range(ns):
                        kept = nc.scalar.copy(merged[b][s][:, :, :].rearrange("p t d -> p (t d)"),
                                              bank[3 + s][:, 0:T * D2])
                    kept.then_inc(merged_ready, 1)

                for_all(act, G, step)

            by_kind(act, lambda: layer0(False), lambda: layer0(True))

            act.wait_ge(edges0_dve, 1)
            def merging(m, b, width, s_staged, s_turned):
                wait(act, s_turned, m - 1)
                nc.scalar.copy(mst[b][0:width, :, :],
                               sum_t[0:width, 0:N].rearrange("f (p c) -> f c p", c=NC)[:, bass.ds(m * MB, MB), :])\
                  .then_inc(s_staged, 1)

            def merge_all(width, s_staged, s_turned):
                merging(0, 0, width, s_staged, s_turned)
                merging(1, 1, width, s_staged, s_turned)
                with act.Fori(1, MBLK // 2) as i:
                    merging(i * 2, 0, width, s_staged, s_turned)
                    merging(i * 2 + 1, 1, width, s_staged, s_turned)

            merge_all(D2, m_staged, m_turned)
            root(1)
            root(2)

            def layer1(general):
                def step(g, n, b):
                    for c in range(2):
                        act.wait_ge(l1_mlp1, g * 2 + (c + 1))
                        wait(act, l1_mlp2, g - 1)
                        nc.scalar.activation(hid[b][c][:, :], bank[c][:, :], ACT.Relu).then_inc(l1_relu, 1)
                    act.wait_ge(l1_gathered[b], n * (16 * T) + 16 * T)
                    act.wait_ge(l1_ea4_in[b], n * 16 + 16)
                    wait(act, l1_prod, g - 1)
                    wait(act, l1_outer, g - 1)
                    rows = got[b][0]
                    nc.scalar.copy(v2[b][:, :, :], ea4[b][:, :, 1:4])
                    nc.scalar.copy(zc[b][:, :, 2 * U:3 * U], rows[:, :, 0:U])
                    for j in range(T):
                        s2 = ea4[b][:, j, 0:1]
                        nc.scalar.activation(zc[b][:, j, 0:U], rows[:, j, 0:U], ACT.Copy, scale=s2)
                        last = nc.scalar.activation(zc[b][:, j, 3 * U:6 * U].rearrange("p (i u) -> p i u", i=VEC),
                                                    rows[:, j, U:D].rearrange("p (u i) -> p i u", i=VEC),
                                                    ACT.Copy, scale=s2)
                    last.then_inc(l1_sz, 1)
                    if not general:
                        wait(act, l1_win, g - 1)
                        wait(act, l1_oh, g)
                        for j in range(T):
                            far = nc.scalar.activation(apart[:, j, :], iota_w[:, :], ACT.Square, scale=-1.0,
                                                       bias=local[:, bass.ds(g, 1), j:j + 1].rearrange("p a o -> p (a o)"))
                        far.then_inc(l1_far, 1)
                        act.wait_ge(l1_far, g + 1)
                        nc.scalar.activation(onehot[b][:, :, :], apart[:, :, :], ACT.Relu, scale=-1.0,
                                             bias=ones[:, 0:1]).then_inc(l1_oh, 1)
                    if general:
                        act.wait_ge(l1_merge, g + 1)
                        wait(act, l1_scattered, (g - 1) * (16 * T))
                        nc.scalar.copy(merged[b][1][:, :, 0:D],
                                       bank[6][:, 0:T * D].rearrange("p (t d) -> p t d", t=T)).then_inc(l1_merged, 1)

                for_all(act, G, step)

            by_kind(act, lambda: layer1(False), lambda: layer1(True))
            act.wait_ge(edges1_dve, 1)
            merge_all(D, m1_staged, m1_turned)

        @block.tensor
        def _(pe):
            pe.wait_ge(c_pool, 8)
            for q, rows in enumerate(ROWQ):
                pe.wait_ge(rows_ready, q + 1)
                wait(pe, rows_kept, 3 * q)
                for s, table in enumerate([rows_f[0:rows, 0, :], rows_f[0:rows, 1, :], rows_l[0:rows, :]]):
                    for j in range(T):
                        mm = nc.tensor.transpose(bank[s][:, j * P:j * P + rows], table[:, j:GROUP:T],
                                                 ident[0:rows, 0:rows])
                mm.then_inc(rows_turned, 1)
                nc.tensor.transpose(bank[3][0:1, q * P:q * P + rows], rows_f[0:rows, 1, 0:1],
                                    ident[0:rows, 0:rows]).then_inc(base_turned, 1)
            pe.wait_ge(outside_ready, 1)
            nc.tensor.matmul(bank[4][0:1, 0:1], ones[:, :], outside_sum[:, :], start=True, stop=True)\
              .then_inc(outside_counted, 1)

            pe.wait_ge(w_loads, 16 * W_LOADS)
            pe.wait_ge(flag_ready, 1)

            def perceptron(m, n, b):
                pe.wait_ge(staged, m + 1)
                wait(pe, turned_kept, m)
                stand(pe)
                for c in range(BLK):
                    mm = nc.tensor.transpose(bank[0][0:D, c * NP:(c + 1) * NP], stage[b][0:NP, c * D:(c + 1) * D],
                                             ident[0:NP, 0:NP])
                mm.then_inc(turned, 1)
                pe.wait_ge(turned_kept, m + 1)
                for k in range(2):
                    wait(pe, hid_kept, m * 2 - (1 - k))
                    nc.tensor.matmul(bank[1 + k][:, 0:BLK * NP], w1s[k][:, :], node_t[b][:, :],
                                     start=True, stop=True).then_inc(hid_mm, 1)
                for k in range(2):
                    pe.wait_ge(hid_kept, m * 2 + (k + 1))
                    wait(pe, out_kept, m * 2 - (1 - k))
                    for c in range(BLK):
                        mm = nc.tensor.matmul(bank[3 + k][0:NP, c * D:(c + 1) * D], hid_n[b][k][:, c, :], w2s[k][:, :],
                                              start=True, stop=True)
                    mm.then_inc(out_mm, 1)

            for_all(pe, NBLK, perceptron)

            def spread(keys, to, s_done):
                for j in range(T):
                    mm = nc.tensor.matmul(to[:, j * P:(j + 1) * P], keys[:, j:j + 1].to_broadcast([P, P]), ident[:, :],
                                          start=True, stop=True)
                mm.then_inc(s_done, 1)

            def layer0(general):
                ns = 2 if general else 1

                def step(g, n, b):
                    wait(pe, same_ready, g * (T * ns))
                    for s in range(ns):
                        pe.wait_ge(key_ready, g * ns + (s + 1))
                        spread(key[b][s], bank[s], key_spread)
                    if not general:
                        pe.wait_ge(oh_ready, g + 1)
                        wait(pe, oht_ready, g)
                        stand(pe)
                        for j in range(T):
                            mm = nc.tensor.transpose(bank[1][0:WINDOW, j * P:(j + 1) * P], onehot[b][:, j, :],
                                                     ident[:, :])
                        mm.then_inc(oh_turned, 1)
                    pe.wait_ge(parts_ready, g + 1)
                    wait(pe, est_ready, g)
                    stand(pe)
                    turned_parts = bank[5][0:KS, 0:GROUP // 2].bitcast(BF16)
                    for j in range(T):
                        mm = nc.tensor.transpose(turned_parts[:, j * P:(j + 1) * P],
                                                 parts8[b][:, j, :, :].rearrange("p s k -> p (s k)"), identb[:, :])
                    mm.then_inc(parts_turned, 1)
                    if not general:
                        pe.wait_ge(oht_ready, g + 1)
                        pe.wait_ge(win_in[b], n * 16 + 16)
                        wait(pe, pay0_ready, g)
                        for j in range(T):
                            mm = nc.tensor.matmul(bank[2][:, j * D:(j + 1) * D], onehot_t[b][:, j, :], win[b][:, :],
                                                  start=True, stop=True)
                        mm.then_inc(dst_rows, 1)
                    pe.wait_ge(pay0_ready, g + 1)
                    if general:
                        pe.wait_ge(pay1_ready, g + 1)
                    pe.wait_ge(same_ready, g * (T * ns) + T * ns)
                    wait(pe, merged_ready, g)
                    for s in range(ns):
                        for j in range(T):
                            mm = nc.tensor.matmul(bank[3 + s][:, j * D2:(j + 1) * D2], same[b][s][:, j, :],
                                                  pay[b][s][:, j, :], start=True, stop=True)
                    mm.then_inc(merge_done, 1)
                    if not general:
                        pe.wait_ge(pay1_ready, g + 1)
                        wait(pe, sum_added, g)
                        for j in range(T):
                            mm = nc.tensor.matmul(bank[4][0:D2, 0:WINDOW], pay[b][1][:, j, :], onehot[b][:, j, :],
                                                  start=(j == 0), stop=(j == T - 1))
                        mm.then_inc(win_summed, 1)

                for_all(pe, G, step)

            by_kind(pe, lambda: layer0(False), lambda: layer0(True))

            def merge_all(width, s_staged, s_turned, s_added):
                def merging(m, b):
                    pe.wait_ge(s_staged, m + 1)
                    wait(pe, s_added, m - 1)
                    stand(pe)
                    for c in range(MB):
                        mm = nc.tensor.transpose(bank[6 + b][0:NP, c * width:(c + 1) * width], mst[b][0:width, c, :],
                                                 ident[0:width, 0:width])
                    mm.then_inc(s_turned, 1)

                merging(0, 0)
                merging(1, 1)
                with pe.Fori(1, MBLK // 2) as i:
                    merging(i * 2, 0)
                    merging(i * 2 + 1, 1)

            merge_all(D2, m_staged, m_turned, m_added)

            def layer1(general):
                def mlp1(g, n, b):
                    pe.wait_ge(l1_est_in[b], n * 16 + 16)
                    for c in range(2):
                        wait(pe, l1_relu, (g - 1) * 2 + (c + 1))
                        nc.tensor.matmul(bank[c][:, :], fc1s[:, c * P:(c + 1) * P], est[b][:, :],
                                         start=True, stop=True).then_inc(l1_mlp1, 1)

                def window(g, b):
                    pe.wait_ge(l1_mess, g + 1)
                    pe.wait_ge(l1_oh, g + 1)
                    wait(pe, l1_added, g - 1)
                    for j in range(T):
                        mm = nc.tensor.matmul(bank[6 + b][0:D, 0:WINDOW], mess[b][:, j, :], onehot[b][:, j, :],
                                              start=(j == 0), stop=(j == T - 1))
                    mm.then_inc(l1_win, 1)

                def step(g, n, b):
                    if not (isinstance(g, int) and g == G - 1):
                        mlp1(g + 1, n + b, 1 - b)
                    pe.wait_ge(l1_relu, g * 2 + 2)
                    for h in range(2):
                        wait(pe, l1_prod, g - 1)
                        for t in range(2):
                            for c in range(2):
                                j = 2 * h + t
                                mm = nc.tensor.matmul(pair[1 + b][:, j * WN:(j + 1) * WN],
                                                      hid[b][c][:, j * P:(j + 1) * P], fc2s[:, c, :],
                                                      start=(c == 0), stop=(c == 1))
                    mm.then_inc(l1_mlp2, 1)
                    if general:
                        pe.wait_ge(l1_key, g + 1)
                        wait(pe, l1_same, g * T)
                        spread(key[b][1], bank[7], l1_spread)
                        pe.wait_ge(l1_same, g * T + T)
                        pe.wait_ge(l1_mess, g + 1)
                        wait(pe, l1_merged, g)
                        for j in range(T):
                            mm = nc.tensor.matmul(bank[6][:, j * D:(j + 1) * D], same[b][1][:, j, :], mess[b][:, j, :],
                                                  start=True, stop=True)
                        mm.then_inc(l1_merge, 1)
                    elif not (isinstance(g, int) and g == 0):
                        window(g - 1, 1 - b)

                mlp1(0, 0, 0)
                for_all(pe, G, step)
                if not general:
                    window(G - 1, (G - 1) % 2)

            pe.wait_ge(fc_moved, 16 * SLOTS)
            pe.wait_ge(fc_scaled, 4)
            by_kind(pe, lambda: layer1(False), lambda: layer1(True))
            merge_all(D, m1_staged, m1_turned, m1_added)

        @block.vector
        def _(dve):
            made = [0]

            def chain(ins):
                made[0] += 1
                ins.then_inc(chained, 1)
                dve.wait_ge(chained, made[0])

            dve.wait_ge(w_loads, 16 * W_LOADS)
            chain(nc.vector.tensor_scalar(fc1f[:, :], fc1f[:, :], float(1.0 / np.sqrt(NB)), None, ALU.mult))
            chain(nc.vector.tensor_copy(fc1p[:, 0, :], fc1f[:, :]))
            chain(nc.vector.tensor_tensor(fc1r[:, 0, :], fc1f[:, :], fc1p[:, 0, :], ALU.subtract))
            chain(nc.vector.tensor_copy(fc1p[:, 1, :], fc1r[:, 0, :]))
            chain(nc.vector.tensor_tensor(fc1r[:, 1, :], fc1r[:, 0, :], fc1p[:, 1, :], ALU.subtract))
            nc.vector.tensor_copy(fc1p[:, 2, :], fc1r[:, 1, :]).then_inc(fc_parts, 1)
            for blk, factor in enumerate(BLOCK_SCALE):
                cols = fc2s[:, :, blk * U * U:(blk + 1) * U * U]
                nc.vector.tensor_scalar(cols, cols, factor, None, ALU.mult).then_inc(fc_scaled, 1)

            dve.wait_ge(c_pool, 8)
            chain(nc.vector.memset(outside[:, :], 0.0))
            loads = 0
            for q, rows in enumerate(ROWQ):
                loads += 2 if (q + 1) * P < G else 4
                dve.wait_ge(row_loads, 16 * loads)
                wait(dve, base_turned, q)
                chain(nc.vector.tensor_copy(rows_f[0:rows, :, :], rows_i[0:rows, :, :]))
                chain(nc.vector.tensor_scalar(rows_l[0:rows, :], rows_f[0:rows, 1, :], rows_f[0:rows, 1, 0:1], None,
                                              ALU.subtract))
                nc.vector.tensor_reduce(bound[0:rows, 2 * q:2 * q + 1], rows_l[0:rows, :], AX, ALU.max)
                nc.vector.tensor_reduce(bound[0:rows, 2 * q + 1:2 * q + 2], rows_l[0:rows, :], AX, ALU.min)\
                  .then_inc(rows_ready, 1)
                dve.wait_ge(rows_ready, q + 1)
                nc.vector.tensor_scalar(outside[0:rows, 2 * q:2 * q + 1], bound[0:rows, 2 * q:2 * q + 1],
                                        WINDOW - 0.5, None, ALU.is_gt)
                chain(nc.vector.tensor_scalar(outside[0:rows, 2 * q + 1:2 * q + 2], bound[0:rows, 2 * q + 1:2 * q + 2],
                                              -0.5, None, ALU.is_lt))
                dve.wait_ge(rows_turned, q + 1)
                for s, table in enumerate([key_all[0], key_all[1], local]):
                    nc.vector.tensor_copy(table[:, q * P:q * P + rows, :].rearrange("p g t -> p t g"),
                                          bank[s][:, :].rearrange("p (t g) -> p t g", t=T)[:, :, 0:rows])\
                      .then_inc(rows_kept, 1)
                dve.wait_ge(base_turned, q + 1)
                nc.vector.tensor_copy(base_i[0:1, q * P:q * P + rows], bank[3][0:1, q * P:q * P + rows])\
                  .then_inc(base_kept, 1)
            dve.wait_ge(rows_kept, 3 * len(ROWQ))
            nc.vector.memset(local[0:SEEN, G - 1, :], -SHIFT).then_inc(rows_kept, 1)
            for s in range(2):
                nc.vector.tensor_copy(key_all[s][0:SEEN, G - 1, :], trash[0:SEEN, :].to_broadcast([SEEN, T]))\
                  .then_inc(rows_kept, 1)
            nc.vector.tensor_reduce(outside_sum[:, :], outside[:, :], AX, ALU.add).then_inc(outside_ready, 1)
            dve.wait_ge(outside_counted, 1)
            dve.wait_ge(base_kept, len(ROWQ))
            dve.wait_ge(rows_kept, 3 * len(ROWQ) + 3)
            nc.vector.tensor_copy(flag_i[:, :], bank[4][0:1, 0:1]).then_inc(flag_ready, 1)

            def norm_relu(v, to, k):
                def wide(a):
                    return a[0:NP, :].rearrange("p (c a) -> p c a", a=1).to_broadcast([NP, NC, D])

                chain(nc.vector.tensor_reduce(small[0][0:NP, :], v, AX, ALU.add))
                chain(nc.vector.tensor_scalar(small[1][0:NP, :], small[0][0:NP, :], 1.0 / D, None, ALU.mult))
                chain(nc.vector.tensor_tensor(tmp_a[0:NP], v, wide(small[1]), ALU.subtract))
                chain(nc.vector.tensor_tensor(tmp_b[0:NP], tmp_a[0:NP], tmp_a[0:NP], ALU.mult))
                chain(nc.vector.tensor_reduce(small[0][0:NP, :], tmp_b[0:NP], AX, ALU.add))
                nc.vector.tensor_scalar(small[1][0:NP, :], small[0][0:NP, :], 1.0 / D, EPS, ALU.mult, ALU.add)\
                  .then_inc(variance_ready, 1)
                dve.wait_ge(root_ready, k + 1)
                chain(nc.vector.reciprocal(small[0][0:NP, :], small[2][0:NP, :]))
                return nc.vector.scalar_tensor_tensor(out=to, in0=tmp_a[0:NP], scalar=0.0, in1=wide(small[0]),
                                                      op0=ALU.max, op1=ALU.mult)

            dve.wait_ge(in_loads, 16)
            norm_relu(x_sb[0:NP, :, :], h_sb[0:NP, :, :], 0).then_inc(h_ready, 1)
            dve.wait_ge(h_ready, 1)

            def perceptron(m, n, b):
                dve.wait_ge(turned, m + 1)
                wait(dve, hid_mm, (m - 1) * 2)
                nc.vector.tensor_copy(node_t[b][:, :], bank[0][0:D, 0:BLK * NP]).then_inc(turned_kept, 1)
                for k, to in enumerate([h1_sb, tmp_b]):
                    dve.wait_ge(out_mm, m * 2 + (k + 1))
                    nc.vector.tensor_tensor(to[0:NP, bass.ds(m * BLK, BLK), :],
                                            bank[3 + k][0:NP, 0:P].rearrange("p (c d) -> p c d", d=D),
                                            b2s[k][0:NP, :].rearrange("p (a d) -> p a d", a=1)
                                            .to_broadcast([NP, BLK, D]), ALU.add).then_inc(out_kept, 1)

            for_all(dve, NBLK, perceptron)

            def in_window(b, g, s_done):
                nc.vector.tensor_tensor(onehot[b][:, :, :],
                                        iota_w[:, :].rearrange("p (a w) -> p a w", a=1).to_broadcast([P, T, WINDOW]),
                                        local[:, bass.ds(g, 1), :].rearrange("p a (t o) -> p (a t) o", o=1)
                                        .to_broadcast([P, T, WINDOW]), ALU.is_equal).then_inc(s_done, 1)

            def window_base(g):
                return dve.value_load(base_i[0:1, bass.ds(g, 1)], min_val=0, max_val=N - 1)

            def add_window(base, g, rows, psum, s_done):
                wait(dve, s_done, g)
                span = sum_t[0:rows, bass.ds(base, WINDOW)]
                nc.vector.tensor_tensor(span, span, psum[0:rows, 0:WINDOW], ALU.add).then_inc(s_done, 1)

            def take_keys(b, g, s, s_ready):
                nc.vector.tensor_copy(key[b][s][:, :],
                                      key_all[s][:, bass.ds(g, 1), :].rearrange("p a t -> p (a t)"))
                nc.vector.tensor_scalar(keym[b][s][:, :],
                                        key_all[s][:, bass.ds(g, 1), :].rearrange("p a t -> p (a t)"),
                                        trash[:, 0:1], None, ALU.subtract).then_inc(s_ready, 1)

            def compare(b, s, spread_keys, s_done):
                for j in range(T):
                    nc.vector.scalar_tensor_tensor(out=same[b][s][:, j, :], in0=spread_keys[:, j * P:(j + 1) * P],
                                                   scalar=key[b][s][:, j:j + 1], in1=later[:, :],
                                                   op0=ALU.is_equal, op1=ALU.mult,
                                                   accum_out=count[b][s][:, j:j + 1]).then_inc(s_done, 1)

            def scatter_rows(b, s, n_same, s_same, n_done, s_f, s_done):
                dve.wait_ge(s_same, n_same)
                nc.vector.scalar_tensor_tensor(out=sidx_f[b][s][:, :], in0=count[b][s][:, :], scalar=1.0,
                                               in1=keym[b][s][:, :], op0=ALU.is_equal, op1=ALU.mult).then_inc(s_f, 1)
                dve.wait_ge(s_f, n_done)
                nc.vector.tensor_scalar(sidx[b][s][:, :], sidx_f[b][s][:, :], trash[:, 0:1], None, ALU.add)\
                  .then_inc(s_done, 1)

            def layer0(general):
                ns = 2 if general else 1

                def step(g, n, b):
                    wait(dve, key_spread, (g - 1) * ns)
                    for s in range(ns):
                        take_keys(b, g, s, key_ready)
                    if not general:
                        if not (isinstance(g, int) and g == 0):
                            base = window_base(g - 1)
                            dve.wait_ge(win_summed, g)
                            add_window(base, g - 1, D2, bank[4], sum_added)
                        in_window(b, g, oh_ready)
                    dve.wait_ge(part1_done, g + 1)
                    nc.vector.tensor_tensor(rest8[b][:, :, :], ea8[b][:, :, :], parts8[b][:, :, 0, :], ALU.subtract)\
                      .then_inc(rest_done, 1)
                    dve.wait_ge(part2_done, g + 1)
                    nc.vector.tensor_tensor(parts8[b][:, :, 5, :], rest8[b][:, :, :], parts8[b][:, :, 3, :],
                                            ALU.subtract).then_inc(parts_ready, 1)
                    wait(dve, merge_done, g - 1)
                    for s in range(ns):
                        dve.wait_ge(key_spread, g * ns + (s + 1))
                        compare(b, s, bank[s], same_ready)
                    for j in range(T):
                        wait(dve, scattered[j], (g - 1) * (16 * ns))
                    for s in range(ns):
                        scatter_rows(b, s, g * (T * ns) + T * (s + 1), same_ready, g * ns + (s + 1), sidxf_done,
                                     sidx_ready)
                    dve.wait_ge(sig_done, g + 1)
                    if general:
                        dve.wait_ge(gathered[b], n * (16 * T * ns) + 16 * T * ns)
                        nc.vector.tensor_tensor(pay[b][0][:, :, D:D2], pay[b][0][:, :, 0:D], got[b][1][:, :, :],
                                                ALU.mult).then_inc(pay0_ready, 1)
                    else:
                        dve.wait_ge(dst_rows, g + 1)
                        nc.vector.tensor_tensor(pay[b][0][:, :, D:D2], pay[b][0][:, :, 0:D],
                                                bank[2][:, 0:T * D].rearrange("p (t d) -> p t d", t=T),
                                                ALU.mult).then_inc(pay0_ready, 1)
                        dve.wait_ge(gathered[b], n * (16 * T) + 16 * T)
                    nc.vector.tensor_tensor(pay[b][1][:, :, D:D2], pay[b][1][:, :, 0:D], got[b][0][:, :, :],
                                            ALU.mult).then_inc(pay1_ready, 1)

                for_all(dve, G, step)
                if not general:
                    dve.wait_ge(win_summed, G)
                    add_window(window_base(G - 1), G - 1, D2, bank[4], sum_added)
                    dve.wait_ge(sum_added, G)

            by_kind(dve, lambda: layer0(False), lambda: layer0(True))
            nc.vector.memset(count[0][1][0:1, 0:1], 0.0).then_inc(edges0_dve, 1)

            def merging(m, n, b):
                wide_in = [tab_in[b][0:NP, j, :, :] for j in range(TABLES)]
                to = work[0:NP, bass.ds(m * MB, MB), :]
                dve.wait_ge(m_tabs[b], n * (16 * TABLES) + 16 * TABLES)
                dve.wait_ge(m_turned, m + 1)
                nc.vector.tensor_tensor(to, wide_in[0], bank[6 + b][0:NP, 0:MB * D2].rearrange("p (c d) -> p c d", d=D2),
                                        ALU.add).then_inc(m_summed, 1)
                for j in range(1, TABLES):
                    dve.wait_ge(m_summed, m * (TABLES - 1) + j)
                    done = nc.vector.tensor_tensor(to, to, wide_in[j], ALU.add)
                    done.then_inc(m_summed if j < TABLES - 1 else m_added, 1)

            merging(0, 0, 0)
            merging(1, 0, 1)
            with dve.Fori(1, MBLK // 2) as i:
                merging(i * 2, i, 0)
                merging(i * 2 + 1, i, 1)
            dve.wait_ge(m_added, MBLK)
            gates, sums = work[0:NP, :, 0:D], work[0:NP, :, D:D2]
            chain(nc.vector.tensor_scalar(gates, gates, EPS_DENOM, None, ALU.add))
            chain(nc.vector.reciprocal(gates, gates))
            chain(nc.vector.tensor_tensor(sums, sums, gates, ALU.mult))
            chain(nc.vector.tensor_tensor(h1_sb[0:NP, :, :], h1_sb[0:NP, :, :], sums, ALU.add))
            chain(norm_relu(h1_sb[0:NP, :, :], h1_sb[0:NP, :, :], 1))
            chain(nc.vector.tensor_tensor(h1_sb[0:NP, :, :], h1_sb[0:NP, :, :], h_sb[0:NP, :, :], ALU.add))
            chain(nc.vector.tensor_tensor(x_sb[0:NP, :, :], x_sb[0:NP, :, :], h1_sb[0:NP, :, :], ALU.add))
            norm_relu(x_sb[0:NP, :, :], h_sb[0:NP, :, :], 2).then_inc(h_ready, 1)
            dve.wait_ge(sum_zeroed, 1)

            def layer1(general):
                def factors(g, n, b):
                    rows = got[b][0]
                    dve.wait_ge(l1_gathered[b], n * (16 * T) + 16 * T)
                    dve.wait_ge(l1_ea4_in[b], n * 16 + 16)
                    nc.vector.tensor_tensor(vv[b][:, :, :, :], rows[:, :, U:D].rearrange("p t (u i) -> p t u i", i=VEC),
                                            ea4[b][:, :, 1:4].rearrange("p t (a i) -> p t a i", a=1)
                                            .to_broadcast([P, T, U, VEC]), ALU.mult).then_inc(l1_vv, 1)
                    dve.wait_ge(l1_vv, g + 1)
                    nc.vector.tensor_reduce(zc[b][:, :, U:2 * U], vv[b][:, :, :, :], AX, ALU.add).then_inc(l1_vz, 1)

                def step(g, n, b):
                    if general:
                        wait(dve, l1_spread, g - 1)
                        take_keys(b, g, 1, l1_key)
                    dve.wait_ge(l1_mlp2, g + 1)
                    dve.wait_ge(l1_sz, g + 1)
                    dve.wait_ge(l1_vz, g + 1)
                    weights = pair[1 + b][:, :].rearrange("p (t n) -> p t n", t=T)
                    z = zc[b]
                    nc.vector.tensor_tensor(
                        prod[:, :, 0:3, :, :].rearrange("p t k u w -> p t (k u) w"),
                        weights[:, :, 0:3 * U * U].rearrange("p t (m w) -> p t m w", w=U),
                        z[:, :, 0:3 * U].rearrange("p t (m a) -> p t m a", a=1).to_broadcast([P, T, 3 * U, U]),
                        ALU.mult)
                    for i in range(VEC):
                        last = nc.vector.tensor_tensor(
                            prod[:, :, 3 + i, :, :],
                            weights[:, :, 3 * U * U:4 * U * U].rearrange("p t (u w) -> p t u w", w=U),
                            z[:, :, (3 + i) * U:(4 + i) * U].rearrange("p t (u a) -> p t u a", a=1)
                            .to_broadcast([P, T, U, U]), ALU.mult)
                    last.then_inc(l1_prod, 1)
                    if not general and not (isinstance(g, int) and g < 2):
                        base = window_base(g - 2)
                    if not (isinstance(g, int) and g == G - 1):
                        factors(g + 1, n + b, 1 - b)
                    if not general and not (isinstance(g, int) and g < 2):
                        dve.wait_ge(l1_win, g - 1)
                        add_window(base, g - 2, D, bank[6 + b], l1_added)
                    dve.wait_ge(l1_prod, g + 1)
                    nc.vector.tensor_reduce(red[b][:, :, :, :].rearrange("p t k w -> p (t k) w"),
                                            prod[:, :, :, :, :].rearrange("p t k u w -> p (t k) w u"),
                                            AX, ALU.add).then_inc(l1_red, 1)
                    dve.wait_ge(l1_red, g + 1)
                    r = red[b]
                    nc.vector.tensor_tensor(outer[b][:, :, :, :],
                                            r[:, :, 2, :].rearrange("p t (w a) -> p t w a", a=1)
                                            .to_broadcast([P, T, U, VEC]),
                                            v2[b][:, :, :].rearrange("p t (a i) -> p t a i", a=1)
                                            .to_broadcast([P, T, U, VEC]), ALU.mult).then_inc(l1_outer, 1)
                    wait(dve, l1_merge if general else l1_win, g - 1)
                    nc.vector.tensor_tensor(mess[b][:, :, 0:U], r[:, :, 0, :], r[:, :, 1, :], ALU.add)
                    dve.wait_ge(l1_outer, g + 1)
                    nc.vector.tensor_tensor(mess[b][:, :, U:D].rearrange("p t (w i) -> p t w i", i=VEC),
                                            outer[b][:, :, :, :],
                                            r[:, :, 3:6, :].rearrange("p t i w -> p t w i"),
                                            ALU.add).then_inc(l1_mess, 1)
                    if general:
                        dve.wait_ge(l1_spread, g + 1)
                        compare(b, 1, bank[7], l1_same)
                        wait(dve, l1_scattered, (g - 1) * (16 * T))
                        scatter_rows(b, 1, g * T + T, l1_same, g + 1, l1_sidxf, l1_sidx)

                factors(0, 0, 0)
                for_all(dve, G, step)
                if not general:
                    for g in (G - 2, G - 1):
                        dve.wait_ge(l1_win, g + 1)
                        add_window(window_base(g), g, D, bank[6 + g % 2], l1_added)
                    dve.wait_ge(l1_added, G)

            by_kind(dve, lambda: layer1(False), lambda: layer1(True))
            nc.vector.memset(count[0][1][0:1, 0:1], 0.0).then_inc(edges1_dve, 1)

            def finishing(m, b):
                dve.wait_ge(m1_turned, m + 1)
                to = x_sb[0:NP, bass.ds(m * MB, MB), :]
                nc.vector.tensor_tensor(to, to, bank[6 + b][0:NP, 0:MB * D].rearrange("p (c d) -> p c d", d=D),
                                        ALU.add).then_inc(m1_added, 1)

            finishing(0, 0)
            finishing(1, 1)
            with dve.Fori(1, MBLK // 2) as i:
                finishing(i * 2, 0)
                finishing(i * 2 + 1, 1)
            dve.wait_ge(m1_added, MBLK)
            dve.wait_ge(tab1_read, 16)
            nc.vector.tensor_tensor(x_sb[0:NP, :, :], x_sb[0:NP, :, :], h1_sb[0:NP, :, :], ALU.add)\
              .then_inc(m1_added, 1)


_INS = ['x', 'src', 'dst', 'edge_attr_32', 'edge_attr_4', 'edge_attr_8', 'L0_gnn_W1a', 'L0_gnn_b1a', 'L0_gnn_W2a',
        'L0_gnn_b2a', 'L0_gnn_W1b', 'L0_gnn_b1b', 'L0_gnn_W2b', 'L0_gnn_b2b', 'L1_gnn_fc_w1', 'L1_gnn_fc_w2']


def kernel(**inputs):
    import numpy as _np
    import concourse.bacc as _bacc
    from concourse import mybir as _mybir
    from concourse.bass_utils import run_bass_kernel_spmd as _run

    nc = _bacc.Bacc("TRN2", target_bir_lowering=False, num_devices=1)
    arrays, args = {}, []
    for name in _INS:
        a = _np.ascontiguousarray(inputs[name])
        arrays[f"in_{name}_dram"] = a
        args.append(nc.dram_tensor(f"in_{name}_dram", a.shape, _mybir.dt.from_np(a.dtype), kind="ExternalInput").ap())
    out = nc.dram_tensor("out_0_dram", inputs["x"].shape, _mybir.dt.float32, kind="ExternalOutput").ap()
    gnn_kernel(nc, *args, out)
    r = _run(nc, [arrays], core_ids=[0])
    return r.results[0]["out_0_dram"]
```

```python
from contextlib import ExitStack

import numpy as np

import concourse.bass as bass
from concourse import mybir

F32 = mybir.dt.float32
BF16 = mybir.dt.bfloat16
I32 = mybir.dt.int32
ALU = mybir.AluOpType
ACT = mybir.ActivationFunctionType
AX = mybir.AxisListType.X

P = 128
T = 4
GROUP = P * T
WINDOW = 64
TABLES = T
SLOTS = 6
SHIFT = 1000.0


def gnn_kernel(nc, x, src, dst, edge32, edge4, edge8, w1a, b1a, w2a, b2a, w1b, b1b, w2b, b2b,
               fc1, fc2, out):
    N, D = x.shape
    E = src.shape[0]
    H = w1a.shape[1]
    NB = edge8.shape[1]
    HID = fc1.shape[1]
    WN = fc2.shape[1]
    U = 8
    VEC = 3
    D2 = 2 * D
    G = -(-E // GROUP)
    SEEN = (G * GROUP - E) // T
    assert N + P <= 2 ** 16 and WINDOW <= 2 ** 8
    assert G % 2 == 1 and (G * GROUP - E) % T == 0 and SEEN <= P
    NP = 125
    NC = N // NP
    NBLK, BLK = 25, 4
    MBLK, MB = 20, 5
    assert NP * NC == N and NBLK * BLK == NC and MBLK * MB == NC and BLK * D == P and D == 4 * U
    ROWS = N + P
    NPAD = N + WINDOW
    EPS = 1e-5
    EPS_DENOM = 1e-7
    KS = SLOTS * NB
    A_SCALAR = float(np.sqrt(1.0 / 128.0))
    A_VECTOR = float(np.sqrt(3.0 / 128.0))
    INV3 = float(1.0 / np.sqrt(3.0))
    COMMON = float(np.sqrt(2.0) / np.sqrt(HID) / np.sqrt(E / N))
    BLOCK_SCALE = [A_SCALAR * COMMON, A_SCALAR * INV3 * COMMON, A_VECTOR * INV3 * COMMON, A_VECTOR * INV3 * COMMON]
    W_LOADS = 2 * 4 + 2
    ROWQ = [min(P, G - q * P) for q in range(-(-G // P))]

    acc_tab = [nc.dram_tensor(f"acc_tab{j}", (ROWS, D2), F32).ap() for j in range(TABLES)]
    acc1_tab = nc.dram_tensor("acc1_tab", (ROWS, D), F32).ap()
    h2_tab = nc.dram_tensor("h2_tab", (NPAD, D), F32).ap()
    h1_tab = nc.dram_tensor("h1_tab", (N, D), F32).ap()
    est_tab = nc.dram_tensor("est_tab", (G, KS, GROUP), BF16).ap()

    def nodes(a):
        return a[0:N, :].rearrange("(p c) d -> p c d", c=NC)

    def edges(a, g):
        start = E - GROUP if isinstance(g, int) and g == G - 1 else g * GROUP
        if len(a.shape) == 1:
            return a[bass.ds(start, GROUP)].rearrange("(p j) -> p j", j=T)
        return a[bass.ds(start, GROUP), :].rearrange("(p j) d -> p j d", j=T)

    ctx = ExitStack()
    with ctx:
        def sb(name, shape, dt=F32):
            return ctx.enter_context(nc.sbuf_tensor(name, shape, dt))

        def sem(name):
            return ctx.enter_context(nc.semaphore(name))

        ident = sb("ident", [P, P])
        identb = sb("identb", [P, P], BF16)
        later = sb("later", [P, P])
        iota_w = sb("iota_w", [P, WINDOW])
        trash = sb("trash", [P, 1])
        ones = sb("ones", [P, 1])
        row = sb("row", [P, 1])
        w1s = [sb(f"w1s{k}", [D, H]) for k in range(2)]
        b1s = [sb(f"b1s{k}", [P, 1]) for k in range(2)]
        w2s = [sb(f"w2s{k}", [P, D]) for k in range(2)]
        b2s = [sb(f"b2s{k}", [P, D]) for k in range(2)]
        fc1f = sb("fc1f", [NB, HID])
        fc1r = sb("fc1r", [NB, 2, HID])
        fc1p = sb("fc1p", [NB, 3, HID], BF16)
        fc1s = sb("fc1s", [KS, HID], BF16)
        fc2s = sb("fc2s", [P, 2, WN])
        local = sb("local", [P, G, T])
        key_all = [sb(f"key_all{s}", [P, G, T]) for s in range(2)]
        base_i = sb("base_i", [1, G], I32)
        bound = sb("bound", [P, 2 * len(ROWQ)])
        outside = sb("outside", [P, 2 * len(ROWQ)])
        outside_sum = sb("outside_sum", [P, 1])
        flag_i = sb("flag_i", [1, 1], I32)
        sum_t = sb("sum_t", [P, NPAD])
        all_t = sum_t[D2:D2 + D, 0:N]
        x_sb = sb("x_sb", [P, NC, D])
        h_sb = sb("h_sb", [P, NC, D])
        h1_sb = sb("h1_sb", [P, NC, D])
        work = sb("work", [P, NC, D2])
        flat = work[:, :, :].rearrange("p c d -> p (c d)")
        tmp_a = flat[:, 0:NC * D].rearrange("p (c d) -> p c d", d=D)
        tmp_b = flat[:, NC * D:].rearrange("p (c d) -> p c d", d=D)
        small = [sb(f"small{k}", [P, NC]) for k in range(3)]
        stage = [sb(f"stage{b}", [P, P]) for b in range(2)]
        mst = [sb(f"mst{b}", [D2, MB, NP]) for b in range(2)]
        hid = [[sb(f"hid{b}{c}", [P, GROUP]) for c in range(2)] for b in range(2)]
        hid_n = [hid[b][0][:, 0:BLK * NP].rearrange("p (c n) -> p c n", c=BLK) for b in range(2)]
        tab_in = [sb(f"tab_in{b}", [P, TABLES, MB, D2]) for b in range(2)]
        tab_flat_in = [tab_in[b][:, :, :, :].rearrange("p j c d -> p (j c d)") for b in range(2)]
        rows_i = [tab_flat_in[b][:, 0:2 * GROUP].bitcast(I32).rearrange("p (s e) -> p s e", s=2) for b in range(2)]
        node_t = [tab_flat_in[b][0:D, 0:BLK * NP] for b in range(2)]
        rows_f = hid
        gidx = [[sb(f"gidx{b}{s}", [P, T], I32) for s in range(2)] for b in range(2)]
        same = [[sb(f"same{b}{s}", [P, T, P]) for s in range(2)] for b in range(2)]
        rows_l = [same[b][0][:, :, :].rearrange("p t e -> p (t e)") for b in range(2)]
        key = [[sb(f"key{b}{s}", [P, T]) for s in range(2)] for b in range(2)]
        key_parts = [[sb(f"key_parts{b}{s}", [P, 2, T], BF16) for s in range(2)] for b in range(2)]
        localb = [sb(f"localb{b}", [P, T], BF16) for b in range(2)]
        keym = [[sb(f"keym{b}{s}", [P, T]) for s in range(2)] for b in range(2)]
        count = [[sb(f"count{b}{s}", [P, T]) for s in range(2)] for b in range(2)]
        sidx_f = [[sb(f"sidx_f{b}{s}", [P, T]) for s in range(2)] for b in range(2)]
        sidx = [[sb(f"sidx{b}{s}", [P, T], I32) for s in range(2)] for b in range(2)]
        merged = [[sb(f"merged{b}{s}", [P, T, D2]) for s in range(2)] for b in range(2)]
        onehot = [sb(f"onehot{b}", [P, T, WINDOW]) for b in range(2)]
        got = [[sb(f"got{b}{s}", [P, T, D]) for s in range(2)] for b in range(2)]
        ea32 = [sb(f"ea32{b}", [P, T, D]) for b in range(2)]
        ea8 = [sb(f"ea8{b}", [P, T, NB]) for b in range(2)]
        rest8 = [sb(f"rest8{b}", [P, T, NB]) for b in range(2)]
        parts8 = [sb(f"parts8{b}", [P, T, SLOTS, NB], BF16) for b in range(2)]
        onehot_t = [mst[b][0:WINDOW, :, :].rearrange("w c n -> w (c n)")[:, 0:T * P]
                    .rearrange("w (t e) -> w t e", t=T) for b in range(2)]
        win = [sb(f"win{b}", [WINDOW, D]) for b in range(2)]
        pay = [[sb(f"pay{b}{s}", [P, T, D2]) for s in range(2)] for b in range(2)]
        est = [sb(f"est{b}", [KS, GROUP], BF16) for b in range(2)]
        ea4 = [sb(f"ea4{b}", [P, T, 4]) for b in range(2)]
        v2 = [sb(f"v2{b}", [P, T, VEC]) for b in range(2)]
        zc = [sb(f"zc{b}", [P, T, 6 * U]) for b in range(2)]
        vv = sb("vv", [P, T, U, VEC])
        prod = sb("prod", [P, T, 6, U, U])
        apart = sb("apart", [P, T, WINDOW])
        red = sb("red", [P, T, 4, U])
        outer = sb("outer", [P, T, U, VEC])
        mess = [sb(f"mess{b}", [P, T, D]) for b in range(2)]

        BANK = 512
        pair = [ctx.enter_context(nc.psum_tensor(f"pair{i}", [P, 2 * BANK], F32)) for i in range(4)]
        bank = [pair[i // 2][:, (i % 2) * BANK:(i % 2 + 1) * BANK] for i in range(8)]
        turn_bank, hid_bank, out_bank = [bank[0], bank[7]], [bank[1], bank[2]], [bank[5], bank[6]]
        late_hid_bank, late_out_bank = bank[6], bank[7]
        index_bank = [bank[0:3], bank[5:8]]

        in_loads = sem("in_loads")
        w_loads = sem("w_loads")
        c_pool = sem("c_pool")
        zeroed = sem("zeroed")
        tab_zero = sem("tab_zero")
        fc_parts = sem("fc_parts")
        fc_scaled = sem("fc_scaled")
        rows_conv = sem("rows_conv")
        rows_ready = sem("rows_ready")
        rows_turned = sem("rows_turned")
        rows_kept = sem("rows_kept")
        base_turned = sem("base_turned")
        base_kept = sem("base_kept")
        outside_ready = sem("outside_ready")
        outside_counted = sem("outside_counted")
        chained = sem("chained")
        passed = {e.engine: sem(f"passed_{k}") for k, e in enumerate([nc.sync, nc.gpsimd, nc.tensor])}
        row_loads = [sem(f"row_loads{b}") for b in range(2)]
        fc_moved = sem("fc_moved")
        flag_ready = sem("flag_ready")
        variance_ready = sem("variance_ready")
        root_ready = sem("root_ready")
        h_ready = sem("h_ready")
        staged = sem("staged")
        turned = sem("turned")
        turned_kept = sem("turned_kept")
        hid_mm = sem("hid_mm")
        hid_kept = sem("hid_kept")
        out_mm = sem("out_mm")
        out_kept = sem("out_kept")
        late_taken = sem("late_taken")
        late_hid_mm = sem("late_hid_mm")
        late_hid_kept = sem("late_hid_kept")
        late_out_mm = sem("late_out_mm")
        late_out_kept = sem("late_out_kept")
        h2_stored = sem("h2_stored")
        m_staged = sem("m_staged")
        m_turned = sem("m_turned")
        m_summed = sem("m_summed")
        m_added = sem("m_added")
        m_tabs = [sem(f"m_tabs{b}") for b in range(2)]
        m1_staged = sem("m1_staged")
        m1_turned = sem("m1_turned")
        m1_added = sem("m1_added")
        sum_zeroed = sem("sum_zeroed")
        h1_stored = sem("h1_stored")
        tab1_read = sem("tab1_read")
        stored = sem("stored")
        ea32_in = [sem(f"ea32_in{b}") for b in range(2)]
        ea8_in = [sem(f"ea8_in{b}") for b in range(2)]
        gidx_in = [sem(f"gidx_in{b}") for b in range(2)]
        win_in = [sem(f"win_in{b}") for b in range(2)]
        est_out = [sem(f"est_out{b}") for b in range(2)]
        gathered = [sem(f"gathered{b}") for b in range(2)]
        scattered = [sem(f"scattered{j}") for j in range(TABLES)]
        sig_done = sem("sig_done")
        part1_done = sem("part1_done")
        rest_done = sem("rest_done")
        part2_done = sem("part2_done")
        parts_ready = sem("parts_ready")
        parts_turned = sem("parts_turned")
        est_ready = sem("est_ready")
        key_split = sem("key_split")
        key_ready = sem("key_ready")
        local_ready = sem("local_ready")
        local_spread = sem("local_spread")
        key_spread = sem("key_spread")
        same_ready = sem("same_ready")
        sidxf_done = sem("sidxf_done")
        sidx_ready = sem("sidx_ready")
        oh_ready = sem("oh_ready")
        oht_ready = sem("oht_ready")
        dst_rows = sem("dst_rows")
        pay0_ready = sem("pay0_ready")
        pay1_ready = sem("pay1_ready")
        merge_done = sem("merge_done")
        merged_ready = sem("merged_ready")
        win_summed = sem("win_summed")
        sum_added = sem("sum_added")
        edges0_pool = sem("edges0_pool")
        edges0_dve = sem("edges0_dve")
        edges0_sp = sem("edges0_sp")
        l1_ea4_in = [sem(f"l1_ea4_in{b}") for b in range(2)]
        l1_est_in = [sem(f"l1_est_in{b}") for b in range(2)]
        l1_gidx_in = [sem(f"l1_gidx_in{b}") for b in range(2)]
        l1_gathered = [sem(f"l1_gathered{b}") for b in range(2)]
        l1_scattered = sem("l1_scattered")
        l1_mlp1 = sem("l1_mlp1")
        l1_relu = sem("l1_relu")
        l1_mlp2 = sem("l1_mlp2")
        l1_sz = sem("l1_sz")
        l1_far = sem("l1_far")
        l1_vv = sem("l1_vv")
        l1_vz = sem("l1_vz")
        l1_prod = sem("l1_prod")
        l1_vred = sem("l1_vred")
        l1_red = sem("l1_red")
        l1_outer = sem("l1_outer")
        l1_mess = sem("l1_mess")
        l1_oh = sem("l1_oh")
        l1_win = sem("l1_win")
        l1_added = sem("l1_added")
        l1_key_split = sem("l1_key_split")
        l1_key = sem("l1_key")
        l1_spread = sem("l1_spread")
        l1_same = sem("l1_same")
        l1_sidxf = sem("l1_sidxf")
        l1_sidx = sem("l1_sidx")
        l1_merge = sem("l1_merge")
        l1_merged = sem("l1_merged")
        edges1_pool = sem("edges1_pool")
        edges1_dve = sem("edges1_dve")

        def wait(eng, s, n):
            if not isinstance(n, int) or n > 0:
                eng.wait_ge(s, n)

        def stand(eng):
            eng.sem_inc(passed[eng.engine], 1)

        def for_all(eng, n, step):
            step(0, 0, 0)
            step(1, 0, 1)
            with eng.Fori(1, n // 2) as i:
                step(i * 2, i, 0)
                step(i * 2 + 1, i, 1)
            step(n - 1, (n - 1) // 2, 0)

        def for_all_with(eng, n, step, count, before, amid, after):
            def two(i, base):
                before(i)
                step(base, i, 0)
                amid(i)
                step(base + 1, i, 1)
                after(i)

            two(0, 0)
            with eng.Fori(1, count) as i:
                two(i, i * 2)
            with eng.Fori(count, n // 2) as i:
                step(i * 2, i, 0)
                step(i * 2 + 1, i, 1)
            step(n - 1, (n - 1) // 2, 0)

        def nothing(m):
            pass

        def by_kind(eng, fast, general):
            eng.wait_ge(flag_ready, 1)
            n_outside = eng.value_load(flag_i[0:1, 0:1], min_val=0, max_val=4 * P * len(ROWQ))
            with eng.If(n_outside > 0):
                general()
            with eng.Else():
                fast()

        block = ctx.enter_context(nc.Block())

        @block.sync
        def _(sp):
            sp.dma_start(x_sb[0:NP, :, :], nodes(x)).then_inc(in_loads, 16)

            def index_rows(q):
                rows = ROWQ[q]
                whole = rows if (q + 1) * P < G else rows - 1
                wait(sp, rows_conv, (q - 1) * 2)
                for s, a in enumerate([src, dst]):
                    sp.dma_start(rows_i[q % 2][0:whole, s, :],
                                 a[q * P * GROUP:(q * P + whole) * GROUP].rearrange("(g e) -> g e", e=GROUP))\
                        .then_inc(row_loads[q % 2], 16)
                    if whole < rows:
                        sp.dma_start(rows_i[q % 2][whole:rows, s, :], a[E - GROUP:E].rearrange("(g e) -> g e", g=1))\
                            .then_inc(row_loads[q % 2], 16)

            index_rows(0)
            index_rows(1)
            for k, (w1, b1, w2, b2) in enumerate([(w1a, b1a, w2a, b2a), (w1b, b1b, w2b, b2b)]):
                sp.dma_start(w1s[k][:, :], w1).then_inc(w_loads, 16)
                sp.dma_start(b1s[k][:, :], b1.rearrange("(h a) -> h a", a=1)).then_inc(w_loads, 16)
                sp.dma_start(w2s[k][:, :], w2).then_inc(w_loads, 16)
                sp.dma_start(b2s[k][:, :], b2.rearrange("(a d) -> a d", a=1).to_broadcast([P, D])).then_inc(w_loads, 16)
            sp.dma_start(fc1f[:, :], fc1).then_inc(w_loads, 16)
            sp.dma_start(fc2s[:, :, :], fc2.rearrange("(c k) n -> k c n", c=2)).then_inc(w_loads, 16)
            for q in range(2, len(ROWQ)):
                index_rows(q)
            sp.wait_ge(fc_parts, 1)
            for k, part in enumerate([0, 1, 2, 0, 1, 0]):
                sp.dma_start(fc1s[k * NB:(k + 1) * NB, :], fc1p[:, part, :]).then_inc(fc_moved, 16)
            sp.wait_ge(out_kept, NBLK)
            sp.dma_start(nodes(h2_tab), tmp_b[0:NP, :, :]).then_inc(h2_stored, 16)
            sp.wait_ge(zeroed, 2)
            sp.dma_start(h2_tab[N:NPAD, :], sum_t[0:WINDOW, 0:D]).then_inc(h2_stored, 16)
            sp.wait_ge(h2_stored, 32)

            def layer0(general):
                ns = 2 if general else 1

                def step(g, n, b):
                    wait(sp, sig_done, g - 1)
                    stand(sp)
                    sp.dma_start(ea32[b][:, :, :], edges(edge32, g)).then_inc(ea32_in[b], 16)
                    wait(sp, gathered[b], n * (16 * T * ns))
                    stand(sp)
                    sp.dma_start(gidx[b][0][:, :], edges(src, g)).then_inc(gidx_in[b], 16)
                    if general:
                        sp.dma_start(gidx[b][1][:, :], edges(dst, g)).then_inc(gidx_in[b], 16)
                    wait(sp, parts_ready, g - 1)
                    stand(sp)
                    sp.dma_start(ea8[b][:, :, :], edges(edge8, g)).then_inc(ea8_in[b], 16)
                    if not general:
                        wait(sp, dst_rows, g - 1)
                        stand(sp)
                        base = sp.value_load(base_i[0:1, bass.ds(g, 1)], min_val=0, max_val=N - 1)
                        sp.dma_start(win[b][:, :], h2_tab[bass.ds(base, WINDOW), :]).then_inc(win_in[b], 16)
                    if not (isinstance(g, int) and g == 0):
                        store(g - 1, 1 - b)

                def store(g, b):
                    wait(sp, est_ready, g + 1)
                    stand(sp)
                    sp.dma_start(est_tab[bass.ds(g, 1), :, :].rearrange("a k e -> (a k) e"), est[b][:, :])\
                      .then_inc(est_out[b], 16)

                for_all(sp, G, step)
                store(G - 1, (G - 1) % 2)
                sp.wait_ge(est_out[0], 16 * (G // 2 + 1))
                sp.wait_ge(est_out[1], 16 * (G // 2))

            by_kind(sp, lambda: layer0(False), lambda: layer0(True))

            sp.wait_ge(edges0_pool, 1)

            def tables(m, b):
                for j in range(TABLES):
                    sp.dma_start(tab_in[b][0:NP, j, :, :], nodes(acc_tab[j])[:, bass.ds(m * MB, MB), :])\
                      .then_inc(m_tabs[b], 16)

            tables(0, 0)
            tables(1, 1)
            with sp.Fori(1, MBLK // 2) as i:
                for b in range(2):
                    sp.wait_ge(m_added, i * 2 + (b - 1))
                    stand(sp)
                    tables(i * 2 + b, b)
            sp.wait_ge(h_ready, 2)
            sp.dma_start(nodes(h1_tab), h_sb[0:NP, :, :]).then_inc(h1_stored, 16)
            sp.wait_ge(h1_stored, 16)

            def layer1(g, n, b):
                wait(sp, l1_gathered[b], n * (16 * T))
                stand(sp)
                sp.dma_start(gidx[b][0][:, :], edges(src, g)).then_inc(l1_gidx_in[b], 16)
                wait(sp, l1_mlp1, (g - 1) * 2)
                stand(sp)
                sp.dma_start(est[b][:, :], est_tab[bass.ds(g, 1), :, :].rearrange("a k e -> (a k) e"))\
                  .then_inc(l1_est_in[b], 16)
                wait(sp, l1_vz, g - 1)
                wait(sp, l1_sz, g - 1)
                stand(sp)
                sp.dma_start(ea4[b][:, :, :], edges(edge4, g)).then_inc(l1_ea4_in[b], 16)

            for_all(sp, G, layer1)
            sp.wait_ge(edges1_pool, 1)
            sp.dma_start(h1_sb[0:NP, :, :], nodes(acc1_tab)).then_inc(tab1_read, 16)
            sp.wait_ge(m1_added, MBLK + 1)
            sp.dma_start(nodes(out), x_sb[0:NP, :, :]).then_inc(stored, 16)
            sp.wait_ge(stored, 16)

        @block.gpsimd
        def _(pool):
            nc.gpsimd.memset(h1_sb[:, :, :], 0.0).then_inc(zeroed, 1)
            nc.gpsimd.memset(ones[:, :], 1.0).then_inc(c_pool, 1)
            nc.gpsimd.memset(ident[:, :], 0.0).then_inc(c_pool, 1)
            nc.gpsimd.memset(later[:, :], 1.0).then_inc(c_pool, 1)
            pool.wait_ge(c_pool, 3)
            nc.gpsimd.affine_select(out=ident[:, :], in_=ident[:, :], compare_op=ALU.not_equal, fill=1.0, base=0,
                                    pattern=[[-1, P]], channel_multiplier=1).then_inc(c_pool, 1)
            nc.gpsimd.affine_select(out=later[:, :], in_=later[:, :], compare_op=ALU.is_ge, fill=0.0, base=0,
                                    pattern=[[1, P]], channel_multiplier=-1).then_inc(c_pool, 1)
            nc.gpsimd.iota(iota_w[:, :], pattern=[[1, WINDOW]], base=0, channel_multiplier=0,
                           allow_small_or_imprecise_dtypes=True).then_inc(c_pool, 1)
            nc.gpsimd.iota(trash[:, :], pattern=[[0, 1]], base=N, channel_multiplier=1,
                           allow_small_or_imprecise_dtypes=True).then_inc(c_pool, 1)
            nc.gpsimd.iota(row[:, :], pattern=[[0, 1]], base=0, channel_multiplier=1,
                           allow_small_or_imprecise_dtypes=True).then_inc(c_pool, 1)
            pool.wait_ge(c_pool, 8)
            nc.gpsimd.tensor_copy(identb[:, :], ident[:, :]).then_inc(c_pool, 1)
            pool.wait_ge(zeroed, 1)
            for tab in acc_tab + [acc1_tab]:
                tab_flat = tab.rearrange("n d -> (n d)").rearrange("(p n) -> p n", p=P)
                width = ROWS * tab.shape[1] // P
                for start in range(0, width, NC * D):
                    size = min(NC * D, width - start)
                    pool.dma_start(tab_flat[:, start:start + size],
                                   h1_sb[:, :, :].rearrange("p c d -> p (c d)")[:, 0:size]).then_inc(tab_zero, 16)
            nc.gpsimd.memset(sum_t[0:D2, :], 0.0).then_inc(zeroed, 1)
            pool.wait_ge(tab_zero, 16 * sum(-(-ROWS * tab.shape[1] // P // (NC * D)) for tab in acc_tab + [acc1_tab]))
            pool.wait_ge(h2_stored, 32)

            def layer0(general):
                ns = 2 if general else 1

                def gather(g, n, b):
                    pool.wait_ge(gidx_in[b], n * (16 * ns) + 16 * ns)
                    wait(pool, pay1_ready, g - 1)
                    if general:
                        wait(pool, pay0_ready, g - 1)
                    stand(pool)
                    for s in range(ns):
                        for j in range(T):
                            pool.indirect_dma_start(got[b][s][:, j, :], None, h2_tab,
                                                    bass.IndirectOffsetOnAxis(ap=gidx[b][s][:, j:j + 1], axis=0))\
                                .then_inc(gathered[b], 16)

                def step(g, n, b):
                    if not (isinstance(g, int) and g == G - 1):
                        gather(g + 1, n + b, 1 - b)
                    pool.wait_ge(merged_ready, g + 1)
                    pool.wait_ge(sidx_ready, (g + 1) * ns)
                    for s in range(ns):
                        for j in range(T):
                            wait(pool, scattered[j], (g * ns + s) * 16)
                            stand(pool)
                            pool.indirect_dma_start(acc_tab[j],
                                                    bass.IndirectOffsetOnAxis(ap=sidx[b][s][:, j:j + 1], axis=0),
                                                    merged[b][s][:, j, :], None, compute_op=ALU.add)\
                                .then_inc(scattered[j], 16)

                gather(0, 0, 0)
                for_all(pool, G, step)
                for j in range(TABLES):
                    pool.wait_ge(scattered[j], 16 * G * ns)

            by_kind(pool, lambda: layer0(False), lambda: layer0(True))
            nc.gpsimd.memset(count[0][0][0:1, 0:1], 0.0).then_inc(edges0_pool, 1)

            pool.wait_ge(m_staged, MBLK)
            nc.gpsimd.memset(sum_t[0:D, :], 0.0).then_inc(sum_zeroed, 1)
            pool.wait_ge(h1_stored, 16)

            def layer1(general):
                def gather(g, n, b):
                    pool.wait_ge(l1_gidx_in[b], n * 16 + 16)
                    wait(pool, l1_vz, g - 1)
                    wait(pool, l1_sz, g - 1)
                    stand(pool)
                    for j in range(T):
                        pool.indirect_dma_start(got[b][0][:, j, :], None, h1_tab,
                                                bass.IndirectOffsetOnAxis(ap=gidx[b][0][:, j:j + 1], axis=0))\
                            .then_inc(l1_gathered[b], 16)

                def step(g, n, b):
                    if not (isinstance(g, int) and g == G - 1):
                        gather(g + 1, n + b, 1 - b)
                    pool.wait_ge(l1_merged, g + 1)
                    pool.wait_ge(l1_sidx, g + 1)
                    for j in range(T):
                        wait(pool, l1_scattered, (g * T + j) * 16)
                        stand(pool)
                        pool.indirect_dma_start(acc1_tab,
                                                bass.IndirectOffsetOnAxis(ap=sidx[b][1][:, j:j + 1], axis=0),
                                                merged[b][1][:, j, 0:D], None, compute_op=ALU.add)\
                            .then_inc(l1_scattered, 16)

                if general:
                    gather(0, 0, 0)
                    for_all(pool, G, step)
                    pool.wait_ge(l1_scattered, 16 * T * G)
                else:
                    for_all(pool, G, gather)

            by_kind(pool, lambda: layer1(False), lambda: layer1(True))
            nc.gpsimd.memset(count[0][0][0:1, 0:1], 0.0).then_inc(edges1_pool, 1)

        @block.scalar
        def _(act):
            def root(k):
                act.wait_ge(variance_ready, k + 1)
                nc.scalar.activation(small[2][0:NP, :], small[1][0:NP, :], ACT.Sqrt).then_inc(root_ready, 1)

            def convert_rows(q):
                rows = ROWQ[q]
                act.wait_ge(row_loads[q % 2], 16 * sum(2 if (k + 1) * P < G else 4 for k in range(q % 2, q + 1, 2)))
                wait(act, base_turned, q - 1)
                for s in range(2):
                    nc.scalar.copy(rows_f[q % 2][s][0:rows, :], rows_i[q % 2][0:rows, s, :]).then_inc(rows_conv, 1)

            def keep_rows(q):
                rows = ROWQ[q]
                act.wait_ge(rows_turned, q + 1)
                for s, table in enumerate([key_all[0], key_all[1], local]):
                    nc.scalar.copy(table[:, q * P:q * P + rows, :].rearrange("p g t -> p t g"),
                                   index_bank[q % 2][s][:, :].rearrange("p (t g) -> p t g", t=T)[:, :, 0:rows])\
                      .then_inc(rows_kept, 1)
                act.wait_ge(base_turned, q + 1)
                nc.scalar.copy(base_i[0:1, q * P:q * P + rows], bank[3][0:1, q * P:q * P + rows])\
                  .then_inc(base_kept, 1)

            for q in range(len(ROWQ)):
                convert_rows(q)
                if q > 0:
                    keep_rows(q - 1)
            keep_rows(len(ROWQ) - 1)

            root(0)

            act.wait_ge(w_loads, 16 * W_LOADS)
            act.wait_ge(h_ready, 1)

            def to_stage(m, b):
                wait(act, turned, m - 1)
                nc.scalar.copy(stage[b][0:NP, 0:P],
                               h_sb[0:NP, bass.ds(m * BLK, BLK), :].rearrange("p c d -> p (c d)")).then_inc(staged, 1)

            def perceptron(m, n, b):
                if not (isinstance(m, int) and m == NBLK - 1):
                    to_stage(m + 1, 1 - b)
                wait(act, out_mm, m - 1)
                act.wait_ge(hid_mm, m + 1)
                nc.scalar.activation(hid_n[b][:, :, :],
                                     hid_bank[b][:, 0:BLK * NP].rearrange("p (c n) -> p c n", c=BLK), ACT.Relu,
                                     bias=b1s[1][:, 0:1]).then_inc(hid_kept, 1)

            to_stage(0, 0)
            for_all(act, NBLK, perceptron)

            def layer0(general):
                ns = 2 if general else 1

                def step(g, n, b):
                    act.wait_ge(ea32_in[b], n * 16 + 16)
                    wait(act, merge_done, g - 1)
                    if not general:
                        wait(act, win_summed, g - 1)
                    for s in range(2):
                        gate = nc.scalar.activation(pay[b][s][:, :, 0:D], ea32[b][:, :, :], ACT.Sigmoid)
                    gate.then_inc(sig_done, 1)
                    act.wait_ge(ea8_in[b], n * 16 + 16)
                    wait(act, parts_turned, g - 1)
                    nc.scalar.copy(parts8[b][:, :, 0:3, :],
                                   ea8[b][:, :, :].rearrange("p t (a k) -> p t a k", a=1).to_broadcast([P, T, 3, NB]))\
                      .then_inc(part1_done, 1)
                    act.wait_ge(rest_done, g + 1)
                    nc.scalar.copy(parts8[b][:, :, 3:5, :],
                                   rest8[b][:, :, :].rearrange("p t (a k) -> p t a k", a=1).to_broadcast([P, T, 2, NB]))\
                      .then_inc(part2_done, 1)
                    act.wait_ge(merge_done, g + 1)
                    for j in range(T):
                        wait(act, scattered[j], (g - 1) * (16 * ns))
                    for s in range(ns):
                        kept = nc.scalar.copy(merged[b][s][:, :, :].rearrange("p t d -> p (t d)"),
                                              bank[3 + s][:, 0:T * D2])
                    kept.then_inc(merged_ready, 1)
                    act.wait_ge(parts_turned, g + 1)
                    wait(act, est_out[b], n * 16)
                    nc.scalar.copy(est[b][:, :], bank[5][0:KS, 0:GROUP // 2].bitcast(BF16)).then_inc(est_ready, 1)

                def late_relu(m):
                    act.wait_ge(late_hid_mm, m + 1)
                    wait(act, late_out_mm, m)
                    nc.scalar.activation(hid_n[0][:, :, :],
                                         late_hid_bank[:, 0:BLK * NP].rearrange("p (c n) -> p c n", c=BLK), ACT.Relu,
                                         bias=b1s[0][:, 0:1]).then_inc(late_hid_kept, 1)

                for_all_with(act, G, step, NBLK, nothing, late_relu, nothing)

            by_kind(act, lambda: layer0(False), lambda: layer0(True))

            act.wait_ge(edges0_dve, 1)
            def merging(m, b, width, s_staged, s_turned):
                wait(act, s_turned, m - 1)
                nc.scalar.copy(mst[b][0:width, :, :],
                               sum_t[0:width, 0:N].rearrange("f (p c) -> f c p", c=NC)[:, bass.ds(m * MB, MB), :])\
                  .then_inc(s_staged, 1)

            def merge_all(width, s_staged, s_turned):
                merging(0, 0, width, s_staged, s_turned)
                merging(1, 1, width, s_staged, s_turned)
                with act.Fori(1, MBLK // 2) as i:
                    merging(i * 2, 0, width, s_staged, s_turned)
                    merging(i * 2 + 1, 1, width, s_staged, s_turned)

            merge_all(D2, m_staged, m_turned)
            root(1)
            root(2)

            def layer1(general):
                def step(g, n, b):
                    for c in range(2):
                        act.wait_ge(l1_mlp1, g * 2 + (c + 1))
                        wait(act, l1_mlp2, g - 1)
                        nc.scalar.activation(hid[b][c][:, :], bank[c][:, :], ACT.Relu).then_inc(l1_relu, 1)
                    act.wait_ge(l1_gathered[b], n * (16 * T) + 16 * T)
                    act.wait_ge(l1_ea4_in[b], n * 16 + 16)
                    wait(act, l1_prod, g - 1)
                    wait(act, l1_outer, g - 1)
                    rows = got[b][0]
                    nc.scalar.copy(v2[b][:, :, :], ea4[b][:, :, 1:4])
                    nc.scalar.copy(zc[b][:, :, 2 * U:3 * U], rows[:, :, 0:U])
                    for j in range(T):
                        s2 = ea4[b][:, j, 0:1]
                        nc.scalar.activation(zc[b][:, j, 0:U], rows[:, j, 0:U], ACT.Copy, scale=s2)
                        last = nc.scalar.activation(zc[b][:, j, 3 * U:6 * U].rearrange("p (i u) -> p i u", i=VEC),
                                                    rows[:, j, U:D].rearrange("p (u i) -> p i u", i=VEC),
                                                    ACT.Copy, scale=s2)
                    last.then_inc(l1_sz, 1)
                    if not general:
                        wait(act, l1_win, g - 1)
                        wait(act, l1_oh, g)
                        for j in range(T):
                            far = nc.scalar.activation(apart[:, j, :], iota_w[:, :], ACT.Square, scale=-1.0,
                                                       bias=local[:, bass.ds(g, 1), j:j + 1].rearrange("p a o -> p (a o)"))
                        far.then_inc(l1_far, 1)
                        act.wait_ge(l1_far, g + 1)
                        nc.scalar.activation(onehot[b][:, :, :], apart[:, :, :], ACT.Relu, scale=-1.0,
                                             bias=ones[:, 0:1]).then_inc(l1_oh, 1)
                    if general:
                        act.wait_ge(l1_merge, g + 1)
                        wait(act, l1_scattered, (g - 1) * (16 * T))
                        nc.scalar.copy(merged[b][1][:, :, 0:D],
                                       bank[6][:, 0:T * D].rearrange("p (t d) -> p t d", t=T)).then_inc(l1_merged, 1)

                for_all(act, G, step)

            by_kind(act, lambda: layer1(False), lambda: layer1(True))
            act.wait_ge(edges1_dve, 1)
            merge_all(D, m1_staged, m1_turned)

        @block.tensor
        def _(pe):
            pe.wait_ge(c_pool, 9)
            for q, rows in enumerate(ROWQ):
                pe.wait_ge(rows_ready, q + 1)
                wait(pe, rows_kept, 3 * (q - 1))
                for s, table in enumerate([rows_f[q % 2][0][0:rows, :], rows_f[q % 2][1][0:rows, :],
                                           rows_l[q % 2][0:rows, :]]):
                    for j in range(T):
                        mm = nc.tensor.transpose(index_bank[q % 2][s][:, j * P:j * P + rows], table[:, j:GROUP:T],
                                                 ident[0:rows, 0:rows])
                mm.then_inc(rows_turned, 1)
                wait(pe, base_kept, q)
                nc.tensor.transpose(bank[3][0:1, q * P:q * P + rows], rows_f[q % 2][1][0:rows, 0:1],
                                    ident[0:rows, 0:rows]).then_inc(base_turned, 1)
            pe.wait_ge(outside_ready, 1)
            nc.tensor.matmul(bank[4][0:1, 0:1], ones[:, :], outside_sum[:, :], start=True, stop=True)\
              .then_inc(outside_counted, 1)

            pe.wait_ge(w_loads, 16 * W_LOADS)
            pe.wait_ge(rows_kept, 3 * len(ROWQ))

            def turn(m, b):
                pe.wait_ge(staged, m + 1)
                wait(pe, turned_kept, m - 1)
                stand(pe)
                for c in range(BLK):
                    mm = nc.tensor.transpose(turn_bank[b][0:D, c * NP:(c + 1) * NP], stage[b][0:NP, c * D:(c + 1) * D],
                                             ident[0:NP, 0:NP])
                mm.then_inc(turned, 1)

            def project(m, b):
                pe.wait_ge(hid_kept, m + 1)
                wait(pe, out_kept, m - 1)
                for c in range(BLK):
                    mm = nc.tensor.matmul(out_bank[b][0:NP, c * D:(c + 1) * D], hid_n[b][:, c, :], w2s[1][:, :],
                                          start=True, stop=True)
                mm.then_inc(out_mm, 1)

            def perceptron(m, n, b):
                pe.wait_ge(turned_kept, m + 1)
                wait(pe, hid_kept, m - 1)
                nc.tensor.matmul(hid_bank[b][:, 0:BLK * NP], w1s[1][:, :], node_t[b][:, :],
                                 start=True, stop=True).then_inc(hid_mm, 1)
                if not (isinstance(m, int) and m == NBLK - 1):
                    turn(m + 1, 1 - b)
                if not (isinstance(m, int) and m == 0):
                    project(m - 1, 1 - b)

            turn(0, 0)
            for_all(pe, NBLK, perceptron)
            project(NBLK - 1, (NBLK - 1) % 2)

            def spread(parts, rows, to, s_done):
                for j in range(T):
                    for k, part in enumerate(parts):
                        mm = nc.tensor.matmul(to[0:rows, j * P:(j + 1) * P], part[:, j:j + 1].to_broadcast([P, rows]),
                                              identb[:, :], start=(k == 0), stop=(k == len(parts) - 1))
                mm.then_inc(s_done, 1)

            def spread_keys(b, s, to, s_done):
                spread([key_parts[b][s][:, 0, :], key_parts[b][s][:, 1, :]], P, to, s_done)

            def layer0(general):
                ns = 2 if general else 1

                def spread_local(g, b):
                    pe.wait_ge(local_ready, g + 1)
                    wait(pe, oht_ready, g)
                    spread([localb[b]], WINDOW, bank[1], local_spread)

                def spread_all_keys(g, b):
                    wait(pe, same_ready, g * (T * ns))
                    for s in range(ns):
                        pe.wait_ge(key_ready, g * ns + (s + 1))
                        spread_keys(b, s, bank[s], key_spread)

                def step(g, n, b):
                    last = isinstance(g, int) and g == G - 1
                    if not general:
                        pe.wait_ge(oht_ready, g + 1)
                        pe.wait_ge(win_in[b], n * 16 + 16)
                        wait(pe, pay0_ready, g)
                        for j in range(T):
                            mm = nc.tensor.matmul(bank[2][:, j * D:(j + 1) * D], onehot_t[b][:, j, :], win[b][:, :],
                                                  start=True, stop=True)
                        mm.then_inc(dst_rows, 1)
                        if not last:
                            spread_local(g + 1, 1 - b)
                    pe.wait_ge(pay0_ready, g + 1)
                    if general:
                        pe.wait_ge(pay1_ready, g + 1)
                    pe.wait_ge(same_ready, g * (T * ns) + T * ns)
                    wait(pe, merged_ready, g)
                    for s in range(ns):
                        for j in range(T):
                            mm = nc.tensor.matmul(bank[3 + s][:, j * D2:(j + 1) * D2], same[b][s][:, j, :],
                                                  pay[b][s][:, j, :], start=True, stop=True)
                    mm.then_inc(merge_done, 1)
                    if not general:
                        pe.wait_ge(pay1_ready, g + 1)
                        pe.wait_ge(oh_ready, g + 1)
                        wait(pe, sum_added, g)
                        for j in range(T):
                            mm = nc.tensor.matmul(bank[4][0:D2, 0:WINDOW], pay[b][1][:, j, :], onehot[b][:, j, :],
                                                  start=(j == 0), stop=(j == T - 1))
                        mm.then_inc(win_summed, 1)
                    if not last:
                        spread_all_keys(g + 1, 1 - b)
                    pe.wait_ge(parts_ready, g + 1)
                    wait(pe, est_ready, g)
                    stand(pe)
                    turned_parts = bank[5][0:KS, 0:GROUP // 2].bitcast(BF16)
                    for j in range(T):
                        mm = nc.tensor.transpose(turned_parts[:, j * P:(j + 1) * P],
                                                 parts8[b][:, j, :, :].rearrange("p s k -> p (s k)"), identb[:, :])
                    mm.then_inc(parts_turned, 1)

                def late_hidden(m):
                    pe.wait_ge(late_taken, m + 1)
                    wait(pe, late_hid_kept, m)
                    nc.tensor.matmul(late_hid_bank[:, 0:BLK * NP], w1s[0][:, :], node_t[0][:, :],
                                     start=True, stop=True).then_inc(late_hid_mm, 1)

                def late_project(m):
                    pe.wait_ge(late_hid_kept, m + 1)
                    wait(pe, late_out_kept, m)
                    for c in range(BLK):
                        mm = nc.tensor.matmul(late_out_bank[0:NP, c * D:(c + 1) * D], hid_n[0][:, c, :], w2s[0][:, :],
                                              start=True, stop=True)
                    mm.then_inc(late_out_mm, 1)

                if not general:
                    spread_local(0, 0)
                spread_all_keys(0, 0)
                for_all_with(pe, G, step, NBLK, late_hidden, late_project, nothing)

            by_kind(pe, lambda: layer0(False), lambda: layer0(True))

            def merge_all(width, s_staged, s_turned, s_added):
                def merging(m, b):
                    pe.wait_ge(s_staged, m + 1)
                    wait(pe, s_added, m - 1)
                    stand(pe)
                    for c in range(MB):
                        mm = nc.tensor.transpose(bank[6 + b][0:NP, c * width:(c + 1) * width], mst[b][0:width, c, :],
                                                 ident[0:width, 0:width])
                    mm.then_inc(s_turned, 1)

                merging(0, 0)
                merging(1, 1)
                with pe.Fori(1, MBLK // 2) as i:
                    merging(i * 2, 0)
                    merging(i * 2 + 1, 1)

            merge_all(D2, m_staged, m_turned, m_added)

            def layer1(general):
                def mlp1(g, n, b):
                    pe.wait_ge(l1_est_in[b], n * 16 + 16)
                    for c in range(2):
                        wait(pe, l1_relu, (g - 1) * 2 + (c + 1))
                        nc.tensor.matmul(bank[c][:, :], fc1s[:, c * P:(c + 1) * P], est[b][:, :],
                                         start=True, stop=True).then_inc(l1_mlp1, 1)

                def window(g, b):
                    pe.wait_ge(l1_mess, g + 1)
                    pe.wait_ge(l1_oh, g + 1)
                    wait(pe, l1_added, g - 1)
                    for j in range(T):
                        mm = nc.tensor.matmul(bank[6 + b][0:D, 0:WINDOW], mess[b][:, j, :], onehot[b][:, j, :],
                                              start=(j == 0), stop=(j == T - 1))
                    mm.then_inc(l1_win, 1)

                def step(g, n, b):
                    if not (isinstance(g, int) and g == G - 1):
                        mlp1(g + 1, n + b, 1 - b)
                    pe.wait_ge(l1_relu, g * 2 + 2)
                    for h in range(2):
                        wait(pe, l1_prod, g - 1)
                        for t in range(2):
                            for c in range(2):
                                j = 2 * h + t
                                mm = nc.tensor.matmul(pair[1 + b][:, j * WN:(j + 1) * WN],
                                                      hid[b][c][:, j * P:(j + 1) * P], fc2s[:, c, :],
                                                      start=(c == 0), stop=(c == 1))
                    mm.then_inc(l1_mlp2, 1)
                    if general:
                        pe.wait_ge(l1_key, g + 1)
                        wait(pe, l1_same, g * T)
                        spread_keys(b, 1, bank[7], l1_spread)
                        pe.wait_ge(l1_same, g * T + T)
                        pe.wait_ge(l1_mess, g + 1)
                        wait(pe, l1_merged, g)
                        for j in range(T):
                            mm = nc.tensor.matmul(bank[6][:, j * D:(j + 1) * D], same[b][1][:, j, :], mess[b][:, j, :],
                                                  start=True, stop=True)
                        mm.then_inc(l1_merge, 1)
                    elif not (isinstance(g, int) and g == 0):
                        window(g - 1, 1 - b)

                mlp1(0, 0, 0)
                for_all(pe, G, step)
                if not general:
                    window(G - 1, (G - 1) % 2)

            pe.wait_ge(fc_moved, 16 * SLOTS)
            pe.wait_ge(fc_scaled, 4)
            by_kind(pe, lambda: layer1(False), lambda: layer1(True))
            merge_all(D, m1_staged, m1_turned, m1_added)

        @block.vector
        def _(dve):
            made = [0]

            def chain(ins):
                made[0] += 1
                ins.then_inc(chained, 1)
                dve.wait_ge(chained, made[0])

            def prepare_fc(m):
                dve.wait_ge(w_loads, 16 * W_LOADS)
                chain(nc.vector.tensor_scalar(fc1f[:, :], fc1f[:, :], float(1.0 / np.sqrt(NB)), None, ALU.mult))
                chain(nc.vector.tensor_copy(fc1p[:, 0, :], fc1f[:, :]))
                chain(nc.vector.tensor_tensor(fc1r[:, 0, :], fc1f[:, :], fc1p[:, 0, :], ALU.subtract))
                chain(nc.vector.tensor_copy(fc1p[:, 1, :], fc1r[:, 0, :]))
                chain(nc.vector.tensor_tensor(fc1r[:, 1, :], fc1r[:, 0, :], fc1p[:, 1, :], ALU.subtract))
                nc.vector.tensor_copy(fc1p[:, 2, :], fc1r[:, 1, :]).then_inc(fc_parts, 1)
                for blk, factor in enumerate(BLOCK_SCALE):
                    cols = fc2s[:, :, blk * U * U:(blk + 1) * U * U]
                    nc.vector.tensor_scalar(cols, cols, factor, None, ALU.mult).then_inc(fc_scaled, 1)

            def localise(q):
                rows = ROWQ[q]
                dve.wait_ge(rows_conv, 2 * q + 2)
                wait(dve, rows_turned, q - 1)
                dest = rows_f[q % 2][1]
                nc.vector.tensor_scalar(rows_l[q % 2][0:rows, :], dest[0:rows, :], dest[0:rows, 0:1], None,
                                        ALU.subtract).then_inc(rows_ready, 1)
                dve.wait_ge(rows_ready, q + 1)
                nc.vector.tensor_reduce(bound[0:rows, 2 * q:2 * q + 1], rows_l[q % 2][0:rows, :], AX, ALU.max)
                chain(nc.vector.tensor_reduce(bound[0:rows, 2 * q + 1:2 * q + 2], rows_l[q % 2][0:rows, :], AX,
                                              ALU.min))

            def norm_relu(v, to, k, beside=(nothing,) * 4):
                def wide(a):
                    return a[0:NP, :].rearrange("p (c a) -> p c a", a=1).to_broadcast([NP, NC, D])

                chain(nc.vector.tensor_reduce(small[0][0:NP, :], v, AX, ALU.add))
                chain(nc.vector.tensor_scalar(small[1][0:NP, :], small[0][0:NP, :], 1.0 / D, None, ALU.mult))
                chain(nc.vector.tensor_tensor(tmp_a[0:NP], v, wide(small[1]), ALU.subtract))
                beside[0](0)
                chain(nc.vector.tensor_tensor(tmp_b[0:NP], tmp_a[0:NP], tmp_a[0:NP], ALU.mult))
                beside[1](1)
                chain(nc.vector.tensor_reduce(small[0][0:NP, :], tmp_b[0:NP], AX, ALU.add))
                beside[2](2)
                nc.vector.tensor_scalar(small[1][0:NP, :], small[0][0:NP, :], 1.0 / D, EPS, ALU.mult, ALU.add)\
                  .then_inc(variance_ready, 1)
                beside[3](3)
                dve.wait_ge(root_ready, k + 1)
                chain(nc.vector.reciprocal(small[0][0:NP, :], small[2][0:NP, :]))
                return nc.vector.scalar_tensor_tensor(out=to, in0=tmp_a[0:NP], scalar=0.0, in1=wide(small[0]),
                                                      op0=ALU.max, op1=ALU.mult)

            chain(nc.vector.memset(bound[:, :], 0.0))
            dve.wait_ge(in_loads, 16)

            def two_local(k):
                localise(k)
                if k == 0:
                    prepare_fc(0)
                if k == 2:
                    for q in range(3, len(ROWQ)):
                        localise(q)

            norm_relu(x_sb[0:NP, :, :], h_sb[0:NP, :, :], 0, (two_local, two_local, two_local, nothing))\
                .then_inc(h_ready, 1)
            chain(nc.vector.tensor_scalar(outside[:, 0:2 * len(ROWQ):2], bound[:, 0:2 * len(ROWQ):2],
                                          WINDOW - 0.5, None, ALU.is_gt))
            chain(nc.vector.tensor_scalar(outside[:, 1:2 * len(ROWQ):2], bound[:, 1:2 * len(ROWQ):2],
                                          -0.5, None, ALU.is_lt))
            dve.wait_ge(rows_kept, 3 * len(ROWQ))
            nc.vector.memset(local[0:SEEN, G - 1, :], -SHIFT).then_inc(rows_kept, 1)
            for s in range(2):
                nc.vector.tensor_copy(key_all[s][0:SEEN, G - 1, :], trash[0:SEEN, :].to_broadcast([SEEN, T]))\
                  .then_inc(rows_kept, 1)
            nc.vector.tensor_reduce(outside_sum[:, :], outside[:, :], AX, ALU.add).then_inc(outside_ready, 1)
            def keep_turned(m, b):
                dve.wait_ge(turned, m + 1)
                wait(dve, hid_mm, m - 1)
                nc.vector.tensor_copy(all_t[:, bass.ds(m * (BLK * NP), BLK * NP)], turn_bank[b][0:D, 0:BLK * NP])
                nc.vector.tensor_copy(node_t[b][:, :], turn_bank[b][0:D, 0:BLK * NP]).then_inc(turned_kept, 1)

            def keep_block(m, k, psum, to, s_done):
                nc.vector.tensor_tensor(to[0:NP, bass.ds(m * BLK, BLK), :],
                                        psum[0:NP, 0:P].rearrange("p (c d) -> p c d", d=D),
                                        b2s[k][0:NP, :].rearrange("p (a d) -> p a d", a=1)
                                        .to_broadcast([NP, BLK, D]), ALU.add).then_inc(s_done, 1)

            def keep_projected(m, b):
                dve.wait_ge(out_mm, m + 1)
                keep_block(m, 1, out_bank[b], tmp_b, out_kept)

            def perceptron(m, n, b):
                if not (isinstance(m, int) and m == NBLK - 1):
                    keep_turned(m + 1, 1 - b)
                if not (isinstance(m, int) and m == 0):
                    keep_projected(m - 1, 1 - b)

            keep_turned(0, 0)
            for_all(dve, NBLK, perceptron)
            keep_projected(NBLK - 1, (NBLK - 1) % 2)
            dve.wait_ge(outside_counted, 1)
            dve.wait_ge(base_kept, len(ROWQ))
            dve.wait_ge(rows_kept, 3 * len(ROWQ) + 3)
            nc.vector.tensor_copy(flag_i[:, :], bank[4][0:1, 0:1]).then_inc(flag_ready, 1)

            def in_window(b, g, s_done):
                nc.vector.tensor_tensor(onehot[b][:, :, :],
                                        iota_w[:, :].rearrange("p (a w) -> p a w", a=1).to_broadcast([P, T, WINDOW]),
                                        local[:, bass.ds(g, 1), :].rearrange("p a (t o) -> p (a t) o", o=1)
                                        .to_broadcast([P, T, WINDOW]), ALU.is_equal).then_inc(s_done, 1)

            def window_base(g):
                return dve.value_load(base_i[0:1, bass.ds(g, 1)], min_val=0, max_val=N - 1)

            def add_window(base, g, rows, psum, s_done):
                wait(dve, s_done, g)
                span = sum_t[0:rows, bass.ds(base, WINDOW)]
                nc.vector.tensor_tensor(span, span, psum[0:rows, 0:WINDOW], ALU.add).then_inc(s_done, 1)

            def take_keys(b, g, s, n_split, s_split, s_ready):
                keys = key_all[s][:, bass.ds(g, 1), :].rearrange("p a t -> p (a t)")
                nc.vector.tensor_copy(key_parts[b][s][:, 0, :], keys).then_inc(s_split, 1)
                nc.vector.tensor_copy(key[b][s][:, :], keys)
                nc.vector.tensor_scalar(keym[b][s][:, :], keys, trash[:, 0:1], None, ALU.subtract)
                dve.wait_ge(s_split, n_split)
                nc.vector.tensor_tensor(key_parts[b][s][:, 1, :], keys, key_parts[b][s][:, 0, :], ALU.subtract)\
                  .then_inc(s_ready, 1)

            def compare(b, s, spread_keys, s_done):
                for j in range(T):
                    nc.vector.scalar_tensor_tensor(out=same[b][s][:, j, :], in0=spread_keys[:, j * P:(j + 1) * P],
                                                   scalar=key[b][s][:, j:j + 1], in1=later[:, :],
                                                   op0=ALU.is_equal, op1=ALU.mult,
                                                   accum_out=count[b][s][:, j:j + 1]).then_inc(s_done, 1)

            def scatter_rows(b, s, n_same, s_same, n_done, s_f, s_done):
                dve.wait_ge(s_same, n_same)
                nc.vector.scalar_tensor_tensor(out=sidx_f[b][s][:, :], in0=count[b][s][:, :], scalar=1.0,
                                               in1=keym[b][s][:, :], op0=ALU.is_equal, op1=ALU.mult).then_inc(s_f, 1)
                dve.wait_ge(s_f, n_done)
                nc.vector.tensor_scalar(sidx[b][s][:, :], sidx_f[b][s][:, :], trash[:, 0:1], None, ALU.add)\
                  .then_inc(s_done, 1)

            def layer0(general):
                ns = 2 if general else 1

                def take_group(g, b):
                    if not general:
                        wait(dve, local_spread, g - 1)
                        nc.vector.tensor_copy(localb[b][:, :],
                                              local[:, bass.ds(g, 1), :].rearrange("p a t -> p (a t)"))\
                          .then_inc(local_ready, 1)
                    wait(dve, key_spread, (g - 1) * ns)
                    for s in range(ns):
                        take_keys(b, g, s, g * ns + (s + 1), key_split, key_ready)

                def one_hots(g, b):
                    if not (isinstance(g, int) and g < 2):
                        dve.wait_ge(win_summed, g - 1)
                    in_window(b, g, oh_ready)
                    dve.wait_ge(local_spread, g + 1)
                    wait(dve, dst_rows, g - 1)
                    nc.vector.tensor_scalar(onehot_t[b][:, :, :].rearrange("w t e -> w (t e)"), bank[1][0:WINDOW, :],
                                            row[0:WINDOW, 0:1], None, ALU.is_equal).then_inc(oht_ready, 1)

                def step(g, n, b):
                    first, last = (isinstance(g, int) and g == k for k in (0, G - 1))
                    base = None if general or first else window_base(g - 1)
                    dve.wait_ge(part1_done, g + 1)
                    nc.vector.tensor_tensor(rest8[b][:, :, :], ea8[b][:, :, :], parts8[b][:, :, 0, :], ALU.subtract)\
                      .then_inc(rest_done, 1)
                    wait(dve, merge_done, g - 1)
                    for s in range(ns):
                        dve.wait_ge(key_spread, g * ns + (s + 1))
                        compare(b, s, bank[s], same_ready)
                    dve.wait_ge(part2_done, g + 1)
                    nc.vector.tensor_tensor(parts8[b][:, :, 5, :], rest8[b][:, :, :], parts8[b][:, :, 3, :],
                                            ALU.subtract).then_inc(parts_ready, 1)
                    if base is not None:
                        dve.wait_ge(win_summed, g)
                        add_window(base, g - 1, D2, bank[4], sum_added)
                    if not last:
                        take_group(g + 1, 1 - b)
                    for j in range(T):
                        wait(dve, scattered[j], (g - 1) * (16 * ns))
                    for s in range(ns):
                        scatter_rows(b, s, g * (T * ns) + T * (s + 1), same_ready, g * ns + (s + 1), sidxf_done,
                                     sidx_ready)
                    dve.wait_ge(sig_done, g + 1)
                    if general:
                        dve.wait_ge(gathered[b], n * (16 * T * ns) + 16 * T * ns)
                        nc.vector.tensor_tensor(pay[b][0][:, :, D:D2], pay[b][0][:, :, 0:D], got[b][1][:, :, :],
                                                ALU.mult).then_inc(pay0_ready, 1)
                    else:
                        dve.wait_ge(dst_rows, g + 1)
                        nc.vector.tensor_tensor(pay[b][0][:, :, D:D2], pay[b][0][:, :, 0:D],
                                                bank[2][:, 0:T * D].rearrange("p (t d) -> p t d", t=T),
                                                ALU.mult).then_inc(pay0_ready, 1)
                        dve.wait_ge(gathered[b], n * (16 * T) + 16 * T)
                    nc.vector.tensor_tensor(pay[b][1][:, :, D:D2], pay[b][1][:, :, 0:D], got[b][0][:, :, :],
                                            ALU.mult).then_inc(pay1_ready, 1)
                    if not general and not last:
                        one_hots(g + 1, 1 - b)

                def late_take(m):
                    wait(dve, late_hid_mm, m)
                    nc.vector.tensor_copy(node_t[0][:, :], all_t[:, bass.ds(m * (BLK * NP), BLK * NP)])\
                      .then_inc(late_taken, 1)

                def late_keep(m):
                    dve.wait_ge(late_out_mm, m + 1)
                    keep_block(m, 0, late_out_bank, h1_sb, late_out_kept)

                take_group(0, 0)
                if not general:
                    one_hots(0, 0)
                for_all_with(dve, G, step, NBLK, late_take, nothing, late_keep)
                if not general:
                    dve.wait_ge(win_summed, G)
                    add_window(window_base(G - 1), G - 1, D2, bank[4], sum_added)
                    dve.wait_ge(sum_added, G)

            by_kind(dve, lambda: layer0(False), lambda: layer0(True))
            nc.vector.memset(count[0][1][0:1, 0:1], 0.0).then_inc(edges0_dve, 1)

            def merging(m, n, b):
                wide_in = [tab_in[b][0:NP, j, :, :] for j in range(TABLES)]
                to = work[0:NP, bass.ds(m * MB, MB), :]
                dve.wait_ge(m_tabs[b], n * (16 * TABLES) + 16 * TABLES)
                dve.wait_ge(m_turned, m + 1)
                nc.vector.tensor_tensor(to, wide_in[0], bank[6 + b][0:NP, 0:MB * D2].rearrange("p (c d) -> p c d", d=D2),
                                        ALU.add).then_inc(m_summed, 1)
                for j in range(1, TABLES):
                    dve.wait_ge(m_summed, m * (TABLES - 1) + j)
                    done = nc.vector.tensor_tensor(to, to, wide_in[j], ALU.add)
                    done.then_inc(m_summed if j < TABLES - 1 else m_added, 1)

            merging(0, 0, 0)
            merging(1, 0, 1)
            with dve.Fori(1, MBLK // 2) as i:
                merging(i * 2, i, 0)
                merging(i * 2 + 1, i, 1)
            dve.wait_ge(m_added, MBLK)
            gates, sums = work[0:NP, :, 0:D], work[0:NP, :, D:D2]
            chain(nc.vector.tensor_scalar(gates, gates, EPS_DENOM, None, ALU.add))
            chain(nc.vector.reciprocal(gates, gates))
            chain(nc.vector.tensor_tensor(sums, sums, gates, ALU.mult))
            chain(nc.vector.tensor_tensor(h1_sb[0:NP, :, :], h1_sb[0:NP, :, :], sums, ALU.add))
            chain(norm_relu(h1_sb[0:NP, :, :], h1_sb[0:NP, :, :], 1))
            chain(nc.vector.tensor_tensor(h1_sb[0:NP, :, :], h1_sb[0:NP, :, :], h_sb[0:NP, :, :], ALU.add))
            chain(nc.vector.tensor_tensor(x_sb[0:NP, :, :], x_sb[0:NP, :, :], h1_sb[0:NP, :, :], ALU.add))
            norm_relu(x_sb[0:NP, :, :], h_sb[0:NP, :, :], 2).then_inc(h_ready, 1)
            dve.wait_ge(sum_zeroed, 1)

            def layer1(general):
                def factors(g, n, b, between):
                    dve.wait_ge(l1_gathered[b], n * (16 * T) + 16 * T)
                    dve.wait_ge(l1_ea4_in[b], n * 16 + 16)
                    nc.vector.tensor_tensor(vv[:, :, :, :],
                                            got[b][0][:, :, U:D].rearrange("p t (u i) -> p t u i", i=VEC),
                                            ea4[b][:, :, 1:4].rearrange("p t (a i) -> p t a i", a=1)
                                            .to_broadcast([P, T, U, VEC]), ALU.mult).then_inc(l1_vv, 1)
                    between()
                    dve.wait_ge(l1_vv, g + 1)
                    nc.vector.tensor_reduce(zc[b][:, :, U:2 * U], vv[:, :, :, :], AX, ALU.add).then_inc(l1_vz, 1)

                def step(g, n, b):
                    if general:
                        wait(dve, l1_spread, g - 1)
                        take_keys(b, g, 1, g + 1, l1_key_split, l1_key)
                    dve.wait_ge(l1_mlp2, g + 1)
                    dve.wait_ge(l1_sz, g + 1)
                    dve.wait_ge(l1_vz, g + 1)
                    wait(dve, l1_red, g)
                    weights = pair[1 + b][:, :].rearrange("p (t n) -> p t n", t=T)
                    z = zc[b]
                    for i in range(VEC):
                        nc.vector.tensor_tensor(
                            prod[:, :, 3 + i, :, :],
                            weights[:, :, 3 * U * U:4 * U * U].rearrange("p t (u w) -> p t u w", w=U),
                            z[:, :, (3 + i) * U:(4 + i) * U].rearrange("p t (u a) -> p t u a", a=1)
                            .to_broadcast([P, T, U, U]), ALU.mult)
                    nc.vector.tensor_tensor(
                        prod[:, :, 0:3, :, :].rearrange("p t k u w -> p t (k u) w"),
                        weights[:, :, 0:3 * U * U].rearrange("p t (m w) -> p t m w", w=U),
                        z[:, :, 0:3 * U].rearrange("p t (m a) -> p t m a", a=1).to_broadcast([P, T, 3 * U, U]),
                        ALU.mult).then_inc(l1_prod, 1)

                    def last_window():
                        if base is not None:
                            dve.wait_ge(l1_win, g - 1)
                            add_window(base, g - 2, D, bank[6 + b], l1_added)

                    base = None if general or (isinstance(g, int) and g < 2) else window_base(g - 2)
                    if not (isinstance(g, int) and g == G - 1):
                        factors(g + 1, n + b, 1 - b, last_window)
                    else:
                        last_window()
                    wait(dve, l1_merge if general else l1_win, g - 1)
                    dve.wait_ge(l1_prod, g + 1)
                    nc.vector.tensor_reduce(red[:, :, :, :], prod[:, :, 2:6, :, :].rearrange("p t k u w -> p t k w u"),
                                            AX, ALU.add).then_inc(l1_vred, 1)
                    nc.vector.tensor_reduce(mess[b][:, :, 0:U],
                                            prod[:, :, 0:2, :, :].rearrange("p t k u w -> p t w (k u)"),
                                            AX, ALU.add).then_inc(l1_red, 1)
                    dve.wait_ge(l1_vred, g + 1)
                    nc.vector.tensor_tensor(outer[:, :, :, :],
                                            red[:, :, 0, :].rearrange("p t (w a) -> p t w a", a=1)
                                            .to_broadcast([P, T, U, VEC]),
                                            v2[b][:, :, :].rearrange("p t (a i) -> p t a i", a=1)
                                            .to_broadcast([P, T, U, VEC]), ALU.mult).then_inc(l1_outer, 1)
                    dve.wait_ge(l1_outer, g + 1)
                    nc.vector.tensor_tensor(mess[b][:, :, U:D].rearrange("p t (w i) -> p t w i", i=VEC),
                                            outer[:, :, :, :],
                                            red[:, :, 1:4, :].rearrange("p t i w -> p t w i"),
                                            ALU.add).then_inc(l1_mess, 1)
                    if general:
                        dve.wait_ge(l1_spread, g + 1)
                        compare(b, 1, bank[7], l1_same)
                        wait(dve, l1_scattered, (g - 1) * (16 * T))
                        scatter_rows(b, 1, g * T + T, l1_same, g + 1, l1_sidxf, l1_sidx)

                factors(0, 0, 0, lambda: None)
                for_all(dve, G, step)
                if not general:
                    for g in (G - 2, G - 1):
                        dve.wait_ge(l1_win, g + 1)
                        add_window(window_base(g), g, D, bank[6 + g % 2], l1_added)
                    dve.wait_ge(l1_added, G)

            by_kind(dve, lambda: layer1(False), lambda: layer1(True))
            nc.vector.memset(count[0][1][0:1, 0:1], 0.0).then_inc(edges1_dve, 1)

            def finishing(m, b):
                dve.wait_ge(m1_turned, m + 1)
                to = x_sb[0:NP, bass.ds(m * MB, MB), :]
                nc.vector.tensor_tensor(to, to, bank[6 + b][0:NP, 0:MB * D].rearrange("p (c d) -> p c d", d=D),
                                        ALU.add).then_inc(m1_added, 1)

            finishing(0, 0)
            finishing(1, 1)
            with dve.Fori(1, MBLK // 2) as i:
                finishing(i * 2, 0)
                finishing(i * 2 + 1, 1)
            dve.wait_ge(m1_added, MBLK)
            dve.wait_ge(tab1_read, 16)
            nc.vector.tensor_tensor(x_sb[0:NP, :, :], x_sb[0:NP, :, :], h1_sb[0:NP, :, :], ALU.add)\
              .then_inc(m1_added, 1)


_INS = ['x', 'src', 'dst', 'edge_attr_32', 'edge_attr_4', 'edge_attr_8', 'L0_gnn_W1a', 'L0_gnn_b1a', 'L0_gnn_W2a',
        'L0_gnn_b2a', 'L0_gnn_W1b', 'L0_gnn_b1b', 'L0_gnn_W2b', 'L0_gnn_b2b', 'L1_gnn_fc_w1', 'L1_gnn_fc_w2']


def kernel(**inputs):
    import numpy as _np
    import concourse.bacc as _bacc
    from concourse import mybir as _mybir
    from concourse.bass_utils import run_bass_kernel_spmd as _run

    nc = _bacc.Bacc("TRN2", target_bir_lowering=False, num_devices=1)
    arrays, args = {}, []
    for name in _INS:
        a = _np.ascontiguousarray(inputs[name])
        arrays[f"in_{name}_dram"] = a
        args.append(nc.dram_tensor(f"in_{name}_dram", a.shape, _mybir.dt.from_np(a.dtype), kind="ExternalInput").ap())
    out = nc.dram_tensor("out_0_dram", inputs["x"].shape, _mybir.dt.float32, kind="ExternalOutput").ap()
    gnn_kernel(nc, *args, out)
    r = _run(nc, [arrays], core_ids=[0])
    return r.results[0]["out_0_dram"]
```

```python
from contextlib import ExitStack

import numpy as np

import concourse.bass as bass
from concourse import mybir

F32 = mybir.dt.float32
BF16 = mybir.dt.bfloat16
I32 = mybir.dt.int32
ALU = mybir.AluOpType
ACT = mybir.ActivationFunctionType
AX = mybir.AxisListType.X

P = 128
T = 4
GROUP = P * T
WINDOW = 64
TABLES = T
SLOTS = 6
SHIFT = 1000.0


def gnn_kernel(nc, x, src, dst, edge32, edge4, edge8, w1a, b1a, w2a, b2a, w1b, b1b, w2b, b2b,
               fc1, fc2, out):
    N, D = x.shape
    E = src.shape[0]
    H = w1a.shape[1]
    NB = edge8.shape[1]
    HID = fc1.shape[1]
    WN = fc2.shape[1]
    U = 8
    VEC = 3
    D2 = 2 * D
    G = -(-E // GROUP)
    SEEN = (G * GROUP - E) // T
    assert N + P <= 2 ** 16 and WINDOW <= 2 ** 8
    assert G % 2 == 1 and (G * GROUP - E) % T == 0 and SEEN <= P
    NP = 125
    NC = N // NP
    NBLK, BLK = 25, 4
    MBLK, MB = 20, 5
    assert NP * NC == N and NBLK * BLK == NC and MBLK * MB == NC and BLK * D == P and D == 4 * U
    ROWS = N + P
    NPAD = N + WINDOW
    EPS = 1e-5
    EPS_DENOM = 1e-7
    KS = SLOTS * NB
    A_SCALAR = float(np.sqrt(1.0 / 128.0))
    A_VECTOR = float(np.sqrt(3.0 / 128.0))
    INV3 = float(1.0 / np.sqrt(3.0))
    COMMON = float(np.sqrt(2.0) / np.sqrt(HID) / np.sqrt(E / N))
    BLOCK_SCALE = [A_SCALAR * COMMON, A_SCALAR * INV3 * COMMON, A_VECTOR * INV3 * COMMON, A_VECTOR * INV3 * COMMON]
    ORDER = [2, 0, 1, 3]
    SCALARS = 2
    HALF, KEPT = U // 2, U // 4
    SUM = (SCALARS + VEC) * KEPT * U
    W_LOADS = 2 * 4 + 1 + len(ORDER)
    ROWQ = [min(P, G - q * P) for q in range(-(-G // P))]

    acc_tab = [nc.dram_tensor(f"acc_tab{j}", (ROWS, D2), F32).ap() for j in range(TABLES)]
    acc1_tab = nc.dram_tensor("acc1_tab", (ROWS, D), F32).ap()
    h2_tab = nc.dram_tensor("h2_tab", (NPAD, D), F32).ap()
    h1_tab = nc.dram_tensor("h1_tab", (N, D), F32).ap()
    est_tab = nc.dram_tensor("est_tab", (G, KS, GROUP), BF16).ap()

    def nodes(a):
        return a[0:N, :].rearrange("(p c) d -> p c d", c=NC)

    def edges(a, g):
        start = E - GROUP if isinstance(g, int) and g == G - 1 else g * GROUP
        if len(a.shape) == 1:
            return a[bass.ds(start, GROUP)].rearrange("(p j) -> p j", j=T)
        return a[bass.ds(start, GROUP), :].rearrange("(p j) d -> p j d", j=T)

    ctx = ExitStack()
    with ctx:
        def sb(name, shape, dt=F32):
            return ctx.enter_context(nc.sbuf_tensor(name, shape, dt))

        def sem(name):
            return ctx.enter_context(nc.semaphore(name))

        ident = sb("ident", [P, P])
        identb = sb("identb", [P, P], BF16)
        later = sb("later", [P, P])
        iota_w = sb("iota_w", [P, WINDOW])
        trash = sb("trash", [P, 1])
        ones = sb("ones", [P, 1])
        row = sb("row", [P, 1])
        w1s = [sb(f"w1s{k}", [D, H]) for k in range(2)]
        b1s = [sb(f"b1s{k}", [P, 1]) for k in range(2)]
        w2s = [sb(f"w2s{k}", [P, D]) for k in range(2)]
        b2s = [sb(f"b2s{k}", [P, D]) for k in range(2)]
        fc1f = sb("fc1f", [NB, HID])
        fc1r = sb("fc1r", [NB, 2, HID])
        fc1p = sb("fc1p", [NB, 3, HID], BF16)
        fc1s = sb("fc1s", [KS, HID], BF16)
        fc2s = sb("fc2s", [P, 2, WN])
        local = sb("local", [P, G, T])
        key_all = [sb(f"key_all{s}", [P, G, T]) for s in range(2)]
        base_i = sb("base_i", [1, G], I32)
        bound = sb("bound", [P, 2 * len(ROWQ)])
        outside = sb("outside", [P, 2 * len(ROWQ)])
        outside_sum = sb("outside_sum", [P, 1])
        flag_i = sb("flag_i", [1, 1], I32)
        sum_t = sb("sum_t", [P, NPAD])
        all_t = sum_t[D2:D2 + D, 0:N]
        x_sb = sb("x_sb", [P, NC, D])
        h_sb = sb("h_sb", [P, NC, D])
        h1_sb = sb("h1_sb", [P, NC, D])
        work = sb("work", [P, NC, D2])
        flat = work[:, :, :].rearrange("p c d -> p (c d)")
        tmp_a = flat[:, 0:NC * D].rearrange("p (c d) -> p c d", d=D)
        tmp_b = flat[:, NC * D:].rearrange("p (c d) -> p c d", d=D)
        small = [sb(f"small{k}", [P, NC]) for k in range(3)]
        stage = [sb(f"stage{b}", [P, P]) for b in range(2)]
        mst = [sb(f"mst{b}", [max(D2, SUM), MB, NP]) for b in range(2)]
        hid = [[sb(f"hid{b}{c}", [P, GROUP]) for c in range(2)] for b in range(2)]
        hid_n = [hid[b][0][:, 0:BLK * NP].rearrange("p (c n) -> p c n", c=BLK) for b in range(2)]
        tab_in = [sb(f"tab_in{b}", [P, TABLES, MB, D2]) for b in range(2)]
        tab_flat_in = [tab_in[b][:, :, :, :].rearrange("p j c d -> p (j c d)") for b in range(2)]
        rows_i = [tab_flat_in[b][:, 0:2 * GROUP].bitcast(I32).rearrange("p (s e) -> p s e", s=2) for b in range(2)]
        node_t = [tab_flat_in[b][0:D, 0:BLK * NP] for b in range(2)]
        rows_f = hid
        gidx = [[sb(f"gidx{b}{s}", [P, T], I32) for s in range(2)] for b in range(2)]
        same = [[sb(f"same{b}{s}", [P, T, P]) for s in range(2)] for b in range(2)]
        rows_l = [same[b][0][:, :, :].rearrange("p t e -> p (t e)") for b in range(2)]
        key = [[sb(f"key{b}{s}", [P, T]) for s in range(2)] for b in range(2)]
        key_parts = [[sb(f"key_parts{b}{s}", [P, 2, T], BF16) for s in range(2)] for b in range(2)]
        localb = [sb(f"localb{b}", [P, T], BF16) for b in range(2)]
        keym = [[sb(f"keym{b}{s}", [P, T]) for s in range(2)] for b in range(2)]
        count = [[sb(f"count{b}{s}", [P, T]) for s in range(2)] for b in range(2)]
        sidx_f = [[sb(f"sidx_f{b}{s}", [P, T]) for s in range(2)] for b in range(2)]
        sidx = [[sb(f"sidx{b}{s}", [P, T], I32) for s in range(2)] for b in range(2)]
        merged = [[sb(f"merged{b}{s}", [P, T, D2]) for s in range(2)] for b in range(2)]
        onehot = [sb(f"onehot{b}", [P, T, WINDOW]) for b in range(2)]
        got = [[sb(f"got{b}{s}", [P, T, D]) for s in range(2)] for b in range(2)]
        ea32 = [sb(f"ea32{b}", [P, T, D]) for b in range(2)]
        ea8 = [sb(f"ea8{b}", [P, T, NB]) for b in range(2)]
        rest8 = [sb(f"rest8{b}", [P, T, NB]) for b in range(2)]
        parts8 = [sb(f"parts8{b}", [P, T, SLOTS, NB], BF16) for b in range(2)]
        onehot_t = [mst[b][0:WINDOW, :, :].rearrange("w c n -> w (c n)")[:, 0:T * P]
                    .rearrange("w (t e) -> w t e", t=T) for b in range(2)]
        win = [sb(f"win{b}", [WINDOW, D]) for b in range(2)]
        pay = [[sb(f"pay{b}{s}", [P, T, D2]) for s in range(2)] for b in range(2)]
        est = [sb(f"est{b}", [KS, GROUP], BF16) for b in range(2)]
        ea4 = [sb(f"ea4{b}", [P, T, 4]) for b in range(2)]
        v2 = [sb(f"v2{b}", [P, T, VEC]) for b in range(2)]
        zc = [sb(f"zc{b}", [P, T, 6 * U]) for b in range(2)]
        vv = sb("vv", [P, T, U, VEC])
        prod = sb("prod", [P, T, 6, U, U])
        apart = sb("apart", [P, T, WINDOW])
        red = sb("red", [P, T, U])
        pick = sb("pick", [SUM, D])
        terms = [sb(f"terms{b}", [P, T, SUM]) for b in range(2)]
        outer = sb("outer", [P, T, U, VEC])
        mess = [sb(f"mess{b}", [P, T, D]) for b in range(2)]

        BANK = 512
        pair = [ctx.enter_context(nc.psum_tensor(f"pair{i}", [P, 2 * BANK], F32)) for i in range(4)]
        bank = [pair[i // 2][:, (i % 2) * BANK:(i % 2 + 1) * BANK] for i in range(8)]
        turn_bank, hid_bank, out_bank = [bank[0], bank[7]], [bank[1], bank[2]], [bank[5], bank[6]]
        late_hid_bank, late_out_bank = bank[6], bank[7]
        index_bank = [bank[0:3], bank[5:8]]

        in_loads = sem("in_loads")
        w_loads = sem("w_loads")
        c_pool = sem("c_pool")
        zeroed = sem("zeroed")
        tab_zero = sem("tab_zero")
        fc_parts = sem("fc_parts")
        fc_scaled = sem("fc_scaled")
        pick_ready = sem("pick_ready")
        rows_conv = sem("rows_conv")
        rows_ready = sem("rows_ready")
        rows_turned = sem("rows_turned")
        rows_kept = sem("rows_kept")
        base_turned = sem("base_turned")
        base_kept = sem("base_kept")
        outside_ready = sem("outside_ready")
        outside_counted = sem("outside_counted")
        chained = sem("chained")
        passed = {e.engine: sem(f"passed_{k}") for k, e in enumerate([nc.sync, nc.gpsimd, nc.tensor, nc.vector])}
        row_loads = [sem(f"row_loads{b}") for b in range(2)]
        fc_moved = sem("fc_moved")
        flag_ready = sem("flag_ready")
        centred = sem("centred")
        squared = sem("squared")
        variance_ready = sem("variance_ready")
        root_ready = sem("root_ready")
        h_ready = sem("h_ready")
        staged = sem("staged")
        turned = sem("turned")
        turned_kept = sem("turned_kept")
        hid_mm = sem("hid_mm")
        hid_kept = sem("hid_kept")
        out_mm = sem("out_mm")
        out_kept = sem("out_kept")
        late_taken = sem("late_taken")
        late_hid_mm = sem("late_hid_mm")
        late_hid_kept = sem("late_hid_kept")
        late_out_mm = sem("late_out_mm")
        late_out_kept = sem("late_out_kept")
        h2_stored = sem("h2_stored")
        m_staged = sem("m_staged")
        m_turned = sem("m_turned")
        m_paired = sem("m_paired")
        m_summed = sem("m_summed")
        m_steps = sem("m_steps")
        m_done = sem("m_done")
        m_added = sem("m_added")
        m_tabs = [sem(f"m_tabs{b}") for b in range(2)]
        m1_staged = sem("m1_staged")
        m1_turned = sem("m1_turned")
        m1_added = sem("m1_added")
        sum_zeroed = sem("sum_zeroed")
        h1_stored = sem("h1_stored")
        tab1_read = sem("tab1_read")
        stored = sem("stored")
        ea32_in = [sem(f"ea32_in{b}") for b in range(2)]
        ea8_in = [sem(f"ea8_in{b}") for b in range(2)]
        gidx_in = [sem(f"gidx_in{b}") for b in range(2)]
        win_in = [sem(f"win_in{b}") for b in range(2)]
        est_out = [sem(f"est_out{b}") for b in range(2)]
        gathered = [sem(f"gathered{b}") for b in range(2)]
        scattered = [sem(f"scattered{j}") for j in range(TABLES)]
        sig_done = sem("sig_done")
        part1_done = sem("part1_done")
        rest_done = sem("rest_done")
        part2_done = sem("part2_done")
        parts_ready = sem("parts_ready")
        parts_turned = sem("parts_turned")
        est_ready = sem("est_ready")
        key_split = sem("key_split")
        key_ready = sem("key_ready")
        local_ready = sem("local_ready")
        local_spread = sem("local_spread")
        key_spread = sem("key_spread")
        same_ready = sem("same_ready")
        sidxf_done = sem("sidxf_done")
        sidx_ready = sem("sidx_ready")
        oh_ready = sem("oh_ready")
        oht_ready = sem("oht_ready")
        dst_rows = sem("dst_rows")
        pay0_ready = sem("pay0_ready")
        pay1_ready = sem("pay1_ready")
        merge_done = sem("merge_done")
        merged_ready = sem("merged_ready")
        win_summed = sem("win_summed")
        sum_added = sem("sum_added")
        edges0_pool = sem("edges0_pool")
        edges0_dve = sem("edges0_dve")
        l1_ea4_in = [sem(f"l1_ea4_in{b}") for b in range(2)]
        l1_est_in = [sem(f"l1_est_in{b}") for b in range(2)]
        l1_gidx_in = [sem(f"l1_gidx_in{b}") for b in range(2)]
        l1_gathered = [sem(f"l1_gathered{b}") for b in range(2)]
        l1_scattered = sem("l1_scattered")
        l1_mlp1 = sem("l1_mlp1")
        l1_relu = sem("l1_relu")
        l1_mlp2 = sem("l1_mlp2")
        l1_sz = sem("l1_sz")
        l1_far = sem("l1_far")
        l1_vv = sem("l1_vv")
        l1_vz = sem("l1_vz")
        l1_prod_a = sem("l1_prod_a")
        l1_prod = sem("l1_prod")
        l1_vred = sem("l1_vred")
        l1_halved = sem("l1_halved")
        l1_terms = sem("l1_terms")
        l1_outer = sem("l1_outer")
        l1_mess = sem("l1_mess")
        l1_oh = sem("l1_oh")
        l1_win = sem("l1_win")
        l1_added = sem("l1_added")
        l1_key_split = sem("l1_key_split")
        l1_key = sem("l1_key")
        l1_spread = sem("l1_spread")
        l1_same = sem("l1_same")
        l1_sidxf = sem("l1_sidxf")
        l1_sidx = sem("l1_sidx")
        l1_merge = sem("l1_merge")
        l1_merged = sem("l1_merged")
        edges1_pool = sem("edges1_pool")
        edges1_dve = sem("edges1_dve")

        def wait(eng, s, n):
            if not isinstance(n, int) or n > 0:
                eng.wait_ge(s, n)

        def stand(eng):
            eng.sem_inc(passed[eng.engine], 1)

        def for_all(eng, n, step):
            step(0, 0, 0)
            step(1, 0, 1)
            with eng.Fori(1, n // 2) as i:
                step(i * 2, i, 0)
                step(i * 2 + 1, i, 1)
            step(n - 1, (n - 1) // 2, 0)

        def for_all_by_four(eng, n, step):
            peeled = 6 + (n - 3) % 4
            for g in range(peeled):
                step(g, g // 2, g % 2)
            with eng.Fori(0, (n - 1 - peeled) // 4) as i:
                for k in range(peeled, peeled + 4):
                    step(i * 4 + k, i * 2 + k // 2, k % 2)
            step(n - 1, (n - 1) // 2, 0)

        def for_all_with(eng, n, step, count, before, amid, after):
            def two(i, base):
                before(i)
                step(base, i, 0)
                amid(i)
                step(base + 1, i, 1)
                after(i)

            two(0, 0)
            with eng.Fori(1, count) as i:
                two(i, i * 2)
            with eng.Fori(count, n // 2) as i:
                step(i * 2, i, 0)
                step(i * 2 + 1, i, 1)
            step(n - 1, (n - 1) // 2, 0)

        def nothing(m):
            pass

        def by_kind(eng, fast, general):
            eng.wait_ge(flag_ready, 1)
            n_outside = eng.value_load(flag_i[0:1, 0:1], min_val=0, max_val=4 * P * len(ROWQ))
            with eng.If(n_outside > 0):
                general()
            with eng.Else():
                fast()

        block = ctx.enter_context(nc.Block())

        @block.sync
        def _(sp):
            sp.dma_start(x_sb[0:NP, :, :], nodes(x)).then_inc(in_loads, 16)

            def index_rows(q):
                rows = ROWQ[q]
                whole = rows if (q + 1) * P < G else rows - 1
                wait(sp, rows_conv, (q - 1) * 2)
                for s, a in enumerate([src, dst]):
                    sp.dma_start(rows_i[q % 2][0:whole, s, :],
                                 a[q * P * GROUP:(q * P + whole) * GROUP].rearrange("(g e) -> g e", e=GROUP))\
                        .then_inc(row_loads[q % 2], 16)
                    if whole < rows:
                        sp.dma_start(rows_i[q % 2][whole:rows, s, :], a[E - GROUP:E].rearrange("(g e) -> g e", g=1))\
                            .then_inc(row_loads[q % 2], 16)

            index_rows(0)
            index_rows(1)
            for k, (w1, b1, w2, b2) in enumerate([(w1a, b1a, w2a, b2a), (w1b, b1b, w2b, b2b)]):
                sp.dma_start(w1s[k][:, :], w1).then_inc(w_loads, 16)
                sp.dma_start(b1s[k][:, :], b1.rearrange("(h a) -> h a", a=1)).then_inc(w_loads, 16)
                sp.dma_start(w2s[k][:, :], w2).then_inc(w_loads, 16)
                sp.dma_start(b2s[k][:, :], b2.rearrange("(a d) -> a d", a=1).to_broadcast([P, D])).then_inc(w_loads, 16)
            sp.dma_start(fc1f[:, :], fc1).then_inc(w_loads, 16)
            for at, blk in enumerate(ORDER):
                sp.dma_start(fc2s[:, :, at * U * U:(at + 1) * U * U],
                             fc2[:, blk * U * U:(blk + 1) * U * U].rearrange("(c k) n -> k c n", c=2))\
                    .then_inc(w_loads, 16)
            for q in range(2, len(ROWQ)):
                index_rows(q)
            sp.wait_ge(fc_parts, 1)
            for k, part in enumerate([0, 1, 2, 0, 1, 0]):
                sp.dma_start(fc1s[k * NB:(k + 1) * NB, :], fc1p[:, part, :]).then_inc(fc_moved, 16)
            sp.wait_ge(out_kept, NBLK)
            sp.dma_start(nodes(h2_tab), tmp_b[0:NP, :, :]).then_inc(h2_stored, 16)
            sp.wait_ge(zeroed, 2)
            sp.dma_start(h2_tab[N:NPAD, :], sum_t[0:WINDOW, 0:D]).then_inc(h2_stored, 16)
            sp.wait_ge(h2_stored, 32)

            def layer0(general):
                ns = 2 if general else 1

                def step(g, n, b):
                    wait(sp, sig_done, g - 1)
                    stand(sp)
                    sp.dma_start(ea32[b][:, :, :], edges(edge32, g)).then_inc(ea32_in[b], 16)
                    wait(sp, gathered[b], n * (16 * T * ns))
                    stand(sp)
                    sp.dma_start(gidx[b][0][:, :], edges(src, g)).then_inc(gidx_in[b], 16)
                    if general:
                        sp.dma_start(gidx[b][1][:, :], edges(dst, g)).then_inc(gidx_in[b], 16)
                    wait(sp, parts_ready, g - 1)
                    stand(sp)
                    sp.dma_start(ea8[b][:, :, :], edges(edge8, g)).then_inc(ea8_in[b], 16)
                    if not general:
                        wait(sp, dst_rows, g - 1)
                        stand(sp)
                        base = sp.value_load(base_i[0:1, bass.ds(g, 1)], min_val=0, max_val=N - 1)
                        sp.dma_start(win[b][:, :], h2_tab[bass.ds(base, WINDOW), :]).then_inc(win_in[b], 16)
                    if not (isinstance(g, int) and g == 0):
                        store(g - 1, 1 - b)

                def store(g, b):
                    wait(sp, est_ready, g + 1)
                    stand(sp)
                    sp.dma_start(est_tab[bass.ds(g, 1), :, :].rearrange("a k e -> (a k) e"), est[b][:, :])\
                      .then_inc(est_out[b], 16)

                for_all(sp, G, step)
                store(G - 1, (G - 1) % 2)
                sp.wait_ge(est_out[0], 16 * (G // 2 + 1))
                sp.wait_ge(est_out[1], 16 * (G // 2))

            by_kind(sp, lambda: layer0(False), lambda: layer0(True))

            sp.wait_ge(edges0_pool, 1)

            def tables(m, b):
                for j in range(TABLES):
                    sp.dma_start(tab_in[b][0:NP, j, :, :], nodes(acc_tab[j])[:, bass.ds(m * MB, MB), :])\
                      .then_inc(m_tabs[b], 16)

            tables(0, 0)
            tables(1, 1)
            with sp.Fori(1, MBLK // 2) as i:
                for b in range(2):
                    sp.wait_ge(m_summed, i * 2 + (b - 1))
                    stand(sp)
                    tables(i * 2 + b, b)
            sp.wait_ge(h_ready, 2)
            sp.dma_start(nodes(h1_tab), h_sb[0:NP, :, :]).then_inc(h1_stored, 16)
            sp.wait_ge(h1_stored, 16)

            def layer1(g, n, b):
                wait(sp, l1_gathered[b], n * (16 * T))
                stand(sp)
                sp.dma_start(gidx[b][0][:, :], edges(src, g)).then_inc(l1_gidx_in[b], 16)
                wait(sp, l1_mlp1, (g - 1) * 2)
                stand(sp)
                sp.dma_start(est[b][:, :], est_tab[bass.ds(g, 1), :, :].rearrange("a k e -> (a k) e"))\
                  .then_inc(l1_est_in[b], 16)
                wait(sp, l1_vv, g - 1)
                wait(sp, l1_sz, g - 1)
                stand(sp)
                sp.dma_start(ea4[b][:, :, :], edges(edge4, g)).then_inc(l1_ea4_in[b], 16)

            for_all(sp, G, layer1)
            sp.wait_ge(edges1_pool, 1)
            sp.dma_start(h1_sb[0:NP, :, :], nodes(acc1_tab)).then_inc(tab1_read, 16)
            sp.wait_ge(m1_added, MBLK + 1)
            sp.dma_start(nodes(out), x_sb[0:NP, :, :]).then_inc(stored, 16)
            sp.wait_ge(stored, 16)

        @block.gpsimd
        def _(pool):
            nc.gpsimd.memset(h1_sb[:, :, :], 0.0).then_inc(zeroed, 1)
            nc.gpsimd.memset(ones[:, :], 1.0).then_inc(c_pool, 1)
            nc.gpsimd.memset(ident[:, :], 0.0).then_inc(c_pool, 1)
            nc.gpsimd.memset(later[:, :], 1.0).then_inc(c_pool, 1)
            pool.wait_ge(c_pool, 3)
            nc.gpsimd.affine_select(out=ident[:, :], in_=ident[:, :], compare_op=ALU.not_equal, fill=1.0, base=0,
                                    pattern=[[-1, P]], channel_multiplier=1).then_inc(c_pool, 1)
            nc.gpsimd.affine_select(out=later[:, :], in_=later[:, :], compare_op=ALU.is_ge, fill=0.0, base=0,
                                    pattern=[[1, P]], channel_multiplier=-1).then_inc(c_pool, 1)
            nc.gpsimd.iota(iota_w[:, :], pattern=[[1, WINDOW]], base=0, channel_multiplier=0,
                           allow_small_or_imprecise_dtypes=True).then_inc(c_pool, 1)
            nc.gpsimd.iota(trash[:, :], pattern=[[0, 1]], base=N, channel_multiplier=1,
                           allow_small_or_imprecise_dtypes=True).then_inc(c_pool, 1)
            nc.gpsimd.iota(row[:, :], pattern=[[0, 1]], base=0, channel_multiplier=1,
                           allow_small_or_imprecise_dtypes=True).then_inc(c_pool, 1)
            pool.wait_ge(c_pool, 8)
            nc.gpsimd.tensor_copy(identb[:, :], ident[:, :]).then_inc(c_pool, 1)
            pool.wait_ge(zeroed, 1)
            for tab in acc_tab + [acc1_tab]:
                tab_flat = tab.rearrange("n d -> (n d)").rearrange("(p n) -> p n", p=P)
                width = ROWS * tab.shape[1] // P
                for start in range(0, width, NC * D):
                    size = min(NC * D, width - start)
                    pool.dma_start(tab_flat[:, start:start + size],
                                   h1_sb[:, :, :].rearrange("p c d -> p (c d)")[:, 0:size]).then_inc(tab_zero, 16)
            nc.gpsimd.memset(sum_t[0:D2, :], 0.0).then_inc(zeroed, 1)
            pool.wait_ge(tab_zero, 16 * sum(-(-ROWS * tab.shape[1] // P // (NC * D)) for tab in acc_tab + [acc1_tab]))
            pool.wait_ge(h2_stored, 32)

            def layer0(general):
                ns = 2 if general else 1

                def gather(g, n, b):
                    pool.wait_ge(gidx_in[b], n * (16 * ns) + 16 * ns)
                    wait(pool, pay1_ready, g - 1)
                    if general:
                        wait(pool, pay0_ready, g - 1)
                    stand(pool)
                    for s in range(ns):
                        for j in range(T):
                            pool.indirect_dma_start(got[b][s][:, j, :], None, h2_tab,
                                                    bass.IndirectOffsetOnAxis(ap=gidx[b][s][:, j:j + 1], axis=0))\
                                .then_inc(gathered[b], 16)

                def step(g, n, b):
                    if not (isinstance(g, int) and g == G - 1):
                        gather(g + 1, n + b, 1 - b)
                    pool.wait_ge(merged_ready, g + 1)
                    pool.wait_ge(sidx_ready, (g + 1) * ns)
                    for s in range(ns):
                        for j in range(T):
                            wait(pool, scattered[j], (g * ns + s) * 16)
                            stand(pool)
                            pool.indirect_dma_start(acc_tab[j],
                                                    bass.IndirectOffsetOnAxis(ap=sidx[b][s][:, j:j + 1], axis=0),
                                                    merged[b][s][:, j, :], None, compute_op=ALU.add)\
                                .then_inc(scattered[j], 16)

                gather(0, 0, 0)
                for_all(pool, G, step)
                for j in range(TABLES):
                    pool.wait_ge(scattered[j], 16 * G * ns)

            by_kind(pool, lambda: layer0(False), lambda: layer0(True))
            nc.gpsimd.memset(count[0][0][0:1, 0:1], 0.0).then_inc(edges0_pool, 1)

            def merging(m, n, b):
                rows = [tab_in[b][0:NP, j, :, :] for j in range(TABLES)]
                pool.wait_ge(m_tabs[b], n * (16 * TABLES) + 16 * TABLES)
                nc.gpsimd.tensor_tensor(rows[0], rows[0], rows[1], ALU.add)
                nc.gpsimd.tensor_tensor(rows[2], rows[2], rows[3], ALU.add).then_inc(m_paired, 1)
                pool.wait_ge(m_paired, m + 1)
                nc.gpsimd.tensor_tensor(work[0:NP, bass.ds(m * MB, MB), :], rows[0], rows[2], ALU.add)\
                    .then_inc(m_summed, 1)

            merging(0, 0, 0)
            merging(1, 0, 1)
            with pool.Fori(1, MBLK // 2) as i:
                merging(i * 2, i, 0)
                merging(i * 2 + 1, i, 1)

            pool.wait_ge(m_staged, MBLK)
            nc.gpsimd.memset(sum_t[0:SUM, :], 0.0).then_inc(sum_zeroed, 1)
            pool.wait_ge(h1_stored, 16)

            def layer1(general):
                def gather(g, n, b):
                    pool.wait_ge(l1_gidx_in[b], n * 16 + 16)
                    wait(pool, l1_vv, g - 1)
                    wait(pool, l1_sz, g - 1)
                    stand(pool)
                    for j in range(T):
                        pool.indirect_dma_start(got[b][0][:, j, :], None, h1_tab,
                                                bass.IndirectOffsetOnAxis(ap=gidx[b][0][:, j:j + 1], axis=0))\
                            .then_inc(l1_gathered[b], 16)

                def step(g, n, b):
                    if not (isinstance(g, int) and g == G - 1):
                        gather(g + 1, n + b, 1 - b)
                    pool.wait_ge(l1_merged, g + 1)
                    pool.wait_ge(l1_sidx, g + 1)
                    for j in range(T):
                        wait(pool, l1_scattered, (g * T + j) * 16)
                        stand(pool)
                        pool.indirect_dma_start(acc1_tab,
                                                bass.IndirectOffsetOnAxis(ap=sidx[b][1][:, j:j + 1], axis=0),
                                                merged[b][1][:, j, 0:D], None, compute_op=ALU.add)\
                            .then_inc(l1_scattered, 16)

                if general:
                    gather(0, 0, 0)
                    for_all(pool, G, step)
                    pool.wait_ge(l1_scattered, 16 * T * G)
                else:
                    for_all(pool, G, gather)

            by_kind(pool, lambda: layer1(False), lambda: layer1(True))
            nc.gpsimd.memset(count[0][0][0:1, 0:1], 0.0).then_inc(edges1_pool, 1)

        @block.scalar
        def _(act):
            def root(k):
                act.wait_ge(variance_ready, k + 1)
                nc.scalar.activation(small[2][0:NP, :], small[1][0:NP, :], ACT.Sqrt).then_inc(root_ready, 1)

            def convert_rows(q):
                rows = ROWQ[q]
                act.wait_ge(row_loads[q % 2], 16 * sum(2 if (k + 1) * P < G else 4 for k in range(q % 2, q + 1, 2)))
                wait(act, base_turned, q - 1)
                for s in range(2):
                    nc.scalar.copy(rows_f[q % 2][s][0:rows, :], rows_i[q % 2][0:rows, s, :]).then_inc(rows_conv, 1)

            def keep_rows(q):
                rows = ROWQ[q]
                act.wait_ge(rows_turned, q + 1)
                for s, table in enumerate([key_all[0], key_all[1], local]):
                    nc.scalar.copy(table[:, q * P:q * P + rows, :].rearrange("p g t -> p t g"),
                                   index_bank[q % 2][s][:, :].rearrange("p (t g) -> p t g", t=T)[:, :, 0:rows])\
                      .then_inc(rows_kept, 1)
                act.wait_ge(base_turned, q + 1)
                nc.scalar.copy(base_i[0:1, q * P:q * P + rows], bank[3][0:1, q * P:q * P + rows])\
                  .then_inc(base_kept, 1)

            for q in range(len(ROWQ)):
                convert_rows(q)
                if q > 0:
                    keep_rows(q - 1)
            keep_rows(len(ROWQ) - 1)

            root(0)

            act.wait_ge(w_loads, 16 * W_LOADS)
            act.wait_ge(h_ready, 1)

            def to_stage(m, b):
                wait(act, turned, m - 1)
                nc.scalar.copy(stage[b][0:NP, 0:P],
                               h_sb[0:NP, bass.ds(m * BLK, BLK), :].rearrange("p c d -> p (c d)")).then_inc(staged, 1)

            def perceptron(m, n, b):
                if not (isinstance(m, int) and m == NBLK - 1):
                    to_stage(m + 1, 1 - b)
                wait(act, out_mm, m - 1)
                act.wait_ge(hid_mm, m + 1)
                nc.scalar.activation(hid_n[b][:, :, :],
                                     hid_bank[b][:, 0:BLK * NP].rearrange("p (c n) -> p c n", c=BLK), ACT.Relu,
                                     bias=b1s[1][:, 0:1]).then_inc(hid_kept, 1)

            to_stage(0, 0)
            for_all(act, NBLK, perceptron)

            def layer0(general):
                ns = 2 if general else 1

                def step(g, n, b):
                    act.wait_ge(ea32_in[b], n * 16 + 16)
                    wait(act, merge_done, g - 1)
                    if not general:
                        wait(act, win_summed, g - 1)
                    for s in range(2):
                        gate = nc.scalar.activation(pay[b][s][:, :, 0:D], ea32[b][:, :, :], ACT.Sigmoid)
                    gate.then_inc(sig_done, 1)
                    act.wait_ge(ea8_in[b], n * 16 + 16)
                    wait(act, parts_turned, g - 1)
                    nc.scalar.copy(parts8[b][:, :, 0:3, :],
                                   ea8[b][:, :, :].rearrange("p t (a k) -> p t a k", a=1).to_broadcast([P, T, 3, NB]))\
                      .then_inc(part1_done, 1)
                    act.wait_ge(rest_done, g + 1)
                    nc.scalar.copy(parts8[b][:, :, 3:5, :],
                                   rest8[b][:, :, :].rearrange("p t (a k) -> p t a k", a=1).to_broadcast([P, T, 2, NB]))\
                      .then_inc(part2_done, 1)
                    act.wait_ge(merge_done, g + 1)
                    for j in range(T):
                        wait(act, scattered[j], (g - 1) * (16 * ns))
                    for s in range(ns):
                        kept = nc.scalar.copy(merged[b][s][:, :, :].rearrange("p t d -> p (t d)"),
                                              bank[3 + s][:, 0:T * D2])
                    kept.then_inc(merged_ready, 1)
                    act.wait_ge(parts_turned, g + 1)
                    wait(act, est_out[b], n * 16)
                    nc.scalar.copy(est[b][:, :], bank[5][0:KS, 0:GROUP // 2].bitcast(BF16)).then_inc(est_ready, 1)

                def late_relu(m):
                    act.wait_ge(late_hid_mm, m + 1)
                    wait(act, late_out_mm, m)
                    nc.scalar.activation(hid_n[0][:, :, :],
                                         late_hid_bank[:, 0:BLK * NP].rearrange("p (c n) -> p c n", c=BLK), ACT.Relu,
                                         bias=b1s[0][:, 0:1]).then_inc(late_hid_kept, 1)

                for_all_with(act, G, step, NBLK, nothing, late_relu, nothing)

            by_kind(act, lambda: layer0(False), lambda: layer0(True))

            act.wait_ge(edges0_dve, 1)
            def merging(m, b, width, s_staged, s_turned):
                wait(act, s_turned, m - 1)
                nc.scalar.copy(mst[b][0:width, :, :],
                               sum_t[0:width, 0:N].rearrange("f (p c) -> f c p", c=NC)[:, bass.ds(m * MB, MB), :])\
                  .then_inc(s_staged, 1)

            def merge_all(width, s_staged, s_turned):
                merging(0, 0, width, s_staged, s_turned)
                merging(1, 1, width, s_staged, s_turned)
                with act.Fori(1, MBLK // 2) as i:
                    merging(i * 2, 0, width, s_staged, s_turned)
                    merging(i * 2 + 1, 1, width, s_staged, s_turned)

            merge_all(D2, m_staged, m_turned)
            for k in range(1, 3):
                for half in range(2):
                    act.wait_ge(centred, 2 * (k - 1) + half + 1)
                    cols = slice(half * (NC // 2), (half + 1) * (NC // 2))
                    nc.scalar.activation(tmp_b[0:NP, cols, :], tmp_a[0:NP, cols, :], ACT.Square).then_inc(squared, 1)
                root(k)

            def layer1(general):
                def step(g, n, b):
                    for c in range(2):
                        act.wait_ge(l1_mlp1, g * 2 + (c + 1))
                        wait(act, l1_mlp2, g - 1)
                        nc.scalar.activation(hid[b][c][:, :], bank[c][:, :], ACT.Relu).then_inc(l1_relu, 1)
                    act.wait_ge(l1_gathered[b], n * (16 * T) + 16 * T)
                    act.wait_ge(l1_ea4_in[b], n * 16 + 16)
                    wait(act, l1_prod, g - 1)
                    wait(act, l1_outer, g - 1)
                    rows = got[b][0]
                    nc.scalar.copy(v2[b][:, :, :], ea4[b][:, :, 1:4])
                    nc.scalar.copy(zc[b][:, :, 0:U], rows[:, :, 0:U])
                    for j in range(T):
                        s2 = ea4[b][:, j, 0:1]
                        last = nc.scalar.activation(zc[b][:, j, 3 * U:6 * U].rearrange("p (i u) -> p i u", i=VEC),
                                                    rows[:, j, U:D].rearrange("p (u i) -> p i u", i=VEC),
                                                    ACT.Copy, scale=s2)
                    last.then_inc(l1_sz, 1)
                    if not general:
                        wait(act, l1_win, g - 1)
                        wait(act, l1_oh, g)
                        for j in range(T):
                            far = nc.scalar.activation(apart[:, j, :], iota_w[:, :], ACT.Square, scale=-1.0,
                                                       bias=local[:, bass.ds(g, 1), j:j + 1].rearrange("p a o -> p (a o)"))
                        far.then_inc(l1_far, 1)
                        act.wait_ge(l1_far, g + 1)
                        nc.scalar.activation(onehot[b][:, :, :], apart[:, :, :], ACT.Relu, scale=-1.0,
                                             bias=ones[:, 0:1]).then_inc(l1_oh, 1)
                    if general:
                        act.wait_ge(l1_merge, g + 1)
                        wait(act, l1_scattered, (g - 1) * (16 * T))
                        nc.scalar.copy(merged[b][1][:, :, 0:D],
                                       bank[6][:, 0:T * D].rearrange("p (t d) -> p t d", t=T)).then_inc(l1_merged, 1)

                for_all_by_four(act, G, step)

            by_kind(act, lambda: layer1(False), lambda: layer1(True))
            act.wait_ge(edges1_dve, 1)
            merge_all(SUM, m1_staged, m1_turned)

        @block.tensor
        def _(pe):
            pe.wait_ge(c_pool, 9)
            for q, rows in enumerate(ROWQ):
                pe.wait_ge(rows_ready, q + 1)
                wait(pe, rows_kept, 3 * (q - 1))
                for s, table in enumerate([rows_f[q % 2][0][0:rows, :], rows_f[q % 2][1][0:rows, :],
                                           rows_l[q % 2][0:rows, :]]):
                    for j in range(T):
                        mm = nc.tensor.transpose(index_bank[q % 2][s][:, j * P:j * P + rows], table[:, j:GROUP:T],
                                                 ident[0:rows, 0:rows])
                mm.then_inc(rows_turned, 1)
                wait(pe, base_kept, q)
                nc.tensor.transpose(bank[3][0:1, q * P:q * P + rows], rows_f[q % 2][1][0:rows, 0:1],
                                    ident[0:rows, 0:rows]).then_inc(base_turned, 1)
            pe.wait_ge(outside_ready, 1)
            nc.tensor.matmul(bank[4][0:1, 0:1], ones[:, :], outside_sum[:, :], start=True, stop=True)\
              .then_inc(outside_counted, 1)

            pe.wait_ge(w_loads, 16 * W_LOADS)
            pe.wait_ge(rows_kept, 3 * len(ROWQ))

            def turn(m, b):
                pe.wait_ge(staged, m + 1)
                wait(pe, turned_kept, m - 1)
                stand(pe)
                for c in range(BLK):
                    mm = nc.tensor.transpose(turn_bank[b][0:D, c * NP:(c + 1) * NP], stage[b][0:NP, c * D:(c + 1) * D],
                                             ident[0:NP, 0:NP])
                mm.then_inc(turned, 1)

            def project(m, b):
                pe.wait_ge(hid_kept, m + 1)
                wait(pe, out_kept, m - 1)
                for c in range(BLK):
                    mm = nc.tensor.matmul(out_bank[b][0:NP, c * D:(c + 1) * D], hid_n[b][:, c, :], w2s[1][:, :],
                                          start=True, stop=True)
                mm.then_inc(out_mm, 1)

            def perceptron(m, n, b):
                pe.wait_ge(turned_kept, m + 1)
                wait(pe, hid_kept, m - 1)
                nc.tensor.matmul(hid_bank[b][:, 0:BLK * NP], w1s[1][:, :], node_t[b][:, :],
                                 start=True, stop=True).then_inc(hid_mm, 1)
                if not (isinstance(m, int) and m == NBLK - 1):
                    turn(m + 1, 1 - b)
                if not (isinstance(m, int) and m == 0):
                    project(m - 1, 1 - b)

            turn(0, 0)
            for_all(pe, NBLK, perceptron)
            project(NBLK - 1, (NBLK - 1) % 2)

            def spread(parts, rows, to, s_done):
                for j in range(T):
                    for k, part in enumerate(parts):
                        mm = nc.tensor.matmul(to[0:rows, j * P:(j + 1) * P], part[:, j:j + 1].to_broadcast([P, rows]),
                                              identb[:, :], start=(k == 0), stop=(k == len(parts) - 1))
                mm.then_inc(s_done, 1)

            def spread_keys(b, s, to, s_done):
                spread([key_parts[b][s][:, 0, :], key_parts[b][s][:, 1, :]], P, to, s_done)

            def layer0(general):
                ns = 2 if general else 1

                def spread_local(g, b):
                    pe.wait_ge(local_ready, g + 1)
                    wait(pe, oht_ready, g)
                    spread([localb[b]], WINDOW, bank[1], local_spread)

                def spread_all_keys(g, b):
                    wait(pe, same_ready, g * (T * ns))
                    for s in range(ns):
                        pe.wait_ge(key_ready, g * ns + (s + 1))
                        spread_keys(b, s, bank[s], key_spread)

                def step(g, n, b):
                    last = isinstance(g, int) and g == G - 1
                    if not general:
                        pe.wait_ge(oht_ready, g + 1)
                        pe.wait_ge(win_in[b], n * 16 + 16)
                        wait(pe, pay0_ready, g)
                        for j in range(T):
                            mm = nc.tensor.matmul(bank[2][:, j * D:(j + 1) * D], onehot_t[b][:, j, :], win[b][:, :],
                                                  start=True, stop=True)
                        mm.then_inc(dst_rows, 1)
                        if not last:
                            spread_local(g + 1, 1 - b)
                    pe.wait_ge(pay0_ready, g + 1)
                    if general:
                        pe.wait_ge(pay1_ready, g + 1)
                    pe.wait_ge(same_ready, g * (T * ns) + T * ns)
                    wait(pe, merged_ready, g)
                    for s in range(ns):
                        for j in range(T):
                            mm = nc.tensor.matmul(bank[3 + s][:, j * D2:(j + 1) * D2], same[b][s][:, j, :],
                                                  pay[b][s][:, j, :], start=True, stop=True)
                    mm.then_inc(merge_done, 1)
                    if not general:
                        pe.wait_ge(pay1_ready, g + 1)
                        pe.wait_ge(oh_ready, g + 1)
                        wait(pe, sum_added, g)
                        for j in range(T):
                            mm = nc.tensor.matmul(bank[4][0:D2, 0:WINDOW], pay[b][1][:, j, :], onehot[b][:, j, :],
                                                  start=(j == 0), stop=(j == T - 1))
                        mm.then_inc(win_summed, 1)
                    if not last:
                        spread_all_keys(g + 1, 1 - b)
                    pe.wait_ge(parts_ready, g + 1)
                    wait(pe, est_ready, g)
                    stand(pe)
                    turned_parts = bank[5][0:KS, 0:GROUP // 2].bitcast(BF16)
                    for j in range(T):
                        mm = nc.tensor.transpose(turned_parts[:, j * P:(j + 1) * P],
                                                 parts8[b][:, j, :, :].rearrange("p s k -> p (s k)"), identb[:, :])
                    mm.then_inc(parts_turned, 1)

                def late_hidden(m):
                    pe.wait_ge(late_taken, m + 1)
                    wait(pe, late_hid_kept, m)
                    nc.tensor.matmul(late_hid_bank[:, 0:BLK * NP], w1s[0][:, :], node_t[0][:, :],
                                     start=True, stop=True).then_inc(late_hid_mm, 1)

                def late_project(m):
                    pe.wait_ge(late_hid_kept, m + 1)
                    wait(pe, late_out_kept, m)
                    for c in range(BLK):
                        mm = nc.tensor.matmul(late_out_bank[0:NP, c * D:(c + 1) * D], hid_n[0][:, c, :], w2s[0][:, :],
                                              start=True, stop=True)
                    mm.then_inc(late_out_mm, 1)

                if not general:
                    spread_local(0, 0)
                spread_all_keys(0, 0)
                for_all_with(pe, G, step, NBLK, late_hidden, late_project, nothing)

            by_kind(pe, lambda: layer0(False), lambda: layer0(True))

            def merge_all(width, to_rows, s_staged, s_turned, s_added):
                out_width = to_rows.shape[1]

                def merging(m, b):
                    pe.wait_ge(s_staged, m + 1)
                    wait(pe, s_added, m - 1)
                    stand(pe)
                    for c in range(MB):
                        mm = nc.tensor.matmul(bank[6 + b][0:NP, c * out_width:(c + 1) * out_width],
                                              mst[b][0:width, c, :], to_rows, start=True, stop=True)
                    mm.then_inc(s_turned, 1)

                merging(0, 0)
                merging(1, 1)
                with pe.Fori(1, MBLK // 2) as i:
                    merging(i * 2, 0)
                    merging(i * 2 + 1, 1)

            merge_all(D2, ident[0:D2, 0:D2], m_staged, m_turned, m_added)

            def layer1(general):
                def mlp1(g, n, b):
                    pe.wait_ge(l1_est_in[b], n * 16 + 16)
                    for c in range(2):
                        wait(pe, l1_relu, (g - 1) * 2 + (c + 1))
                        nc.tensor.matmul(bank[c][:, :], fc1s[:, c * P:(c + 1) * P], est[b][:, :],
                                         start=True, stop=True).then_inc(l1_mlp1, 1)

                def window(g, b):
                    pe.wait_ge(l1_oh, g + 1)
                    wait(pe, l1_added, g - 1)
                    pe.wait_ge(l1_mess, g + 1)
                    for j in range(T):
                        mm = nc.tensor.matmul(bank[6 + b][0:SUM, 0:WINDOW], terms[b][:, j, :], onehot[b][:, j, :],
                                              start=(j == 0), stop=(j == T - 1))
                    mm.then_inc(l1_win, 1)

                def step(g, n, b):
                    if not (isinstance(g, int) and g == G - 1):
                        mlp1(g + 1, n + b, 1 - b)
                    if not general and not (isinstance(g, int) and g < 2):
                        window(g - 2, b)
                    pe.wait_ge(l1_relu, g * 2 + 2)
                    for h in range(2):
                        wait(pe, l1_prod, g - 1)
                        for t in range(2):
                            for c in range(2):
                                j = 2 * h + t
                                mm = nc.tensor.matmul(pair[1 + b][:, j * WN:(j + 1) * WN],
                                                      hid[b][c][:, j * P:(j + 1) * P], fc2s[:, c, :],
                                                      start=(c == 0), stop=(c == 1))
                    mm.then_inc(l1_mlp2, 1)
                    if general:
                        pe.wait_ge(l1_key, g + 1)
                        wait(pe, l1_same, g * T)
                        spread_keys(b, 1, bank[7], l1_spread)
                        pe.wait_ge(l1_same, g * T + T)
                        pe.wait_ge(l1_mess, g + 1)
                        wait(pe, l1_merged, g)
                        for j in range(T):
                            mm = nc.tensor.matmul(bank[6][:, j * D:(j + 1) * D], same[b][1][:, j, :], mess[b][:, j, :],
                                                  start=True, stop=True)
                        mm.then_inc(l1_merge, 1)

                mlp1(0, 0, 0)
                for_all_by_four(pe, G, step)
                if not general:
                    window(G - 2, (G - 2) % 2)
                    window(G - 1, (G - 1) % 2)

            pe.wait_ge(fc_moved, 16 * SLOTS)
            pe.wait_ge(fc_scaled, 4)
            by_kind(pe, lambda: layer1(False), lambda: layer1(True))
            pe.wait_ge(pick_ready, 2)
            merge_all(SUM, pick[:, :], m1_staged, m1_turned, m1_added)

        @block.vector
        def _(dve):
            made = [0]

            def chain(ins):
                made[0] += 1
                ins.then_inc(chained, 1)
                dve.wait_ge(chained, made[0])

            def prepare_fc():
                dve.wait_ge(w_loads, 16 * W_LOADS)
                chain(nc.vector.tensor_scalar(fc1f[:, :], fc1f[:, :], float(1.0 / np.sqrt(NB)), None, ALU.mult))
                chain(nc.vector.tensor_copy(fc1p[:, 0, :], fc1f[:, :]))
                chain(nc.vector.tensor_tensor(fc1r[:, 0, :], fc1f[:, :], fc1p[:, 0, :], ALU.subtract))
                chain(nc.vector.tensor_copy(fc1p[:, 1, :], fc1r[:, 0, :]))
                chain(nc.vector.tensor_tensor(fc1r[:, 1, :], fc1r[:, 0, :], fc1p[:, 1, :], ALU.subtract))
                nc.vector.tensor_copy(fc1p[:, 2, :], fc1r[:, 1, :]).then_inc(fc_parts, 1)
                for at, blk in enumerate(ORDER):
                    cols = fc2s[:, :, at * U * U:(at + 1) * U * U]
                    nc.vector.tensor_scalar(cols, cols, BLOCK_SCALE[blk], None, ALU.mult).then_inc(fc_scaled, 1)
                dve.wait_ge(c_pool, 9)
                nc.vector.tensor_reduce(pick[:, 0:U], ident[0:SUM, 0:SCALARS * KEPT * U]
                                        .rearrange("p (u w) -> p w u", w=U),
                                        AX, ALU.add).then_inc(pick_ready, 1)
                nc.vector.tensor_reduce(pick[:, U:D].rearrange("p (w i) -> p i w", i=VEC),
                                        ident[0:SUM, SCALARS * KEPT * U:SUM].rearrange("p (i u w) -> p i w u", i=VEC, u=KEPT),
                                        AX, ALU.add).then_inc(pick_ready, 1)

            def localise(q):
                rows = ROWQ[q]
                dve.wait_ge(rows_conv, 2 * q + 2)
                wait(dve, rows_turned, q - 1)
                dest = rows_f[q % 2][1]
                nc.vector.tensor_scalar(rows_l[q % 2][0:rows, :], dest[0:rows, :], dest[0:rows, 0:1], None,
                                        ALU.subtract).then_inc(rows_ready, 1)
                dve.wait_ge(rows_ready, q + 1)
                nc.vector.tensor_reduce(bound[0:rows, 2 * q:2 * q + 1], rows_l[q % 2][0:rows, :], AX, ALU.max)
                chain(nc.vector.tensor_reduce(bound[0:rows, 2 * q + 1:2 * q + 2], rows_l[q % 2][0:rows, :], AX,
                                              ALU.min))

            def norm_relu(v, to, k, beside=(nothing,) * 4):
                def wide(a):
                    return a[0:NP, :].rearrange("p (c a) -> p c a", a=1).to_broadcast([NP, NC, D])

                chain(nc.vector.tensor_reduce(small[0][0:NP, :], v, AX, ALU.add))
                chain(nc.vector.tensor_scalar(small[1][0:NP, :], small[0][0:NP, :], 1.0 / D, None, ALU.mult))
                if k == 0:
                    chain(nc.vector.tensor_tensor(tmp_a[0:NP], v, wide(small[1]), ALU.subtract))
                    beside[0](0)
                    chain(nc.vector.tensor_tensor(tmp_b[0:NP], tmp_a[0:NP], tmp_a[0:NP], ALU.mult))
                    beside[1](1)
                    chain(nc.vector.tensor_reduce(small[0][0:NP, :], tmp_b[0:NP], AX, ALU.add))
                    beside[2](2)
                else:
                    halves = [slice(half * (NC // 2), (half + 1) * (NC // 2)) for half in range(2)]
                    for cols in halves:
                        nc.vector.tensor_tensor(tmp_a[0:NP, cols, :], v[:, cols, :], wide(small[1])[:, cols, :],
                                                ALU.subtract).then_inc(centred, 1)
                    for half, cols in enumerate(halves):
                        dve.wait_ge(squared, 2 * (k - 1) + half + 1)
                        last = nc.vector.tensor_reduce(small[0][0:NP, cols], tmp_b[0:NP, cols, :], AX, ALU.add)
                    chain(last)
                nc.vector.tensor_scalar(small[1][0:NP, :], small[0][0:NP, :], 1.0 / D, EPS, ALU.mult, ALU.add)\
                  .then_inc(variance_ready, 1)
                beside[3](3)
                dve.wait_ge(root_ready, k + 1)
                chain(nc.vector.reciprocal(small[0][0:NP, :], small[2][0:NP, :]))
                return nc.vector.scalar_tensor_tensor(out=to, in0=tmp_a[0:NP], scalar=0.0, in1=wide(small[0]),
                                                      op0=ALU.max, op1=ALU.mult)

            chain(nc.vector.memset(bound[:, :], 0.0))
            dve.wait_ge(in_loads, 16)

            def rows_and_weights(k):
                localise(k)
                if k == 0:
                    prepare_fc()
                if k == 2:
                    for q in range(3, len(ROWQ)):
                        localise(q)

            norm_relu(x_sb[0:NP, :, :], h_sb[0:NP, :, :], 0, (rows_and_weights,) * 3 + (nothing,))\
                .then_inc(h_ready, 1)
            chain(nc.vector.tensor_scalar(outside[:, 0:2 * len(ROWQ):2], bound[:, 0:2 * len(ROWQ):2],
                                          WINDOW - 0.5, None, ALU.is_gt))
            chain(nc.vector.tensor_scalar(outside[:, 1:2 * len(ROWQ):2], bound[:, 1:2 * len(ROWQ):2],
                                          -0.5, None, ALU.is_lt))
            dve.wait_ge(rows_kept, 3 * len(ROWQ))
            nc.vector.memset(local[0:SEEN, G - 1, :], -SHIFT).then_inc(rows_kept, 1)
            for s in range(2):
                nc.vector.tensor_copy(key_all[s][0:SEEN, G - 1, :], trash[0:SEEN, :].to_broadcast([SEEN, T]))\
                  .then_inc(rows_kept, 1)
            nc.vector.tensor_reduce(outside_sum[:, :], outside[:, :], AX, ALU.add).then_inc(outside_ready, 1)
            def keep_turned(m, b):
                dve.wait_ge(turned, m + 1)
                wait(dve, hid_mm, m - 1)
                nc.vector.tensor_copy(all_t[:, bass.ds(m * (BLK * NP), BLK * NP)], turn_bank[b][0:D, 0:BLK * NP])
                nc.vector.tensor_copy(node_t[b][:, :], turn_bank[b][0:D, 0:BLK * NP]).then_inc(turned_kept, 1)

            def keep_block(m, k, psum, to, s_done):
                nc.vector.tensor_tensor(to[0:NP, bass.ds(m * BLK, BLK), :],
                                        psum[0:NP, 0:P].rearrange("p (c d) -> p c d", d=D),
                                        b2s[k][0:NP, :].rearrange("p (a d) -> p a d", a=1)
                                        .to_broadcast([NP, BLK, D]), ALU.add).then_inc(s_done, 1)

            def keep_projected(m, b):
                dve.wait_ge(out_mm, m + 1)
                keep_block(m, 1, out_bank[b], tmp_b, out_kept)

            def perceptron(m, n, b):
                if not (isinstance(m, int) and m == NBLK - 1):
                    keep_turned(m + 1, 1 - b)
                if not (isinstance(m, int) and m == 0):
                    keep_projected(m - 1, 1 - b)

            keep_turned(0, 0)
            for_all(dve, NBLK, perceptron)
            keep_projected(NBLK - 1, (NBLK - 1) % 2)
            dve.wait_ge(outside_counted, 1)
            dve.wait_ge(base_kept, len(ROWQ))
            dve.wait_ge(rows_kept, 3 * len(ROWQ) + 3)
            nc.vector.tensor_copy(flag_i[:, :], bank[4][0:1, 0:1]).then_inc(flag_ready, 1)

            def in_window(b, g, s_done):
                nc.vector.tensor_tensor(onehot[b][:, :, :],
                                        iota_w[:, :].rearrange("p (a w) -> p a w", a=1).to_broadcast([P, T, WINDOW]),
                                        local[:, bass.ds(g, 1), :].rearrange("p a (t o) -> p (a t) o", o=1)
                                        .to_broadcast([P, T, WINDOW]), ALU.is_equal).then_inc(s_done, 1)

            def window_base(g):
                return dve.value_load(base_i[0:1, bass.ds(g, 1)], min_val=0, max_val=N - 1)

            def add_window(base, g, rows, psum, s_done):
                wait(dve, s_done, g)
                span = sum_t[0:rows, bass.ds(base, WINDOW)]
                nc.vector.tensor_tensor(span, span, psum[0:rows, 0:WINDOW], ALU.add).then_inc(s_done, 1)

            def take_keys(b, g, s, n_split, s_split, s_ready):
                keys = key_all[s][:, bass.ds(g, 1), :].rearrange("p a t -> p (a t)")
                nc.vector.tensor_copy(key_parts[b][s][:, 0, :], keys).then_inc(s_split, 1)
                nc.vector.tensor_copy(key[b][s][:, :], keys)
                nc.vector.tensor_scalar(keym[b][s][:, :], keys, trash[:, 0:1], None, ALU.subtract)
                dve.wait_ge(s_split, n_split)
                nc.vector.tensor_tensor(key_parts[b][s][:, 1, :], keys, key_parts[b][s][:, 0, :], ALU.subtract)\
                  .then_inc(s_ready, 1)

            def compare(b, s, spread_keys, s_done):
                for j in range(T):
                    nc.vector.scalar_tensor_tensor(out=same[b][s][:, j, :], in0=spread_keys[:, j * P:(j + 1) * P],
                                                   scalar=key[b][s][:, j:j + 1], in1=later[:, :],
                                                   op0=ALU.is_equal, op1=ALU.mult,
                                                   accum_out=count[b][s][:, j:j + 1]).then_inc(s_done, 1)

            def scatter_rows(b, s, n_same, s_same, n_done, s_f, s_done):
                dve.wait_ge(s_same, n_same)
                nc.vector.scalar_tensor_tensor(out=sidx_f[b][s][:, :], in0=count[b][s][:, :], scalar=1.0,
                                               in1=keym[b][s][:, :], op0=ALU.is_equal, op1=ALU.mult).then_inc(s_f, 1)
                dve.wait_ge(s_f, n_done)
                nc.vector.tensor_scalar(sidx[b][s][:, :], sidx_f[b][s][:, :], trash[:, 0:1], None, ALU.add)\
                  .then_inc(s_done, 1)

            def layer0(general):
                ns = 2 if general else 1

                def take_group(g, b):
                    if not general:
                        wait(dve, local_spread, g - 1)
                        nc.vector.tensor_copy(localb[b][:, :],
                                              local[:, bass.ds(g, 1), :].rearrange("p a t -> p (a t)"))\
                          .then_inc(local_ready, 1)
                    wait(dve, key_spread, (g - 1) * ns)
                    for s in range(ns):
                        take_keys(b, g, s, g * ns + (s + 1), key_split, key_ready)

                def one_hots(g, b):
                    if not (isinstance(g, int) and g < 2):
                        dve.wait_ge(win_summed, g - 1)
                    in_window(b, g, oh_ready)
                    dve.wait_ge(local_spread, g + 1)
                    wait(dve, dst_rows, g - 1)
                    nc.vector.tensor_scalar(onehot_t[b][:, :, :].rearrange("w t e -> w (t e)"), bank[1][0:WINDOW, :],
                                            row[0:WINDOW, 0:1], None, ALU.is_equal).then_inc(oht_ready, 1)

                def step(g, n, b):
                    first, last = (isinstance(g, int) and g == k for k in (0, G - 1))
                    base = None if general or first else window_base(g - 1)
                    dve.wait_ge(part1_done, g + 1)
                    nc.vector.tensor_tensor(rest8[b][:, :, :], ea8[b][:, :, :], parts8[b][:, :, 0, :], ALU.subtract)\
                      .then_inc(rest_done, 1)
                    wait(dve, merge_done, g - 1)
                    for s in range(ns):
                        dve.wait_ge(key_spread, g * ns + (s + 1))
                        compare(b, s, bank[s], same_ready)
                    dve.wait_ge(part2_done, g + 1)
                    nc.vector.tensor_tensor(parts8[b][:, :, 5, :], rest8[b][:, :, :], parts8[b][:, :, 3, :],
                                            ALU.subtract).then_inc(parts_ready, 1)
                    if base is not None:
                        dve.wait_ge(win_summed, g)
                        add_window(base, g - 1, D2, bank[4], sum_added)
                    if not last:
                        take_group(g + 1, 1 - b)
                    for j in range(T):
                        wait(dve, scattered[j], (g - 1) * (16 * ns))
                    for s in range(ns):
                        scatter_rows(b, s, g * (T * ns) + T * (s + 1), same_ready, g * ns + (s + 1), sidxf_done,
                                     sidx_ready)
                    dve.wait_ge(sig_done, g + 1)
                    if general:
                        dve.wait_ge(gathered[b], n * (16 * T * ns) + 16 * T * ns)
                        nc.vector.tensor_tensor(pay[b][0][:, :, D:D2], pay[b][0][:, :, 0:D], got[b][1][:, :, :],
                                                ALU.mult).then_inc(pay0_ready, 1)
                    else:
                        dve.wait_ge(dst_rows, g + 1)
                        nc.vector.tensor_tensor(pay[b][0][:, :, D:D2], pay[b][0][:, :, 0:D],
                                                bank[2][:, 0:T * D].rearrange("p (t d) -> p t d", t=T),
                                                ALU.mult).then_inc(pay0_ready, 1)
                        dve.wait_ge(gathered[b], n * (16 * T) + 16 * T)
                    nc.vector.tensor_tensor(pay[b][1][:, :, D:D2], pay[b][1][:, :, 0:D], got[b][0][:, :, :],
                                            ALU.mult).then_inc(pay1_ready, 1)
                    if not general and not last:
                        one_hots(g + 1, 1 - b)

                def late_take(m):
                    wait(dve, late_hid_mm, m)
                    nc.vector.tensor_copy(node_t[0][:, :], all_t[:, bass.ds(m * (BLK * NP), BLK * NP)])\
                      .then_inc(late_taken, 1)

                def late_keep(m):
                    dve.wait_ge(late_out_mm, m + 1)
                    keep_block(m, 0, late_out_bank, h1_sb, late_out_kept)
                    part = bass.ds(m * BLK, BLK)
                    nc.vector.tensor_tensor(x_sb[0:NP, part, :], x_sb[0:NP, part, :], h_sb[0:NP, part, :], ALU.add)

                take_group(0, 0)
                if not general:
                    one_hots(0, 0)
                for_all_with(dve, G, step, NBLK, late_take, nothing, late_keep)
                if not general:
                    dve.wait_ge(win_summed, G)
                    add_window(window_base(G - 1), G - 1, D2, bank[4], sum_added)
                    dve.wait_ge(sum_added, G)

            by_kind(dve, lambda: layer0(False), lambda: layer0(True))
            nc.vector.memset(count[0][1][0:1, 0:1], 0.0).then_inc(edges0_dve, 1)

            def merging(m, n, b):
                span = bass.ds(m * MB, MB)
                gates, sums, h1 = work[0:NP, span, 0:D], work[0:NP, span, D:D2], h1_sb[0:NP, span, :]
                dve.wait_ge(m_summed, m + 1)
                dve.wait_ge(m_turned, m + 1)
                nc.vector.tensor_tensor(work[0:NP, span, :], work[0:NP, span, :],
                                        bank[6 + b][0:NP, 0:MB * D2].rearrange("p (c d) -> p c d", d=D2),
                                        ALU.add).then_inc(m_added, 1)
                dve.wait_ge(m_added, m + 1)
                nc.vector.tensor_scalar(gates, gates, EPS_DENOM, None, ALU.add).then_inc(m_steps, 1)
                dve.wait_ge(m_steps, m * 3 + 1)
                stand(dve)
                nc.vector.reciprocal(gates, gates).then_inc(m_steps, 1)
                dve.wait_ge(m_steps, m * 3 + 2)
                nc.vector.tensor_tensor(sums, sums, gates, ALU.mult).then_inc(m_steps, 1)
                dve.wait_ge(m_steps, m * 3 + 3)
                nc.vector.tensor_tensor(h1, h1, sums, ALU.add).then_inc(m_done, 1)

            merging(0, 0, 0)
            merging(1, 0, 1)
            with dve.Fori(1, MBLK // 2) as i:
                merging(i * 2, i, 0)
                merging(i * 2 + 1, i, 1)
            dve.wait_ge(m_done, MBLK)
            chain(norm_relu(h1_sb[0:NP, :, :], h1_sb[0:NP, :, :], 1))
            chain(nc.vector.tensor_tensor(x_sb[0:NP, :, :], x_sb[0:NP, :, :], h1_sb[0:NP, :, :], ALU.add))
            norm_relu(x_sb[0:NP, :, :], h_sb[0:NP, :, :], 2).then_inc(h_ready, 1)
            dve.wait_ge(sum_zeroed, 1)

            def layer1(general):
                def vector_products(g, n, b):
                    dve.wait_ge(l1_gathered[b], n * (16 * T) + 16 * T)
                    dve.wait_ge(l1_ea4_in[b], n * 16 + 16)
                    wait(dve, l1_prod, g - 1)
                    nc.vector.tensor_tensor(zc[b][:, :, U:2 * U], got[b][0][:, :, 0:U],
                                            ea4[b][:, :, 0:1].to_broadcast([P, T, U]), ALU.mult)
                    nc.vector.tensor_tensor(vv[:, :, :, :],
                                            got[b][0][:, :, U:D].rearrange("p t (u i) -> p t u i", i=VEC),
                                            ea4[b][:, :, 1:4].rearrange("p t (a i) -> p t a i", a=1)
                                            .to_broadcast([P, T, U, VEC]), ALU.mult).then_inc(l1_vv, 1)

                def dot_products(g, b):
                    dve.wait_ge(l1_vv, g + 1)
                    nc.vector.tensor_reduce(zc[b][:, :, 2 * U:3 * U], vv[:, :, :, :], AX, ALU.add).then_inc(l1_vz, 1)

                def step(g, n, b):
                    last = isinstance(g, int) and g == G - 1
                    if general:
                        wait(dve, l1_spread, g - 1)
                        take_keys(b, g, 1, g + 1, l1_key_split, l1_key)
                    dve.wait_ge(l1_vz, g + 1)
                    wait(dve, l1_terms, g)
                    dve.wait_ge(l1_sz, g + 1)
                    dve.wait_ge(l1_mlp2, g + 1)
                    weights = pair[1 + b][:, :].rearrange("p (t n) -> p t n", t=T)
                    z = zc[b]
                    nc.vector.tensor_tensor(
                        prod[:, :, 0:3, :, :].rearrange("p t k u w -> p t (k u) w"),
                        weights[:, :, 0:3 * U * U].rearrange("p t (m w) -> p t m w", w=U),
                        z[:, :, 0:3 * U].rearrange("p t (m a) -> p t m a", a=1).to_broadcast([P, T, 3 * U, U]),
                        ALU.mult).then_inc(l1_prod_a, 1)
                    if not last:
                        vector_products(g + 1, n + b, 1 - b)
                    nc.vector.tensor_tensor(
                        prod[:, :, 3:6, :, :],
                        weights[:, :, 3 * U * U:4 * U * U].rearrange("p t (a u w) -> p t a u w", a=1, w=U)
                        .to_broadcast([P, T, VEC, U, U]),
                        z[:, :, 3 * U:6 * U].rearrange("p t (i u a) -> p t i u a", i=VEC, a=1)
                        .to_broadcast([P, T, VEC, U, U]), ALU.mult).then_inc(l1_prod, 1)
                    dve.wait_ge(l1_prod_a, g + 1)
                    nc.vector.tensor_reduce(red[:, :, :], prod[:, :, 0, :, :].rearrange("p t u w -> p t w u"),
                                            AX, ALU.add).then_inc(l1_vred, 1)
                    base = None if general or (isinstance(g, int) and g < 2) else window_base(g - 2)
                    if general:
                        if not last:
                            dot_products(g + 1, 1 - b)
                    else:
                        wait(dve, l1_win, g - 1)
                        part = prod[:, :, 1:6, 0:HALF, :]
                        dve.wait_ge(l1_prod, g + 1)
                        nc.vector.tensor_tensor(part, part, prod[:, :, 1:6, HALF:U, :], ALU.add).then_inc(l1_halved, 1)
                    dve.wait_ge(l1_vred, g + 1)
                    nc.vector.tensor_tensor(outer[:, :, :, :],
                                            red[:, :, :].rearrange("p t (w a) -> p t w a", a=1)
                                            .to_broadcast([P, T, U, VEC]),
                                            v2[b][:, :, :].rearrange("p t (a i) -> p t a i", a=1)
                                            .to_broadcast([P, T, U, VEC]), ALU.mult).then_inc(l1_outer, 1)
                    if general:
                        wait(dve, l1_merge, g - 1)
                        dve.wait_ge(l1_prod, g + 1)
                        vectors = mess[b][:, :, U:D].rearrange("p t (w i) -> p t w i", i=VEC)
                        nc.vector.tensor_reduce(mess[b][:, :, 0:U],
                                                prod[:, :, 1:3, :, :].rearrange("p t k u w -> p t w (k u)"),
                                                AX, ALU.add)
                        nc.vector.tensor_reduce(vectors.rearrange("p t w i -> p t i w"),
                                                prod[:, :, 3:6, :, :].rearrange("p t i u w -> p t i w u"),
                                                AX, ALU.add).then_inc(l1_terms, 1)
                    else:
                        kept = terms[b][:, :, :].rearrange("p t (k u w) -> p t k u w", u=KEPT, w=U)
                        vectors = kept[:, :, SCALARS:SCALARS + VEC, 0, :].rearrange("p t i w -> p t w i")
                        if not last:
                            dot_products(g + 1, 1 - b)
                        dve.wait_ge(l1_halved, g + 1)
                        nc.vector.tensor_tensor(kept, prod[:, :, 1:6, 0:KEPT, :], prod[:, :, 1:6, KEPT:HALF, :],
                                                ALU.add).then_inc(l1_terms, 1)
                        if base is not None:
                            dve.wait_ge(l1_win, g - 1)
                            add_window(base, g - 2, SUM, bank[6 + b], l1_added)
                    dve.wait_ge(l1_outer, g + 1)
                    dve.wait_ge(l1_terms, g + 1)
                    nc.vector.tensor_tensor(vectors, vectors, outer[:, :, :, :], ALU.add).then_inc(l1_mess, 1)
                    if general:
                        dve.wait_ge(l1_spread, g + 1)
                        compare(b, 1, bank[7], l1_same)
                        wait(dve, l1_scattered, (g - 1) * (16 * T))
                        scatter_rows(b, 1, g * T + T, l1_same, g + 1, l1_sidxf, l1_sidx)

                vector_products(0, 0, 0)
                dot_products(0, 0)
                for_all_by_four(dve, G, step)
                if not general:
                    for g in (G - 2, G - 1):
                        dve.wait_ge(l1_win, g + 1)
                        add_window(window_base(g), g, SUM, bank[6 + g % 2], l1_added)
                    dve.wait_ge(l1_added, G)

            by_kind(dve, lambda: layer1(False), lambda: layer1(True))
            nc.vector.memset(count[0][1][0:1, 0:1], 0.0).then_inc(edges1_dve, 1)

            def finishing(m, b):
                dve.wait_ge(m1_turned, m + 1)
                to = x_sb[0:NP, bass.ds(m * MB, MB), :]
                nc.vector.tensor_tensor(to, to, bank[6 + b][0:NP, 0:MB * D].rearrange("p (c d) -> p c d", d=D),
                                        ALU.add).then_inc(m1_added, 1)

            finishing(0, 0)
            finishing(1, 1)
            with dve.Fori(1, MBLK // 2) as i:
                finishing(i * 2, 0)
                finishing(i * 2 + 1, 1)
            dve.wait_ge(m1_added, MBLK)
            dve.wait_ge(tab1_read, 16)
            nc.vector.tensor_tensor(x_sb[0:NP, :, :], x_sb[0:NP, :, :], h1_sb[0:NP, :, :], ALU.add)\
              .then_inc(m1_added, 1)


_INS = ['x', 'src', 'dst', 'edge_attr_32', 'edge_attr_4', 'edge_attr_8', 'L0_gnn_W1a', 'L0_gnn_b1a', 'L0_gnn_W2a',
        'L0_gnn_b2a', 'L0_gnn_W1b', 'L0_gnn_b1b', 'L0_gnn_W2b', 'L0_gnn_b2b', 'L1_gnn_fc_w1', 'L1_gnn_fc_w2']


def kernel(**inputs):
    import numpy as _np
    import concourse.bacc as _bacc
    from concourse import mybir as _mybir
    from concourse.bass_utils import run_bass_kernel_spmd as _run

    nc = _bacc.Bacc("TRN2", target_bir_lowering=False, num_devices=1)
    arrays, args = {}, []
    for name in _INS:
        a = _np.ascontiguousarray(inputs[name])
        arrays[f"in_{name}_dram"] = a
        args.append(nc.dram_tensor(f"in_{name}_dram", a.shape, _mybir.dt.from_np(a.dtype), kind="ExternalInput").ap())
    out = nc.dram_tensor("out_0_dram", inputs["x"].shape, _mybir.dt.float32, kind="ExternalOutput").ap()
    gnn_kernel(nc, *args, out)
    r = _run(nc, [arrays], core_ids=[0])
    return r.results[0]["out_0_dram"]
```
